# Optimizing a Trainium2 kernel written in Bass

```python
import numpy as np
import jax
import jax.numpy as jnp

def _softmax(x, axis=-1):
    return jax.nn.softmax(x, axis=axis)

def _gelu(x):
    return jax.nn.gelu(x, approximate=True)

def _silu(x):
    return jax.nn.silu(x)

def _sigmoid(x):
    return jax.nn.sigmoid(x)

def _layernorm(x, axis=-1, eps=1e-05):
    m = jnp.mean(x, axis=axis, keepdims=True)
    v = jnp.var(x, axis=axis, keepdims=True)
    return (x - m) / jnp.sqrt(v + eps)

def _scatter_add(tgt, idx, src, axis=0):
    return tgt.at[idx].add(src)

def _segment_sum(src, seg, n):
    return jax.ops.segment_sum(src, seg, n)
kernel_name = 'mk_xattn_ffn_d2_seqx_r8_3dd213'

def setup_inputs(seed: int=0):
    np.random.seed(seed)
    _w = jnp.asarray

    def _rec_inputs():
        import jax
        import jax.numpy as jnp
        _rk = jax.random.key(seed)
        x = 7.22e-05 + 1 * jax.random.normal(jax.random.fold_in(_rk, 1), (8, 128, 512), jnp.float32)
        _lenS = 128 - jax.random.randint(jax.random.fold_in(_rk, 7), (8,), 0, max(1, 128 // 4) + 1, jnp.int32)
        _lenS2 = 128 - jax.random.randint(jax.random.fold_in(_rk, 8), (8,), 0, max(1, 128 // 4) + 1, jnp.int32)
        _ctx_4096P = jax.random.normal(jax.random.fold_in(_rk, 11), (8, 16, 512), jnp.float32)
        _ctx_4096c = jax.random.dirichlet(jax.random.fold_in(_rk, 511), 0.3 * jnp.ones((16,), jnp.float32), (8, 128))
        _ctx_4096t = jnp.einsum('bsk,bkd->bsd', _ctx_4096c, _ctx_4096P)
        _ctx_4096t = _ctx_4096t * jax.lax.rsqrt(jnp.mean(jnp.square(_ctx_4096t)) + 1e-12) * 0.953939
        ctx_4096 = 4.13588e-05 + 0.999923 * (_ctx_4096t + 0.3 * jax.random.normal(jax.random.fold_in(_rk, 611), (8, 128, 512), jnp.float32))
        _validS = jnp.arange(128)[None, :] < _lenS[:, None]
        _validS2 = jnp.arange(128)[None, :] < _lenS2[:, None]
        _causal = jnp.tril(jnp.ones((128, 128), dtype=bool))
        mask_BxSxS2_bk0 = jnp.logical_not(jnp.broadcast_to(_validS2[:, None, :], (8, 128, 128)))
        return (x, ctx_4096, mask_BxSxS2_bk0)
    x, ctx_4096, mask_BxSxS2_bk0 = _rec_inputs()

    def _L0_xattn_setup():
        import jax, jax.numpy as jnp
        import numpy as np
        B, LQ, LK, D, H, DH = (2, 128, 128, 512, 32, 128)
        EPS = 1e-05

        def _rmsnorm(x, weight):
            var = jnp.mean(jnp.square(x), axis=-1, keepdims=True)
            return x * jax.lax.rsqrt(var + EPS) * weight
        key = jax.random.key(seed)
        ks = jax.random.split(key, 8)
        scale = 0.02
        return {'hidden_states': jax.random.normal(ks[0], (B, LQ, D), jnp.float32), 'key_value_states': jax.random.normal(ks[1], (B, LK, D), jnp.float32), 'attention_mask': jax.random.randint(ks[2], (B, LQ, LK), 0, 2) > 0, 'position_bias': jax.random.normal(ks[3], (H, LQ, LK), jnp.float32), 'ln_weight': jnp.ones((D,), jnp.float32), 'w_q': jax.random.normal(ks[4], (H * DH, D), jnp.float32) * scale, 'w_k': jax.random.normal(ks[5], (H * DH, D), jnp.float32) * scale, 'w_v': jax.random.normal(ks[6], (H * DH, D), jnp.float32) * scale, 'w_out': jax.random.normal(ks[7], (D, H * DH), jnp.float32) * scale}
    _L0_xattn_all = _L0_xattn_setup()
    _L0_xattn_in = {k: v for k, v in _L0_xattn_all.items() if k in ('position_bias', 'ln_weight', 'w_q', 'w_k', 'w_v', 'w_out')}
    del _L0_xattn_all

    def _L0_ffn_setup():
        import jax, jax.numpy as jnp
        import numpy as np
        HIDDEN = 512
        INTER = 1376
        B, S = (2, 256)
        QMAX = 127.0

        def fake_quant(t, axis):
            s = jnp.max(jnp.abs(t), axis=axis, keepdims=True) / QMAX
            s = jnp.maximum(s, 1e-08)
            q = jnp.clip(jnp.round(t / s), -QMAX - 1.0, QMAX) * s
            return t + jax.lax.stop_gradient(q - t)

        def qlinear(x, w):
            xq = fake_quant(x, axis=-1)
            wq = fake_quant(w, axis=1)
            return jnp.einsum('bsh,oh->bso', xq, wq)
        key = jax.random.key(seed)
        k0, k1, k2, k3 = jax.random.split(key, 4)
        x = jax.random.normal(k0, (B, S, HIDDEN), dtype=jnp.float32)
        sc_h = 1.0 / np.sqrt(HIDDEN)
        sc_i = 1.0 / np.sqrt(INTER)
        w_gate = jax.random.normal(k1, (INTER, HIDDEN), dtype=jnp.float32) * sc_h
        w_up = jax.random.normal(k2, (INTER, HIDDEN), dtype=jnp.float32) * sc_h
        w_down = jax.random.normal(k3, (HIDDEN, INTER), dtype=jnp.float32) * sc_i
        return {'x': x, 'w_gate': w_gate, 'w_up': w_up, 'w_down': w_down}
    _L0_ffn_all = _L0_ffn_setup()
    _L0_ffn_in = {k: v for k, v in _L0_ffn_all.items() if k in ('w_gate', 'w_up', 'w_down')}
    del _L0_ffn_all

    def _L1_xattn_setup():
        import jax, jax.numpy as jnp
        import numpy as np
        import math
        EPS = 1e-05
        LAMBDA = 0.6

        def _crucial_k(C):
            f = math.floor(LAMBDA * C)
            return f + f % 2

        def _conv1d(y, w):
            return jax.lax.conv_general_dilated(y, w, window_strides=(1,), padding=((3, 3),), dimension_numbers=('NCH', 'OIH', 'NCH'))

        def _norm_active(z, gamma, beta):
            mu = jnp.mean(z, axis=(0, 2), keepdims=True)
            var = jnp.mean((z - mu) ** 2, axis=(0, 2), keepdims=True)
            zn = (z - mu) * jax.lax.rsqrt(var + EPS)
            zn = zn * gamma.reshape(1, -1, 1) + beta.reshape(1, -1, 1)
            return jax.nn.sigmoid(jax.nn.relu(zn))
        key = jax.random.key(seed)
        k1, k2, k3 = jax.random.split(key, 3)
        B, C, L = (32, 32, 512)
        x = jax.random.normal(k1, (B, C, L), dtype=jnp.float32)
        channel_map = jax.random.normal(k2, (B, C, L), dtype=jnp.float32)
        fan_in = 2 * 7
        bound = 1.0 / math.sqrt(fan_in)
        conv_w = jax.random.uniform(k3, (1, 2, 7), jnp.float32, -bound, bound)
        bn_gamma = jnp.ones((1,), jnp.float32)
        bn_beta = jnp.zeros((1,), jnp.float32)
        return {'x': x, 'channel_map': channel_map, 'conv_w': conv_w, 'bn_gamma': bn_gamma, 'bn_beta': bn_beta}
    _L1_xattn_all = _L1_xattn_setup()
    _L1_xattn_in = {k: v for k, v in _L1_xattn_all.items() if k in ('conv_w', 'bn_gamma', 'bn_beta')}
    del _L1_xattn_all

    def _L1_ffn_setup():
        import jax, jax.numpy as jnp
        import numpy as np
        B_, S, D = (4, 512, 512)
        E, R, O = (8, 16, 512)
        TOP_K = 2
        SCALING = 8.0 / R
        key = jax.random.key(seed)
        ks = jax.random.split(key, 5)
        x = jax.random.normal(ks[0], (B_, S, D), dtype=jnp.float32)
        router_w = jax.random.normal(ks[1], (E, D), dtype=jnp.float32) * (1.0 / np.sqrt(D))
        router_b = jax.random.normal(ks[2], (E,), dtype=jnp.float32) * 0.01
        A = jax.random.normal(ks[3], (E, R, D), dtype=jnp.float32) * (1.0 / np.sqrt(D))
        Bm = jax.random.normal(ks[4], (E, O, R), dtype=jnp.float32) * 0.02
        return {'x': x, 'router_w': router_w, 'router_b': router_b, 'A': A, 'Bm': Bm}
    _L1_ffn_all = _L1_ffn_setup()
    _L1_ffn_in = {k: v for k, v in _L1_ffn_all.items() if k in ('router_w', 'router_b', 'A', 'Bm')}
    del _L1_ffn_all
    return {'x': x, 'ctx_4096': ctx_4096, 'mask_BxSxS2_bk0': mask_BxSxS2_bk0, 'L0_xattn_position_bias': _L0_xattn_in['position_bias'], 'L0_xattn_ln_weight': _L0_xattn_in['ln_weight'], 'L0_xattn_w_q': _L0_xattn_in['w_q'], 'L0_xattn_w_k': _L0_xattn_in['w_k'], 'L0_xattn_w_v': _L0_xattn_in['w_v'], 'L0_xattn_w_out': _L0_xattn_in['w_out'], 'L0_ffn_w_gate': _L0_ffn_in['w_gate'], 'L0_ffn_w_up': _L0_ffn_in['w_up'], 'L0_ffn_w_down': _L0_ffn_in['w_down'], 'L1_xattn_conv_w': _L1_xattn_in['conv_w'], 'L1_xattn_bn_gamma': _L1_xattn_in['bn_gamma'], 'L1_xattn_bn_beta': _L1_xattn_in['bn_beta'], 'L1_ffn_router_w': _L1_ffn_in['router_w'], 'L1_ffn_router_b': _L1_ffn_in['router_b'], 'L1_ffn_A': _L1_ffn_in['A'], 'L1_ffn_Bm': _L1_ffn_in['Bm']}

def reference(x, ctx_4096, mask_BxSxS2_bk0, L0_xattn_position_bias, L0_xattn_ln_weight, L0_xattn_w_q, L0_xattn_w_k, L0_xattn_w_v, L0_xattn_w_out, L0_ffn_w_gate, L0_ffn_w_up, L0_ffn_w_down, L1_xattn_conv_w, L1_xattn_bn_gamma, L1_xattn_bn_beta, L1_ffn_router_w, L1_ffn_router_b, L1_ffn_A, L1_ffn_Bm):
    import jax
    import jax.numpy as jnp

    def _L0_xattn_ref(hidden_states, key_value_states, attention_mask, position_bias, ln_weight, w_q, w_k, w_v, w_out):
        import jax, jax.numpy as jnp
        import numpy as np
        B, LQ, LK, D, H, DH = (2, 128, 128, 512, 32, 128)
        EPS = 1e-05

        def _rmsnorm(x, weight):
            var = jnp.mean(jnp.square(x), axis=-1, keepdims=True)
            return x * jax.lax.rsqrt(var + EPS) * weight
        x = _rmsnorm(hidden_states, ln_weight)
        b, lq, _ = x.shape
        lk = key_value_states.shape[1]
        h_q = (x @ w_q.T).reshape(b, lq, H, DH)
        h_k = (key_value_states @ w_k.T).reshape(b, lk, H, DH)
        h_v = (key_value_states @ w_v.T).reshape(b, lk, H, DH)
        score = jnp.einsum('bqhd,bkhd->bhqk', h_q, h_k)
        score = score + position_bias[None]
        m = attention_mask[:, None]
        score = jnp.where(m, score, -jnp.inf)
        score = jax.nn.softmax(score, axis=-1)
        score = jnp.where(m, score, 0.0)
        attn = jnp.einsum('bhqk,bkhd->bqhd', score, h_v).reshape(b, lq, H * DH)
        out = attn @ w_out.T
        return hidden_states + out

    def _L0_ffn_ref(x, w_gate, w_up, w_down):
        import jax, jax.numpy as jnp
        import numpy as np
        HIDDEN = 512
        INTER = 1376
        B, S = (2, 256)
        QMAX = 127.0

        def fake_quant(t, axis):
            s = jnp.max(jnp.abs(t), axis=axis, keepdims=True) / QMAX
            s = jnp.maximum(s, 1e-08)
            q = jnp.clip(jnp.round(t / s), -QMAX - 1.0, QMAX) * s
            return t + jax.lax.stop_gradient(q - t)

        def qlinear(x, w):
            xq = fake_quant(x, axis=-1)
            wq = fake_quant(w, axis=1)
            return jnp.einsum('bsh,oh->bso', xq, wq)
        gate = qlinear(x, w_gate)
        up = qlinear(x, w_up)
        h = jax.nn.silu(gate) * up
        return qlinear(h, w_down)

    def _L1_xattn_ref(x, channel_map, conv_w, bn_gamma, bn_beta):
        import jax, jax.numpy as jnp
        import numpy as np
        import math
        EPS = 1e-05
        LAMBDA = 0.6

        def _crucial_k(C):
            f = math.floor(LAMBDA * C)
            return f + f % 2

        def _conv1d(y, w):
            return jax.lax.conv_general_dilated(y, w, window_strides=(1,), padding=((3, 3),), dimension_numbers=('NCH', 'OIH', 'NCH'))

        def _norm_active(z, gamma, beta):
            mu = jnp.mean(z, axis=(0, 2), keepdims=True)
            var = jnp.mean((z - mu) ** 2, axis=(0, 2), keepdims=True)
            zn = (z - mu) * jax.lax.rsqrt(var + EPS)
            zn = zn * gamma.reshape(1, -1, 1) + beta.reshape(1, -1, 1)
            return jax.nn.sigmoid(jax.nn.relu(zn))
        B, C, L = x.shape
        k = _crucial_k(C)
        cm = jnp.moveaxis(channel_map, 1, 2)
        _, topk_idx = jax.lax.top_k(cm, k)
        b_idx = jnp.arange(B)[:, None, None]
        l_idx = jnp.arange(L)[None, :, None]
        mask = jnp.zeros((B, L, C), x.dtype).at[b_idx, l_idx, topk_idx].set(1.0)
        crucial_channels = jnp.moveaxis(mask, 2, 1)
        subcrucial_channels = 1.0 - crucial_channels
        crucial_features = crucial_channels * x
        subcrucial_features = subcrucial_channels * x
        c_max = jnp.max(crucial_features, axis=1, keepdims=True)
        c_avg = jnp.mean(crucial_features, axis=1, keepdims=True) * (C / k)
        s_max = jnp.max(subcrucial_features, axis=1, keepdims=True)
        s_avg = jnp.mean(subcrucial_features, axis=1, keepdims=True) * (C / (C - k))
        crucial_x = jnp.concatenate([c_max, c_avg], axis=1)
        subcrucial_x = jnp.concatenate([s_max, s_avg], axis=1)
        A_S1 = _norm_active(_conv1d(crucial_x, conv_w), bn_gamma, bn_beta)
        A_S2 = _norm_active(_conv1d(subcrucial_x, conv_w), bn_gamma, bn_beta)
        return crucial_features * A_S1 + subcrucial_features * A_S2

    def _L1_ffn_ref(x, router_w, router_b, A, Bm):
        import jax, jax.numpy as jnp
        import numpy as np
        B_, S, D = (4, 512, 512)
        E, R, O = (8, 16, 512)
        TOP_K = 2
        SCALING = 8.0 / R
        flat = x.reshape(-1, x.shape[-1])
        N = flat.shape[0]
        logits = flat @ router_w.T + router_b
        probs = jax.nn.softmax(logits, axis=-1)
        topv, topi = jax.lax.top_k(probs, TOP_K)
        gates = topv / jnp.sum(topv, axis=-1, keepdims=True)
        w = jnp.zeros((N, E), dtype=flat.dtype).at[jnp.arange(N)[:, None], topi].add(gates)
        h = jnp.einsum('nd,erd->ner', flat, A)
        hw = h * w[:, :, None]
        out = jnp.einsum('ner,eor->no', hw, Bm) * SCALING
        return out.reshape(*x.shape[:-1], O)
    x = x + _L0_xattn_ref(_layernorm(x, axis=-1), ctx_4096, mask_BxSxS2_bk0, L0_xattn_position_bias, L0_xattn_ln_weight, L0_xattn_w_q, L0_xattn_w_k, L0_xattn_w_v, L0_xattn_w_out)
    x = x + _L0_ffn_ref(_layernorm(x, axis=-1), L0_ffn_w_gate, L0_ffn_w_up, L0_ffn_w_down)
    x = x + _L1_xattn_ref(_layernorm(x, axis=-1), ctx_4096, L1_xattn_conv_w, L1_xattn_bn_gamma, L1_xattn_bn_beta)
    x = x + _L1_ffn_ref(_layernorm(x, axis=-1), L1_ffn_router_w, L1_ffn_router_b, L1_ffn_A, L1_ffn_Bm)
    return x

_drawn_inputs = setup_inputs


def setup_inputs(seed=0):
    import zlib

    import numpy as np

    out = dict(_drawn_inputs(seed))
    spreads = {'L0_xattn_ln_weight': (1.0, 0.2)}
    factors = {'L1_ffn_router_w': 6.024, 'L1_ffn_router_b': 31.634, 'L1_ffn_A': 5.252, 'L1_ffn_Bm': 5.296}
    for name, (base, spread) in spreads.items():
        noise = np.random.default_rng([zlib.crc32(name.encode()), seed]).standard_normal(out[name].shape)
        drawn = base * np.exp(spread * noise) if base else spread * noise
        out[name] = jnp.asarray(drawn.astype(out[name].dtype))
    for name, factor in factors.items():
        out[name] = (out[name] * factor).astype(out[name].dtype)
    return out
```

```python
from contextlib import ExitStack

import numpy as np

import concourse.bass as bass
from concourse import mybir

F32 = mybir.dt.float32
F32R = mybir.dt.float32r
BF16 = mybir.dt.bfloat16
U8 = mybir.dt.uint8
ALU = mybir.AluOpType
ACT = mybir.ActivationFunctionType
AX = mybir.AxisListType

P = 128
B = 8
S = 128
D = 512
KT = D // P
H = 32
DH = 128
HB = B // 2
NH = HB * S
STEPS = 2 * H
INTER = 1376
IT = -(-INTER // P)
LAST = INTER - (IT - 1) * P
E = 8
R = 16
ER = E * R
EPS = 1e-5
MAGIC = 12582912.0
QMAX = 127.0
LOWEST = -3.4028234663852886e38
MASKED = -1e30
TAPS = 7
CRUCIAL = int(0.6 * S) + int(0.6 * S) % 2
REST = S - CRUCIAL


def layers_kernel(nc, x, cT, mask, bias, ln_w, wq, wk, wv, wo, w_gate, w_up, w_down,
                  conv_w, gamma, beta, router_w, router_b, lora_a, lora_b, out):
    ctx = ExitStack()

    def sbuf(name, shape, dt=F32, stack=ctx):
        return stack.enter_context(nc.sbuf_tensor(name, shape, dt))

    def psum(name, shape, dt=F32, stack=ctx):
        return stack.enter_context(nc.psum_tensor(name, shape, dt))

    def sem(name):
        return ctx.enter_context(nc.semaphore(name))

    with ctx:
        xr = sbuf("xr", [P, B, D])
        top_flat = sbuf("top", [P, KT * B * S], BF16)
        top = top_flat[:].rearrange("p (k b s) -> p k b s", k=KT, b=B)
        ident = sbuf("ident", [P, P])
        ident_b = sbuf("ident_b", [P, P], BF16)
        ident_r = sbuf("ident_r", [P, P], F32R)
        ones = sbuf("ones", [P, P])
        neg_half = sbuf("neg_half", [P, B])

        att = ExitStack()
        xT_hi = sbuf("xT_hi", [P, KT, B * S], F32R, att)
        xT_lo = sbuf("xT_lo", [P, KT, B * S], F32R, att)
        cT_hi = sbuf("cT_hi", [P, KT, B * S], F32R, att)
        cT_lo = sbuf("cT_lo", [P, KT, B * S], F32R, att)
        cT_raw = sbuf("cT_raw", [P, KT * B * S], F32, att)
        w_raw = {c: sbuf(f"raw_{c}", [P, D], F32, att) for c in "qkvo"}
        w_hi = {c: sbuf(f"w{c}_hi", [P, D], F32R, att) for c in "qkvo"}
        w_lo = {c: sbuf(f"w{c}_lo", [P, D], F32R, att) for c in "qkvo"}
        b_raw = sbuf("b_raw", [P, S], F32, att)
        b_hi = sbuf("b_hi", [P, 1, S], F32R, att)
        b_lo = sbuf("b_lo", [P, 1, S], F32R, att)
        q_hi = sbuf("q_hi", [P, NH], F32R, att)
        q_lo = sbuf("q_lo", [P, NH], F32R, att)
        k_hi = sbuf("k_hi", [P, NH], F32R, att)
        k_lo = sbuf("k_lo", [P, NH], F32R, att)
        vT = sbuf("vT", [P, NH], F32, att)
        v_hi = sbuf("v_hi", [P, NH], F32R, att)
        v_lo = sbuf("v_lo", [P, NH], F32R, att)
        prob = sbuf("prob", [P, HB, S], F32, att)
        pT_hi = sbuf("pT_hi", [P, NH], F32R, att)
        pT_lo = sbuf("pT_lo", [P, NH], F32R, att)
        aT_hi = sbuf("aT_hi", [P, NH], F32R, att)
        aT_lo = sbuf("aT_lo", [P, NH], F32R, att)
        mask_u8 = sbuf("mask_u8", [P, B, S], U8, att)
        mask_add = sbuf("mask_add", [P, B, S], BF16, att)
        row_any = sbuf("row_any", [P, B], F32, att)
        neg_max = sbuf("neg_max", [P, HB], F32, att)
        row_sum = sbuf("row_sum", [P, HB], F32, att)
        row_inv = sbuf("row_inv", [P, HB, 1], F32, att)
        hid = sbuf("hid", [P, HB, D], F32, att)
        sq_junk = sbuf("sq_junk", [P, D], F32, att)
        stats = sbuf("stats", [P, HB, 6], F32, att)
        mv = sbuf("mv", [P, HB, 2], F32, att)
        ve = sbuf("ve", [P, HB], F32, att)
        rs = sbuf("rs", [P, HB], F32, att)
        ssq = sbuf("ssq", [P, HB], F32, att)
        lnw_col = sbuf("lnw_col", [P, KT, 1], F32, att)
        pick = sbuf("pick", [P, S], F32, att)
        pick8 = sbuf("pick8", [P, 8], F32, att)
        oacc = [psum(f"oacc{b}", [P, D], F32, att) for b in range(HB)]
        pX0 = psum("pX0", [P, NH], F32, att)
        pX1 = psum("pX1", [P, NH], F32, att)
        pS = psum("pS", [P, NH], F32, att)
        pT = psum("pT", [P, NH], F32, att)
        att.close()

        post = ExitStack()
        wgT = sbuf("wgT", [P, KT, INTER], BF16, post)
        wuT = sbuf("wuT", [P, KT, INTER], BF16, post)
        wdT = sbuf("wdT", [P, IT, D], BF16, post)
        sg_row = sbuf("sg_row", [P, INTER], F32, post)
        su_row = sbuf("su_row", [P, INTER], F32, post)
        sd_row = sbuf("sd_row", [P, D], F32, post)
        f_raw = sbuf("f_raw", [P, INTER], F32, post)
        f_mag = sbuf("f_mag", [P, INTER], F32, post)
        f_q = sbuf("f_q", [P, INTER], BF16, post)
        f_diag = sbuf("f_diag", [P, P], F32, post)
        f_s = sbuf("f_s", [P, 4], F32, post)
        y = sbuf("y", [P, D], F32, post)
        y_mag = sbuf("y_mag", [P, D], F32, post)
        y_q = sbuf("y_q", [P, D], BF16, post)
        y_qT = sbuf("y_qT", [P, KT * S], BF16, post)
        y_s = sbuf("y_s", [P, 4], F32, post)
        gate = sbuf("gate", [P, INTER], F32, post)
        up = sbuf("up", [P, INTER], F32, post)
        th = sbuf("th", [P, INTER], F32, post)
        h_q = sbuf("h_q", [P, INTER], BF16, post)
        h_qT = sbuf("h_qT", [P, IT * S], BF16, post)
        h_s = sbuf("h_s", [P, 4], F32, post)
        z = sbuf("z", [P, B, D], F32, post)
        z_t = sbuf("z_t", [P, D], F32, post)
        cf = sbuf("cf", [P, KT, S], F32, post)
        sf = sbuf("sf", [P, KT, S], F32, post)
        st6 = sbuf("st6", [P, 6], F32, post)
        mv1 = sbuf("mv1", [P, 2], F32, post)
        ve1 = sbuf("ve1", [P, 2], F32, post)
        rs1 = sbuf("rs1", [P, 2], F32, post)
        stat = [sbuf(f"stat{c}", [P, KT, 2, B], F32, post) for c in range(2)]
        taps = sbuf("taps", [P, 2 * TAPS], F32, post)
        diag = sbuf("diag", [P, 3 * P + TAPS - 1], F32, post)
        band = [sbuf(f"band{c}", [P, 3 * P], F32, post) for c in range(2)]
        cz = sbuf("cz", [P, KT, 2, B], F32, post)
        cz2 = sbuf("cz2", [P, KT, 2, B], F32, post)
        csum = sbuf("csum", [P, 2], F32, post)
        cmu = sbuf("cmu", [P, 2], F32, post)
        gb = sbuf("gb", [P, 2], F32, post)
        dA = sbuf("dA", [P, KT, B], F32, post)
        coef = sbuf("coef", [P, KT, S], F32, post)
        x3 = sbuf("x3", [P, D], F32, post)
        f = sbuf("f", [P, D], F32, post)
        fT = sbuf("fT", [P, KT * S], F32, post)
        ra = sbuf("ra", [P, KT, E + ER], F32, post)
        rb = sbuf("rb", [P, E], F32, post)
        lb = sbuf("lb", [P, D], F32, post)
        logit = sbuf("logit", [P, E], F32, post)
        rsm = sbuf("rsm", [P, 4], F32, post)
        prb = sbuf("prb", [P, 2 * E], F32, post)
        prw = sbuf("prw", [P, 2 * E], F32, post)
        best = sbuf("best", [P, 8], F32, post)
        wexp = sbuf("wexp", [P, E, 1], F32, post)
        hw = sbuf("hw", [P, E, R], F32, post)
        hwT = sbuf("hwT", [P, S], F32, post)
        x4 = sbuf("x4", [P, D], F32, post)
        pG = psum("pG", [P, 3 * 512], F32, post)
        pU = psum("pU", [P, 3 * 512], F32, post)
        pTb = psum("pTb", [P, 2 * 1024], BF16, post)
        post.close()

        s_a_done = sem("a_done")
        s_a_hi = sem("a_hi")
        s_a_lo = sem("a_lo")
        s_b_hi = sem("b_hi")
        s_b_lo = sem("b_lo")
        s_band = sem("band")
        s_cT_hi = sem("cT_hi")
        s_cT_lo = sem("cT_lo")
        s_c_in = sem("c_in")
        s_c_trans = sem("c_trans")
        s_coef = sem("coef")
        s_const_in = sem("const_in")
        s_conv = sem("conv")
        s_csum = sem("csum")
        s_ctotal = sem("ctotal")
        s_dA = sem("dA")
        s_d_proj = sem("d_proj")
        s_diag = sem("diag")
        s_exp_done = sem("exp_done")
        s_f = sem("f")
        s_fT = sem("fT")
        s_f_diag = sem("f_diag")
        s_f_in = sem("f_in")
        s_f_mag = sem("f_mag")
        s_f_out = sem("f_out")
        s_f_q = sem("f_q")
        s_f_row = sem("f_row")
        s_f_t = sem("f_t")
        s_f_trans = sem("f_trans")
        s_g_proj = sem("g_proj")
        s_gate = sem("gate")
        s_h_done = sem("h_done")
        s_h_mag = sem("h_mag")
        s_h_q = sem("h_q")
        s_h_qT = sem("h_qT")
        s_h_trans = sem("h_trans")
        s_hw = sem("hw")
        s_hwT = sem("hwT")
        s_hw_t = sem("hw_t")
        s_ident = sem("ident")
        s_k_hi = sem("k_hi")
        s_k_lo = sem("k_lo")
        s_k_proj = sem("k_proj")
        s_l_proj = sem("l_proj")
        s_lnw_in = sem("lnw_in")
        s_mask_add = sem("mask_add")
        s_mask_in = sem("mask_in")
        s_max_done = sem("max_done")
        s_neg_half = sem("neg_half")
        s_norm_done = sem("norm_done")
        s_o_done = sem("o_done")
        s_ones = sem("ones")
        s_out = sem("out")
        s_p_hi = sem("p_hi")
        s_p_lo = sem("p_lo")
        s_p_trans = sem("p_trans")
        s_q_hi = sem("q_hi")
        s_q_lo = sem("q_lo")
        s_q_proj = sem("q_proj")
        s_r_exp = sem("r_exp")
        s_r_proj = sem("r_proj")
        s_rstd = sem("rstd")
        s_s_done = sem("s_done")
        s_sig = sem("sig")
        s_ssq = sem("ssq")
        s_stats = sem("stats")
        s_th = sem("th")
        s_top_logit = sem("top_logit")
        s_u_proj = sem("u_proj")
        s_vT = sem("vT")
        s_v_hi = sem("v_hi")
        s_v_lo = sem("v_lo")
        s_v_proj = sem("v_proj")
        s_v_trans = sem("v_trans")
        s_var_in = sem("var_in")
        s_x1_done = sem("x1_done")
        s_x4_done = sem("x4_done")
        s_xT_hi = sem("xT_hi")
        s_xT_lo = sem("xT_lo")
        s_x_in = sem("x_in")
        s_x_trans = sem("x_trans")
        s_xn = sem("xn")
        s_xw = sem("xw")
        s_y_mag = sem("y_mag")
        s_y_q = sem("y_q")
        s_y_qT = sem("y_qT")
        s_y_trans = sem("y_trans")
        s_z = sem("z")
        s_z_t = sem("z_t")
        s_z_trans = sem("z_trans")
        s_z_used = sem("z_used")
        s_zn = sem("zn")
        s_raw = {c: sem(f"raw_{c}") for c in "qkvob"}
        s_w_hi = {c: sem(f"w{c}_hi") for c in "qkvo"}
        s_w_lo = {c: sem(f"w{c}_lo") for c in "qkvo"}

        block = ctx.enter_context(nc.Block())
        F_TILES = [(c, t) for c, n in (("g", IT), ("u", IT), ("d", KT)) for t in range(n)]

        def at(t):
            return slice(t, t + 1) if isinstance(t, int) else bass.ds(t, 1)

        def later(n):
            return not isinstance(n, int) or n > 0

        @block.sync
        def _(sp):
            def load(c, n, head):
                if later(n):
                    sp.wait_ge(s_w_lo[c], n)
                src = {"q": wq, "k": wk, "v": wv, "o": wo}[c]
                sp.dma_start(w_raw[c][:], src[head]).then_inc(s_raw[c], 16)

            def load_bias(n, head):
                if later(n):
                    sp.wait_ge(s_b_lo, n)
                sp.dma_start(b_raw[:], bias[head]).then_inc(s_raw["b"], 16)

            sp.dma_start(lnw_col[:, :, 0], ln_w).then_inc(s_lnw_in, 16)
            for b in range(HB):
                sp.dma_start(xr[:, b, :], x[b]).then_inc(s_x_in, 16)
            for c in "qk":
                load(c, 0, 0)
            for kt in range(KT):
                sp.dma_start(cT_raw[:, kt * B * S:(kt + 1) * B * S], cT[kt]).then_inc(s_c_in, 16)
            for b in range(HB, B):
                sp.dma_start(xr[:, b, :], x[b]).then_inc(s_x_in, 16)
            sp.dma_start(mask_u8[:], mask).then_inc(s_mask_in, 16)
            load_bias(0, 0)
            load("v", 0, 0)
            load("o", 0, 0)
            for c in "qk":
                load(c, 1, 1)

            def loads(n, head1, head2):
                load_bias(n + 1, head1)
                load("q", n + 2, head2)
                load("k", n + 2, head2)
                load("v", n + 1, head1)
                load("o", n + 1, head1)

            with sp.Fori(0, H - 2) as n:
                loads(n, n + 1, n + 2)
            loads(H - 2, H - 1, 0)
            loads(H - 1, 0, 1)
            with sp.Fori(H, 2 * H - 2) as n:
                loads(n, n - H + 1, n - H + 2)
            load_bias(STEPS - 1, H - 1)
            load("v", STEPS - 1, H - 1)
            load("o", STEPS - 1, H - 1)

            sp.wait_ge(s_x1_done, 2)
            sp.dma_start(taps[:], conv_w).then_inc(s_const_in, 16)
            sp.dma_start(gb[:, 0:1], gamma).then_inc(s_const_in, 16)
            sp.dma_start(gb[:, 1:2], beta).then_inc(s_const_in, 16)
            sp.dma_start(rb[:], router_b).then_inc(s_const_in, 16)
            sp.dma_start(ra[:, :, 0:E], router_w).then_inc(s_const_in, 16)
            sp.dma_start(ra[:, :, E:E + ER], lora_a).then_inc(s_const_in, 16)
            sp.dma_start(lb[:], lora_b).then_inc(s_const_in, 16)
            for i, (c, t) in enumerate(F_TILES):
                src = {"g": w_gate, "u": w_up, "d": w_down}[c]
                rows, cols = min(P, src.shape[0] - t * P), src.shape[1]
                if later(i):
                    sp.wait_ge(s_f_mag, i)
                sp.dma_start(f_raw[0:rows, 0:cols], src[t * P:t * P + rows, :]).then_inc(s_f_in, 16)

            with sp.Fori(0, B) as t:
                sp.wait_ge(s_x4_done, t + 1)
                sp.dma_start(out[t], x4[:]).then_inc(s_out, 16)
            sp.wait_ge(s_out, 16 * B)

        @block.gpsimd
        def _(pool):
            g = nc.gpsimd
            g.memset(ones[:], 1.0).then_inc(s_ones, 1)
            g.memset(neg_half[:], -0.5).then_inc(s_neg_half, 1)
            pool.wait_ge(s_ones, 1)
            g.affine_select(out=ident[:], in_=ones[:], compare_op=ALU.is_equal, fill=0.0, base=0,
                            pattern=[[-1, P]], channel_multiplier=1).then_inc(s_ident, 1)
            pool.wait_ge(s_ident, 1)
            g.tensor_copy(ident_b[:], ident[:]).then_inc(s_ident, 1)
            g.tensor_copy(ident_r[:], ident[:]).then_inc(s_ident, 1)
            pool.wait_ge(s_neg_half, 1)

            def rsqrt(dst, src, n):
                pool.wait_ge(s_var_in, n + 1)
                g.tensor_tensor(dst, src, neg_half[:, 0:src.shape[-1]], ALU.pow).then_inc(s_rstd, 1)

            def lo(c, n):
                pool.wait_ge(s_w_hi[c], n + 1)
                g.tensor_tensor(w_lo[c][:], w_raw[c][:], w_hi[c][:].bitcast(F32),
                                ALU.subtract).then_inc(s_w_lo[c], 1)

            def bias_parts(n):
                pool.wait_ge(s_b_hi, n + 1)
                g.tensor_tensor(b_lo[:, 0, :], b_raw[:], b_hi[:, 0, :].bitcast(F32),
                                ALU.subtract).then_inc(s_b_lo, 1)

            lo("q", 0)
            lo("k", 0)
            rsqrt(rs[:], ve[:], 0)
            rsqrt(rs[:], ve[:], 1)
            for i in range(2 * KT):
                pool.wait_ge(s_cT_hi, i + 1)
                part = slice(i % 2 * NH, (i % 2 + 1) * NH)
                g.tensor_tensor(cT_lo[:, i // 2, part], cT_raw[:, i * NH:(i + 1) * NH],
                                cT_hi[:, i // 2, part].bitcast(F32), ALU.subtract).then_inc(s_cT_lo, 1)
            rsqrt(rs[:], ve[:], 2)
            rsqrt(rs[:], ve[:], 3)
            bias_parts(0)
            lo("v", 0)
            lo("q", 1)
            lo("k", 1)

            def step(n, qk=True, v=True):
                if v:
                    bias_parts(n + 1)
                if qk:
                    lo("q", n + 2)
                    lo("k", n + 2)
                if v:
                    lo("v", n + 1)
                lo("o", n)

            with pool.Fori(0, STEPS - 2) as n:
                step(n)
            step(STEPS - 2, qk=False)
            step(STEPS - 1, qk=False, v=False)

            pool.wait_ge(s_x1_done, 2)
            g.memset(diag[:], 1.0).then_inc(s_diag, 1)
            pool.wait_ge(s_diag, 1)
            g.affine_select(out=diag[:], in_=diag[:], compare_op=ALU.is_equal, fill=0.0, base=P + TAPS // 2,
                            pattern=[[-1, 3 * P + TAPS - 1]], channel_multiplier=1).then_inc(s_diag, 1)

            with pool.Fori(0, B) as t:
                rsqrt(rs1[:, 0:1], ve1[:, 0:1], 2 * t + 4)
                rsqrt(rs1[:, 0:1], ve1[:, 0:1], 2 * t + 5)
            rsqrt(rs1[:], ve1[:], 2 * B + 4)
            with pool.Fori(0, B) as t:
                rsqrt(rs1[:, 0:1], ve1[:, 0:1], t + 2 * B + 5)

        @block.scalar
        def _(act):
            a = nc.scalar

            def copy(dst, src):
                return a.activation(dst, src, ACT.Copy)

            def hi(c, n, used):
                act.wait_ge(s_raw[c], 16 * (n + 1))
                if later(n):
                    act.wait_ge(used, n)
                copy(w_hi[c][:], w_raw[c][:]).then_inc(s_w_hi[c], 1)

            def squares(half):
                for b in range(HB):
                    act.wait_ge(s_h_done, half * HB + b + 1)
                    act.drain()
                    a.activation(sq_junk[:], hid[:, b, :], ACT.Square,
                                 accum_out=ssq[:, b:b + 1]).then_inc(s_ssq, 1)

            def x_high(half):
                for b in range(HB):
                    t = half * HB + b
                    act.wait_ge(s_xw, t + 1)
                    copy(xT_hi[:, :, t * S:(t + 1) * S],
                         hid[:, b, :].rearrange("p (k s) -> p k s", k=KT)).then_inc(s_xT_hi, 1)

            hi("q", 0, s_q_proj)
            hi("k", 0, s_k_proj)
            squares(0)
            for i in range(2 * KT):
                act.wait_ge(s_c_in, 16 * KT)
                copy(cT_hi[:, i // 2, i % 2 * NH:(i % 2 + 1) * NH],
                     cT_raw[:, i * NH:(i + 1) * NH]).then_inc(s_cT_hi, 1)
            x_high(0)
            squares(1)
            x_high(1)

            def query_high(n):
                act.wait_ge(s_q_proj, n + 1)
                copy(q_hi[:], pX0[:]).then_inc(s_q_hi, 1)

            def key_high(n):
                act.wait_ge(s_k_proj, n + 1)
                copy(k_hi[:], pX1[:]).then_inc(s_k_hi, 1)

            def bias_high(n):
                act.wait_ge(s_raw["b"], 16 * (n + 1))
                if later(n):
                    act.wait_ge(s_s_done, n)
                copy(b_hi[:, 0, :], b_raw[:]).then_inc(s_b_hi, 1)

            query_high(0)
            hi("q", 1, s_q_proj)
            key_high(0)
            hi("k", 1, s_k_proj)
            bias_high(0)
            hi("v", 0, s_v_proj)

            def step(n, qk2=True, more=True):
                act.wait_ge(s_max_done, n + 1)
                if later(n):
                    act.wait_ge(s_p_trans, n)
                for b in range(HB):
                    e = a.activation(prob[:, b, :], pS[:, b * S:(b + 1) * S], ACT.Exp,
                                     bias=neg_max[:, b:b + 1], accum_out=row_sum[:, b:b + 1])
                e.then_inc(s_exp_done, 1)
                if more:
                    bias_high(n + 1)
                    query_high(n + 1)
                    if qk2:
                        hi("q", n + 2, s_q_proj)
                    key_high(n + 1)
                    if qk2:
                        hi("k", n + 2, s_k_proj)
                act.wait_ge(s_v_proj, n + 1)
                if later(n):
                    act.wait_ge(s_v_trans, n)
                copy(vT[:], pX0[:]).then_inc(s_vT, 1)
                act.wait_ge(s_p_trans, n + 1)
                copy(pT_hi[:], pS[:]).then_inc(s_p_hi, 1)
                act.wait_ge(s_v_trans, n + 1)
                copy(v_hi[:], pT[:]).then_inc(s_v_hi, 1)
                if more:
                    hi("v", n + 1, s_v_proj)
                hi("o", n, s_o_done)
                act.wait_ge(s_a_done, n + 1)
                copy(aT_hi[:], pT[:]).then_inc(s_a_hi, 1)

            step(0)
            with act.Fori(1, STEPS - 2) as n:
                step(n)
            step(STEPS - 2, qk2=False)
            step(STEPS - 1, more=False)

            for i, (c, t) in enumerate(F_TILES):
                rows = min(P, (D if c == "d" else INTER) - t * P)
                cols = INTER if c == "d" else D
                act.wait_ge(s_f_mag, i + 1)
                if later(i):
                    act.wait_ge(s_f_trans, i)
                a.activation(f_q[0:rows, 0:cols], f_mag[0:rows, 0:cols], ACT.Copy,
                             bias=-MAGIC).then_inc(s_f_q, 1)
                act.wait_ge(s_f_trans, i + 1)
                src = pTb[:].rearrange("p (k s) -> p k s", s=P)
                if c == "d":
                    copy(wdT[:, 0:IT - 1, t * P:(t + 1) * P], src[:, 0:IT - 1, :])
                    copy(wdT[0:LAST, IT - 1, t * P:(t + 1) * P], src[0:LAST, IT - 1, :]).then_inc(s_f_out, 1)
                else:
                    w = wgT if c == "g" else wuT
                    copy(w[:, :, t * P:t * P + rows], src[:, 0:KT, 0:rows]).then_inc(s_f_out, 1)

            def ffn_tile(t):
                act.wait_ge(s_y_mag, t + 1)
                a.activation(y_q[:], y_mag[:], ACT.Copy, bias=-MAGIC).then_inc(s_y_q, 1)
                act.wait_ge(s_y_trans, t + 1)
                copy(y_qT[:], pTb[:, 0:KT * S]).then_inc(s_y_qT, 1)
                act.wait_ge(s_gate, t + 1)
                a.activation(th[:], gate[:], ACT.Tanh, scale=0.5).then_inc(s_th, 1)
                act.wait_ge(s_h_mag, t + 1)
                a.activation(h_q[:], gate[:], ACT.Copy, bias=-MAGIC).then_inc(s_h_q, 1)
                act.wait_ge(s_h_trans, t + 1)
                copy(h_qT[:, 0:(IT - 1) * S], pTb[:, 0:(IT - 1) * S])
                copy(h_qT[0:LAST, (IT - 1) * S:IT * S], pTb[0:LAST, (IT - 1) * S:IT * S]).then_inc(s_h_qT, 1)
                act.wait_ge(s_z_t, t + 1)
                copy(z[:, t, :], z_t[:]).then_inc(s_z, 1)

            ffn_tile(0)
            with act.Fori(1, B) as t:
                ffn_tile(t)

            act.wait_ge(s_zn, 1)
            a.activation(cz[:], cz2[:], ACT.Tanh, scale=0.5).then_inc(s_sig, 1)
            act.wait_ge(s_dA, 1)
            def route_tile(t):
                if later(t):
                    act.wait_ge(s_c_trans, t)
                for lt in range(KT):
                    last = a.activation(coef[:, lt, :], top[:, lt, t, :], ACT.Identity,
                                        scale=dA[:, lt, at(t)], bias=cz[:, lt, 1, at(t)])
                last.then_inc(s_coef, 1)
                act.wait_ge(s_f_t, t + 1)
                copy(fT[:], pU[:, 0:KT * S]).then_inc(s_fT, 1)
                act.wait_ge(s_top_logit, t + 1)
                a.activation(prb[:, 0:E], logit[:], ACT.Exp, bias=rsm[:, 0:1],
                             accum_out=rsm[:, 1:2]).then_inc(s_r_exp, 1)
                act.wait_ge(s_hw_t, t + 1)
                copy(hwT[:], pU[:, 1024:1024 + S]).then_inc(s_hwT, 1)

            route_tile(0)
            with act.Fori(1, B) as t:
                route_tile(t)

        @block.vector
        def _(dve):
            v = nc.vector

            v.memset(stats[:], 0.0)
            dve.wait_ge(s_mask_in, 16)
            dve.drain()
            v.tensor_scalar(mask_add[:], mask_u8[:], -1.0, -MASKED, ALU.add, ALU.mult)
            v.tensor_reduce(row_any[:], mask_u8[:], AX.X, ALU.max).then_inc(s_mask_add, 1)

            for half in range(2):
                tiles = range(half * HB, (half + 1) * HB)
                dve.drain()
                for b, t in enumerate(tiles):
                    dve.wait_ge(s_x_in, 16 * (t + 1))
                    v.bn_stats(stats[:, b, :], xr[:, t, :])
                dve.drain()
                for b in range(HB):
                    v.bn_aggr(mv[:, b, :], stats[:, b, :])
                dve.drain()
                v.tensor_scalar(ve[:], mv[:, :, 1], EPS, None, ALU.add).then_inc(s_var_in, 1)
                dve.wait_ge(s_rstd, 2 * half + 1)
                for b, t in enumerate(tiles):
                    v.tensor_scalar(hid[:, b, :], xr[:, t, :], mv[:, b, 0:1], rs[:, b:b + 1],
                                    ALU.subtract, ALU.mult).then_inc(s_h_done, 1)
                dve.drain()
                for b, t in enumerate(tiles):
                    v.tensor_tensor(xr[:, t, :], xr[:, t, :], hid[:, b, :], ALU.add)
                dve.wait_ge(s_ssq, (half + 1) * HB)
                v.tensor_scalar(ve[:], ssq[:], 1.0 / D, EPS, ALU.mult, ALU.add).then_inc(s_var_in, 1)
                dve.wait_ge(s_rstd, 2 * half + 2)
                dve.drain()
                for b in range(HB):
                    v.tensor_scalar(hid[:, b, :], hid[:, b, :], rs[:, b:b + 1], None,
                                    ALU.mult).then_inc(s_xn, 1)
                dve.wait_ge(s_lnw_in, 16)
                for b, t in enumerate(tiles):
                    dve.wait_ge(s_x_trans, t + 1)
                    v.tensor_tensor(hid[:, b, :].rearrange("p (k s) -> p k s", k=KT),
                                    [pX0, pX1, pS, pT][b][:].rearrange("p (k s) -> p k s", k=KT),
                                    lnw_col[:].to_broadcast([P, KT, S]), ALU.mult).then_inc(s_xw, 1)
                for b, t in enumerate(tiles):
                    dve.wait_ge(s_xT_hi, t + 1)
                    cols = slice(t * S, (t + 1) * S)
                    v.tensor_tensor(xT_lo[:, :, cols], hid[:, b, :].rearrange("p (k s) -> p k s", k=KT),
                                    xT_hi[:, :, cols].bitcast(F32), ALU.subtract).then_inc(s_xT_lo, 1)

            def query_low(n):
                dve.wait_ge(s_q_hi, n + 1)
                v.tensor_tensor(q_lo[:], pX0[:], q_hi[:].bitcast(F32), ALU.subtract).then_inc(s_q_lo, 1)

            def key_low(n):
                dve.wait_ge(s_k_hi, n + 1)
                v.tensor_tensor(k_lo[:], pX1[:], k_hi[:].bitcast(F32), ALU.subtract).then_inc(s_k_lo, 1)

            def pick_round(last=False):
                dve.drain()
                v.max(pick8[:], pick[:])
                dve.drain()
                if last and REST % 8:
                    v.memset(pick8[:, REST % 8:8], LOWEST)
                    dve.drain()
                v.match_replace(pick[:], pick8[:], pick[:], LOWEST)

            def step(n, picks, more=True):
                dve.wait_ge(s_s_done, n + 1)
                v.tensor_reduce(neg_max[:], pS[:].rearrange("p (b s) -> p b s", b=HB), AX.X, ALU.max,
                                negate=True).then_inc(s_max_done, 1)
                if picks:
                    dve.drain()
                    v.tensor_scalar(pick[:][:, ::-1], cT_raw[:, bass.ts(n, S)], -1.0, None, ALU.mult)
                    pick_round()
                    pick_round()
                dve.wait_ge(s_exp_done, n + 1)
                v.reciprocal(row_inv[:, :, 0], row_sum[:])
                dve.drain()
                v.tensor_tensor(row_inv[:, :, 0], row_inv[:, :, 0], row_any[:, half_of(n)], ALU.mult)
                dve.drain()
                v.tensor_tensor(prob[:], prob[:], row_inv[:].to_broadcast([P, HB, S]),
                                ALU.mult).then_inc(s_norm_done, 1)
                if more:
                    query_low(n + 1)
                if picks:
                    pick_round()
                    pick_round()
                if more:
                    key_low(n + 1)
                if picks:
                    pick_round()
                    pick_round()
                dve.wait_ge(s_p_hi, n + 1)
                v.tensor_tensor(pT_lo[:], pS[:], pT_hi[:].bitcast(F32), ALU.subtract).then_inc(s_p_lo, 1)
                dve.wait_ge(s_v_hi, n + 1)
                v.tensor_tensor(v_lo[:], pT[:], v_hi[:].bitcast(F32), ALU.subtract).then_inc(s_v_lo, 1)
                dve.wait_ge(s_a_hi, n + 1)
                v.tensor_tensor(aT_lo[:], pT[:], aT_hi[:].bitcast(F32), ALU.subtract).then_inc(s_a_lo, 1)
                if picks:
                    pick_round(last=True)
                    dve.drain()
                    v.tensor_scalar(top_flat[:, bass.ts(n, S)], pick[:][:, ::-1], LOWEST, None, ALU.not_equal)

            half_ = [0]

            def half_of(n):
                return slice(half_[0] * HB, (half_[0] + 1) * HB)

            def residual(half):
                dve.wait_ge(s_o_done, (half + 1) * H)
                for b in range(HB):
                    t = half * HB + b
                    last = v.tensor_tensor(xr[:, t, :], oacc[b][:], xr[:, t, :], ALU.add)
                last.then_inc(s_x1_done, 1)

            query_low(0)
            key_low(0)
            with dve.Fori(0, H) as n:
                step(n, picks=True)
            half_[0] = 1
            step(H, picks=False)
            residual(0)
            with dve.Fori(H + 1, STEPS - 1) as n:
                step(n, picks=False)
            step(STEPS - 1, picks=False, more=False)
            residual(1)

            for i, (c, t) in enumerate(F_TILES):
                rows = min(P, (D if c == "d" else INTER) - t * P)
                cols = INTER if c == "d" else D
                dve.wait_ge(s_f_in, 16 * (i + 1) )
                dve.drain()
                v.tensor_reduce(f_s[0:rows, 0:1], f_raw[0:rows, 0:cols], AX.X, ALU.max, apply_absolute_value=True)
                dve.drain()
                v.tensor_scalar(f_s[0:rows, 1:2], f_s[0:rows, 0:1], 1.0 / QMAX, 1e-8, ALU.mult, ALU.max)
                dve.drain()
                v.reciprocal(f_s[0:rows, 2:3], f_s[0:rows, 1:2])
                if later(i):
                    dve.wait_ge(s_f_trans, i)
                v.tensor_scalar(f_diag[0:rows, 0:rows], ident[0:rows, 0:rows], f_s[0:rows, 1:2], None,
                                ALU.mult).then_inc(s_f_diag, 1)
                dve.drain()
                if later(i):
                    dve.wait_ge(s_f_q, i)
                v.tensor_scalar(f_mag[0:rows, 0:cols], f_raw[0:rows, 0:cols], f_s[0:rows, 2:3], MAGIC,
                                ALU.mult, ALU.add).then_inc(s_f_mag, 1)
                dve.wait_ge(s_f_trans, i + 1)
                row = {"g": sg_row, "u": su_row, "d": sd_row}[c]
                v.tensor_copy(row[:, t * P:t * P + rows], pU[:, 0:rows]).then_inc(s_f_row, 1)

            dve.wait_ge(s_diag, 2)
            dve.wait_ge(s_const_in, 16 * 7)
            for c in range(2):
                v.tensor_scalar(band[c][:], diag[:, 0:3 * P], taps[:, c * TAPS:c * TAPS + 1], None, ALU.mult)
                for j in range(1, TAPS):
                    dve.drain()
                    v.scalar_tensor_tensor(out=band[c][:], in0=diag[:, j:j + 3 * P],
                                           scalar=taps[:, c * TAPS + j:c * TAPS + j + 1], in1=band[c][:],
                                           op0=ALU.mult, op1=ALU.add)
            dve.drain()
            v.memset(prb[:, E:2 * E], -1.0).then_inc(s_band, 1)

            def layernorm(dst, src, n, tile=0):
                dve.drain()
                v.bn_stats(st6[:], src)
                dve.drain()
                v.bn_aggr(mv1[:], st6[:])
                dve.drain()
                v.tensor_scalar(ve1[:, 0:1], mv1[:, 1:2], EPS, None, ALU.add).then_inc(s_var_in, 1)
                dve.wait_ge(s_rstd, n + 1)
                if later(tile):
                    dve.wait_ge(s_z, tile)
                    dve.wait_ge(s_z_trans, tile)
                return v.tensor_scalar(dst, src, mv1[:, 0:1], rs1[:, 0:1], ALU.subtract, ALU.mult)

            def scale_of(tile, s):
                dve.drain()
                v.tensor_reduce(s[:, 0:1], tile, AX.X, ALU.max, apply_absolute_value=True)
                dve.drain()
                v.tensor_scalar(s[:, 1:2], s[:, 0:1], 1.0 / QMAX, 1e-8, ALU.mult, ALU.max)
                dve.drain()
                v.reciprocal(s[:, 2:3], s[:, 1:2])
                dve.drain()

            def ffn_tile(t):
                layernorm(y[:], xr[:, t, :], 2 * t + 4)
                scale_of(y[:], y_s)
                v.tensor_scalar(y_mag[:], y[:], y_s[:, 2:3], MAGIC, ALU.mult, ALU.add).then_inc(s_y_mag, 1)
                dve.wait_ge(s_g_proj, t + 1)
                v.scalar_tensor_tensor(out=gate[:], in0=pG[:, 0:INTER], scalar=y_s[:, 1:2], in1=sg_row[:],
                                       op0=ALU.mult, op1=ALU.mult).then_inc(s_gate, 1)
                dve.wait_ge(s_u_proj, t + 1)
                v.scalar_tensor_tensor(out=up[:], in0=pU[:, 0:INTER], scalar=y_s[:, 1:2], in1=su_row[:],
                                       op0=ALU.mult, op1=ALU.mult)
                dve.drain()
                dve.wait_ge(s_th, t + 1)
                v.scalar_tensor_tensor(out=th[:], in0=th[:], scalar=1.0, in1=gate[:], op0=ALU.add, op1=ALU.mult)
                dve.drain()
                v.scalar_tensor_tensor(out=up[:], in0=th[:], scalar=0.5, in1=up[:], op0=ALU.mult, op1=ALU.mult)
                scale_of(up[:], h_s)
                v.tensor_scalar(gate[:], up[:], h_s[:, 2:3], MAGIC, ALU.mult, ALU.add).then_inc(s_h_mag, 1)
                dve.wait_ge(s_d_proj, t + 1)
                v.scalar_tensor_tensor(out=y[:], in0=pG[:, 0:D], scalar=h_s[:, 1:2], in1=sd_row[:],
                                       op0=ALU.mult, op1=ALU.mult)
                dve.drain()
                v.tensor_tensor(xr[:, t, :], xr[:, t, :], y[:], ALU.add)
                layernorm(z_t[:], xr[:, t, :], 2 * t + 5, tile=t).then_inc(s_z_t, 1)
                dve.wait_ge(s_z_trans, t + 1)
                zT = pU[:, 0:D].rearrange("p (k s) -> p k s", k=KT)
                v.tensor_tensor(cf[:], zT, top[:, :, t, :], ALU.mult)
                dve.drain()
                v.tensor_tensor(sf[:], zT, cf[:], ALU.subtract)
                dve.drain()
                for br, part in enumerate((cf, sf)):
                    v.tensor_reduce(stat[0][:, :, br, at(t)], part[:], AX.X, ALU.max)
                    last = v.tensor_reduce(stat[1][:, :, br, at(t)], part[:], AX.X, ALU.add)
                last.then_inc(s_z_used, 1)

            ffn_tile(0)
            with dve.Fori(1, B) as t:
                ffn_tile(t)

            dve.drain()
            for br, n in enumerate((CRUCIAL, REST)):
                v.tensor_scalar(stat[1][:, :, br, :], stat[1][:, :, br, :], 1.0 / S, S / n,
                                ALU.mult, ALU.mult).then_inc(s_stats, 1)
            dve.wait_ge(s_conv, 1)
            conv = pG[:, 0:KT * 2 * B].rearrange("p (k r b) -> p k r b", k=KT, r=2)
            v.tensor_copy(cz[:], conv)
            dve.drain()
            v.tensor_reduce(csum[:], cz[:].rearrange("p k r b -> p r k b"), AX.XY, ALU.add).then_inc(s_csum, 1)
            dve.wait_ge(s_ctotal, 1)
            v.tensor_scalar(cmu[:], pG[:, 512:514], 1.0 / (B * D), None, ALU.mult)
            dve.drain()
            for br in range(2):
                v.tensor_scalar(cz[:, :, br, :], cz[:, :, br, :], cmu[:, br:br + 1], None, ALU.subtract)
            dve.drain()
            v.tensor_tensor(cz2[:], cz[:], cz[:], ALU.mult)
            dve.drain()
            v.tensor_reduce(csum[:], cz2[:].rearrange("p k r b -> p r k b"), AX.XY, ALU.add).then_inc(s_csum, 1)
            dve.wait_ge(s_ctotal, 2)
            v.tensor_scalar(ve1[:], pG[:, 1024:1026], 1.0 / (B * D), EPS, ALU.mult, ALU.add).then_inc(s_var_in, 1)
            dve.wait_ge(s_rstd, 2 * B + 5)
            for br in range(2):
                v.tensor_scalar(cz2[:, :, br, :], cz[:, :, br, :], rs1[:, br:br + 1], gb[:, 0:1],
                                ALU.mult, ALU.mult)
            dve.drain()
            v.tensor_scalar(cz2[:], cz2[:], gb[:, 1:2], 0.0, ALU.add, ALU.max).then_inc(s_zn, 1)
            dve.wait_ge(s_sig, 1)
            v.tensor_scalar(cz[:], cz[:], 0.5, 0.5, ALU.mult, ALU.add)
            dve.drain()
            v.tensor_tensor(dA[:], cz[:, :, 0, :], cz[:, :, 1, :], ALU.subtract).then_inc(s_dA, 1)

            def route_tile(t):
                dve.wait_ge(s_c_trans, t + 1)
                v.tensor_tensor(y[:], pG[:, 0:D], z[:, t, :], ALU.mult)
                dve.drain()
                v.tensor_tensor(x3[:], y[:], xr[:, t, :], ALU.add)
                layernorm(f[:], x3[:], t + 2 * B + 5).then_inc(s_f, 1)
                dve.wait_ge(s_r_proj, t + 1)
                v.tensor_tensor(logit[:], pG[:, 512:512 + E], rb[:], ALU.add)
                dve.drain()
                v.tensor_reduce(rsm[:, 0:1], logit[:], AX.X, ALU.max, negate=True).then_inc(s_top_logit, 1)
                dve.wait_ge(s_r_exp, t + 1)
                v.reciprocal(rsm[:, 2:3], rsm[:, 1:2])
                dve.drain()
                v.tensor_scalar(prb[:, 0:E], prb[:, 0:E], rsm[:, 2:3], None, ALU.mult)
                dve.drain()
                v.max(best[:], prb[:])
                dve.drain()
                v.tensor_tensor(rsm[:, 3:4], best[:, 0:1], best[:, 1:2], ALU.add)
                v.memset(best[:, 2:8], -1.0)
                dve.drain()
                v.match_replace(prw[:], best[:], prb[:], -2.0)
                v.reciprocal(rsm[:, 2:3], rsm[:, 3:4])
                dve.drain()
                v.scalar_tensor_tensor(out=prw[:, 0:E], in0=prw[:, 0:E], scalar=-2.0, in1=prb[:, 0:E],
                                       op0=ALU.is_equal, op1=ALU.mult)
                dve.drain()
                v.tensor_scalar(wexp[:, :, 0], prw[:, 0:E], rsm[:, 2:3], None, ALU.mult)
                dve.drain()
                v.tensor_tensor(hw[:], pG[:, 512 + E:512 + E + ER].rearrange("p (e r) -> p e r", e=E),
                                wexp[:].to_broadcast([P, E, R]), ALU.mult).then_inc(s_hw, 1)
                dve.wait_ge(s_l_proj, t + 1)
                if later(t):
                    dve.wait_ge(s_out, 16 * t)
                v.scalar_tensor_tensor(out=x4[:], in0=pG[:, 1024:1024 + D], scalar=8.0 / R, in1=x3[:],
                                       op0=ALU.mult, op1=ALU.add).then_inc(s_x4_done, 1)

            route_tile(0)
            with dve.Fori(1, B) as t:
                route_tile(t)

        @block.tensor
        def _(pe):
            mm = nc.tensor.matmul

            def three(dst, left, right, start=True, stop=True, lint=False):
                (lh, ll), (rh, rl) = left, right
                mm(dst, lh, rl, start=start, stop=False, skip_group_check=lint)
                mm(dst, ll, rh, start=False, stop=False, skip_group_check=lint)
                return mm(dst, lh, rh, start=False, stop=stop, skip_group_check=lint)

            def tr(dst, src, ident):
                return mm(dst, src, ident, is_transpose=True, start=True, stop=True)

            pe.wait_ge(s_ident, 3)
            for t in range(B):
                b = t % HB
                pe.wait_ge(s_xn, t + 1)
                for kt in range(KT):
                    last = tr([pX0, pX1, pS, pT][b][:, kt * S:(kt + 1) * S], hid[:, b, kt * P:(kt + 1) * P], ident[:])
                last.then_inc(s_x_trans, 1)

            def project(dst, c, src, half):
                cols = slice(half * NH, (half + 1) * NH)
                for kt in range(KT):
                    w = tuple(w[c][:, kt * P:(kt + 1) * P] for w in (w_hi, w_lo))
                    last = three(dst, w, tuple(s[:, kt, cols] for s in src), start=kt == 0, stop=kt == KT - 1)
                return last

            xT = (xT_hi, xT_lo)
            cT_ = (cT_hi, cT_lo)

            def queries(n, half):
                pe.wait_ge(s_w_lo["q"], n + 1)
                if later(n - 1):
                    pe.wait_ge(s_vT, n - 1)
                project(pX0[:], "q", xT, half).then_inc(s_q_proj, 1)

            def keys(n, half):
                pe.wait_ge(s_w_lo["k"], n + 1)
                if later(n):
                    pe.wait_ge(s_k_lo, n)
                project(pX1[:], "k", cT_, half).then_inc(s_k_proj, 1)

            def outputs(n, start=False):
                pe.wait_ge(s_a_lo, n + 1)
                pe.wait_ge(s_w_lo["o"], n + 1)
                for b in range(HB):
                    cols = slice(b * S, (b + 1) * S)
                    last = three(oacc[b][:], (aT_hi[:, cols], aT_lo[:, cols]), (w_hi["o"][:], w_lo["o"][:]),
                                 start=start, stop=False, lint=True)
                last.then_inc(s_o_done, 1)

            def step(n, half, next_half, first=False, after_first=False, more=True):
                pe.wait_ge(s_q_lo, n + 1)
                pe.wait_ge(s_k_lo, n + 1)
                pe.wait_ge(s_b_lo, n + 1)
                if later(n):
                    pe.wait_ge(s_p_lo, n)
                mm(pS[:], ident_b[:], mask_add[:, half * HB:(half + 1) * HB, :], start=True, stop=False,
                   skip_group_check=True)
                for part in (b_lo, b_hi):
                    mm(pS[:], ident_r[:], part[:].to_broadcast([P, HB, S]), start=False, stop=False,
                       skip_group_check=True)
                for b in range(HB):
                    cols = slice(b * S, (b + 1) * S)
                    last = three(pS[:, cols], (q_hi[:, cols], q_lo[:, cols]), (k_hi[:, cols], k_lo[:, cols]),
                                 start=False, stop=b == HB - 1, lint=True)
                last.then_inc(s_s_done, 1)
                if more:
                    queries(n + 1, next_half)
                    keys(n + 1, next_half)
                pe.wait_ge(s_w_lo["v"], n + 1)
                if more:
                    pe.wait_ge(s_q_lo, n + 2)
                project(pX0[:], "v", cT_, half).then_inc(s_v_proj, 1)
                pe.wait_ge(s_norm_done, n + 1)
                for b in range(HB):
                    last = tr(pS[:, b * S:(b + 1) * S], prob[:, b, :], ident[:])
                last.then_inc(s_p_trans, 1)
                pe.wait_ge(s_vT, n + 1)
                if later(n):
                    pe.wait_ge(s_a_lo, n)
                for b in range(HB):
                    last = tr(pT[:, b * S:(b + 1) * S], vT[:, b * S:(b + 1) * S], ident[:])
                last.then_inc(s_v_trans, 1)
                if not first:
                    if after_first and half:
                        pe.wait_ge(s_x1_done, 1)
                    outputs(n - 1, start=after_first)
                pe.wait_ge(s_p_lo, n + 1)
                pe.wait_ge(s_v_lo, n + 1)
                for b in range(HB):
                    cols = slice(b * S, (b + 1) * S)
                    last = three(pT[:, cols], (v_hi[:, cols], v_lo[:, cols]), (pT_hi[:, cols], pT_lo[:, cols]))
                last.then_inc(s_a_done, 1)

            pe.wait_ge(s_xT_lo, B)
            pe.wait_ge(s_cT_lo, 2 * KT)
            pe.wait_ge(s_mask_add, 1)
            queries(0, 0)
            keys(0, 0)
            step(0, 0, 0, first=True)
            step(1, 0, 0, after_first=True)
            with pe.Fori(2, H - 1) as n:
                step(n, 0, 0)
            step(H - 1, 0, 1)
            step(H, 1, 1)
            step(H + 1, 1, 1, after_first=True)
            with pe.Fori(H + 2, STEPS - 1) as n:
                step(n, 1, 1)
            step(STEPS - 1, 1, 1, more=False)
            outputs(STEPS - 1)

            for i, (c, t) in enumerate(F_TILES):
                rows = min(P, (D if c == "d" else INTER) - t * P)
                pe.wait_ge(s_f_diag, i + 1)
                if later(i):
                    pe.wait_ge(s_f_row, i)
                if i == 0:
                    pe.wait_ge(s_x1_done, 2)
                mm(pU[:, 0:rows], ones[0:rows, :], f_diag[0:rows, 0:rows], start=True, stop=True)
                pe.wait_ge(s_f_q, i + 1)
                if later(i):
                    pe.wait_ge(s_f_out, i)
                for k in range(IT if c == "d" else KT):
                    cols = min(P, INTER - k * P)
                    last = tr(pTb[0:cols, k * P:k * P + rows], f_q[0:rows, k * P:k * P + cols], ident_b[0:rows, 0:rows])
                last.then_inc(s_f_trans, 1)
            pe.wait_ge(s_f_out, len(F_TILES))
            pe.wait_ge(s_f_row, len(F_TILES))

            def ffn_tile(t):
                pe.wait_ge(s_y_q, t + 1)
                if later(t):
                    pe.wait_ge(s_h_qT, t)
                if later(t):
                    pe.wait_ge(s_z_used, t)
                for kt in range(KT):
                    last = tr(pTb[:, kt * S:(kt + 1) * S], y_q[:, kt * P:(kt + 1) * P], ident_b[:])
                last.then_inc(s_y_trans, 1)
                pe.wait_ge(s_y_qT, t + 1)
                for w, dst, projected in ((wgT, pG, s_g_proj), (wuT, pU, s_u_proj)):
                    for c0 in range(0, INTER, 512):
                        c1 = min(c0 + 512, INTER)
                        for kt in range(KT):
                            last = mm(dst[:, c0:c1], y_qT[:, kt * S:(kt + 1) * S], w[:, kt, c0:c1],
                                      start=kt == 0, stop=kt == KT - 1)
                    last.then_inc(projected, 1)
                pe.wait_ge(s_h_q, t + 1)
                for k in range(IT):
                    cols = min(P, INTER - k * P)
                    last = tr(pTb[0:cols, k * S:(k + 1) * S], h_q[:, k * P:k * P + cols], ident_b[:])
                last.then_inc(s_h_trans, 1)
                pe.wait_ge(s_h_qT, t + 1)
                for k in range(IT):
                    rows = min(P, INTER - k * P)
                    last = mm(pG[:, 0:D], h_qT[0:rows, k * S:(k + 1) * S], wdT[0:rows, k, :],
                              start=k == 0, stop=k == IT - 1)
                last.then_inc(s_d_proj, 1)
                pe.wait_ge(s_z_t, t + 1)
                for kt in range(KT):
                    last = tr(pU[:, kt * S:(kt + 1) * S], z_t[:, kt * P:(kt + 1) * P], ident[:])
                last.then_inc(s_z_trans, 1)

            ffn_tile(0)
            with pe.Fori(1, B) as t:
                ffn_tile(t)

            pe.wait_ge(s_stats, 2)
            pe.wait_ge(s_band, 1)
            for lt in range(KT):
                terms = [(c, d) for c in range(2) for d in (-1, 0, 1) if 0 <= lt + d < KT]
                for i, (c, d) in enumerate(terms):
                    last = mm(pG[:, lt * 2 * B:(lt + 1) * 2 * B], band[c][:, (1 - d) * P:(2 - d) * P],
                              stat[c][:, lt + d, :, :], start=i == 0, stop=i == len(terms) - 1)
            last.then_inc(s_conv, 1)
            for i in range(2):
                pe.wait_ge(s_csum, i + 1)
                mm(pG[:, 512 * (i + 1):512 * (i + 1) + 2], ones[:], csum[:], start=True, stop=True)\
                    .then_inc(s_ctotal, 1)

            pe.wait_ge(s_dA, 1)
            def route_tile(t):
                pe.wait_ge(s_coef, t + 1)
                if later(t):
                    pe.wait_ge(s_x4_done, t)
                for kt in range(KT):
                    last = tr(pG[:, kt * P:(kt + 1) * P], coef[:, kt, :], ident[:])
                last.then_inc(s_c_trans, 1)
                pe.wait_ge(s_f, t + 1)
                for kt in range(KT):
                    last = tr(pU[:, kt * S:(kt + 1) * S], f[:, kt * P:(kt + 1) * P], ident[:])
                last.then_inc(s_f_t, 1)
                pe.wait_ge(s_fT, t + 1)
                for kt in range(KT):
                    last = mm(pG[:, 512:512 + E + ER], fT[:, kt * S:(kt + 1) * S], ra[:, kt, :],
                              start=kt == 0, stop=kt == KT - 1)
                last.then_inc(s_r_proj, 1)
                pe.wait_ge(s_hw, t + 1)
                tr(pU[:, 1024:1024 + S], hw[:].rearrange("p e r -> p (e r)"), ident[:]).then_inc(s_hw_t, 1)
                pe.wait_ge(s_hwT, t + 1)
                mm(pG[:, 1024:1024 + D], hwT[:], lb[:], start=True, stop=True).then_inc(s_l_proj, 1)

            route_tile(0)
            with pe.Fori(1, B) as t:
                route_tile(t)


def kernel(**inputs):
    import concourse.bacc as bacc
    from concourse.bass_utils import run_bass_kernel_spmd

    def host(name):
        return np.asarray(inputs[name])

    def tile_rows(w):
        return w.T.reshape(KT, P, -1).transpose(1, 0, 2)

    def per_head(w):
        return w.reshape(H, DH, KT, P).transpose(0, 3, 2, 1).reshape(H, P, KT * DH)

    def rows(v):
        return np.broadcast_to(v.reshape(1, -1), (P, v.size))

    arrays = {
        "x": host("x"),
        "cT": host("ctx_4096").reshape(B * S, D).T.reshape(KT, P, B * S),
        "mask": host("mask_BxSxS2_bk0").transpose(1, 0, 2),
        "bias": host("L0_xattn_position_bias"),
        "ln_w": host("L0_xattn_ln_weight").reshape(KT, P).T,
        "wq": per_head(host("L0_xattn_w_q")),
        "wk": per_head(host("L0_xattn_w_k")),
        "wv": per_head(host("L0_xattn_w_v")),
        "wo": host("L0_xattn_w_out").reshape(D, H, DH).transpose(1, 2, 0),
        "w_gate": host("L0_ffn_w_gate"),
        "w_up": host("L0_ffn_w_up"),
        "w_down": host("L0_ffn_w_down"),
        "conv_w": rows(host("L1_xattn_conv_w")),
        "gamma": rows(host("L1_xattn_bn_gamma")),
        "beta": rows(host("L1_xattn_bn_beta")),
        "router_w": tile_rows(host("L1_ffn_router_w")),
        "router_b": rows(host("L1_ffn_router_b")),
        "lora_a": tile_rows(host("L1_ffn_A").reshape(ER, D)),
        "lora_b": host("L1_ffn_Bm").transpose(0, 2, 1).reshape(ER, D),
    }
    arrays = {f"in_{name}": np.ascontiguousarray(a) for name, a in arrays.items()}
    nc = bacc.Bacc("TRN2", target_bir_lowering=False, num_devices=1)
    args = [nc.dram_tensor(name, a.shape, mybir.dt.from_np(a.dtype), kind="ExternalInput").ap()
            for name, a in arrays.items()]
    out = nc.dram_tensor("out", (B, S, D), F32, kind="ExternalOutput").ap()
    layers_kernel(nc, *args, out)
    result = run_bass_kernel_spmd(nc, [arrays], core_ids=[0])
    return result.results[0]["out"]
```

```python
from contextlib import ExitStack

import numpy as np

import concourse.bass as bass
from concourse import mybir

F32 = mybir.dt.float32
F32R = mybir.dt.float32r
BF16 = mybir.dt.bfloat16
U8 = mybir.dt.uint8
ALU = mybir.AluOpType
ACT = mybir.ActivationFunctionType
AX = mybir.AxisListType

P = 128
B = 8
S = 128
D = 512
KT = D // P
H = 32
DH = 128
HB = B // 2
NH = HB * S
STEPS = 2 * H
PAIRS = STEPS // 2
INTER = 1376
IT = -(-INTER // P)
LAST = INTER - (IT - 1) * P
FR = INTER * 2 // H
E = 8
R = 16
ER = E * R
EPS = 1e-5
MAGIC = 12582912.0
QMAX = 127.0
LOWEST = -3.4028234663852886e38
MASKED = -1e30
TAPS = 7
CRUCIAL = int(0.6 * S) + int(0.6 * S) % 2
REST = S - CRUCIAL


def layers_kernel(nc, x, cT, mask, bias, ln_w, wq, wk, wv, wo, w_gate, w_up, w_down,
                  conv_w, gamma, beta, router_w, router_b, lora_a, lora_b, out):
    ctx = ExitStack()

    def sbuf(name, shape, dt=F32, stack=ctx):
        return stack.enter_context(nc.sbuf_tensor(name, shape, dt))

    def psum(name, shape, dt=F32, stack=ctx):
        return stack.enter_context(nc.psum_tensor(name, shape, dt))

    def sem(name):
        return ctx.enter_context(nc.semaphore(name))

    with ctx:
        xr = sbuf("xr", [P, B, D])
        top_flat = sbuf("top", [P, KT * B * S], BF16)
        top = top_flat[:].rearrange("p (k b s) -> p k b s", k=KT, b=B)
        ident = sbuf("ident", [P, P])
        ident_b = sbuf("ident_b", [P, P], BF16)
        ones = sbuf("ones", [P, P])
        neg_half = sbuf("neg_half", [P, B])

        early = ExitStack()
        xT_hi = [sbuf("xT0_hi", [P, KT, NH], F32R, early)]
        xT_lo = [sbuf("xT0_lo", [P, KT, NH], F32R, early)]
        cT_hi = [sbuf("cT0_hi", [P, KT, NH], F32R, early)]
        cT_lo = [sbuf("cT0_lo", [P, KT, NH], F32R, early)]
        cT_raw = sbuf("cT_raw", [P, KT * B * S], F32, early)
        hid = sbuf("hid", [P, HB, D], F32, early)
        sq_junk = sbuf("sq_junk", [P, D], F32, early)
        mask_u8 = sbuf("mask_u8", [P, B, S], U8, early)

        att = ExitStack()
        xT_hi.append(sbuf("xT1_hi", [P, KT, NH], F32R, att))
        xT_lo.append(sbuf("xT1_lo", [P, KT, NH], F32R, att))
        cT_hi.append(sbuf("cT1_hi", [P, KT, NH], F32R, att))
        cT_lo.append(sbuf("cT1_lo", [P, KT, NH], F32R, att))
        width = {"q": D, "k": D, "v": 2 * D, "o": D}
        w_raw = {c: sbuf(f"raw_{c}", [P, width[c]], F32, att) for c in "qkvo"}
        w_hi = {c: sbuf(f"w{c}_hi", [P, width[c]], F32R, att) for c in "qkvo"}
        w_lo = {c: sbuf(f"w{c}_lo", [P, width[c]], F32R, att) for c in "qkvo"}
        b_raw = sbuf("b_raw", [P, 1, S], F32, att)
        b_mask = sbuf("b_mask", [P, HB, S], F32, att)
        score = sbuf("score", [P, HB, S], F32, att)
        q_hi = sbuf("q_hi", [P, NH], F32R, att)
        q_lo = sbuf("q_lo", [P, NH], F32R, att)
        k_hi = sbuf("k_hi", [P, NH], F32R, att)
        k_lo = sbuf("k_lo", [P, NH], F32R, att)
        v_hi = sbuf("v_hi", [P, HB, 2 * DH], F32R, att)
        v_lo = sbuf("v_lo", [P, HB, 2 * DH], F32R, att)
        prob = sbuf("prob", [P, HB, S], F32, att)
        pT_hi = sbuf("pT_hi", [P, NH], F32R, att)
        pT_lo = sbuf("pT_lo", [P, NH], F32R, att)
        aT_hi = sbuf("aT_hi", [P, NH], F32R, att)
        aT_lo = sbuf("aT_lo", [P, NH], F32R, att)
        mask_add = sbuf("mask_add", [P, B, S], BF16, att)
        row_any = sbuf("row_any", [P, B], F32, att)
        neg_max = sbuf("neg_max", [P, HB], F32, att)
        row_sum = sbuf("row_sum", [P, HB], F32, att)
        row_inv = sbuf("row_inv", [P, HB, 1], F32, att)
        stats = sbuf("stats", [P, HB, 6], F32, att)
        mv = sbuf("mv", [P, HB, 2], F32, att)
        ve = sbuf("ve", [P, HB], F32, att)
        rs = sbuf("rs", [P, HB], F32, att)
        ssq = sbuf("ssq", [P, HB], F32, att)
        lnw_col = sbuf("lnw_col", [P, KT, 1], F32, att)
        pick = sbuf("pick", [P, 2, S], F32, att)
        pick8 = sbuf("pick8", [P, 2, 8], F32, att)
        oacc = [psum(f"oacc{b}", [P, D], F32, att) for b in range(HB)]
        pX0 = psum("pX0", [P, NH], F32, att)
        pX1 = psum("pX1", [P, NH], F32, att)
        pS = psum("pS", [P, NH], F32, att)
        pT = psum("pT", [P, NH], F32, att)
        att.close()
        early.close()

        wguT = sbuf("wguT", [P, KT, 2 * INTER], BF16)
        gu_row = sbuf("gu_row", [P, 2 * INTER])
        wdT = sbuf("wdT", [P, IT, D], BF16)
        sd_row = sbuf("sd_row", [P, D])
        f_s = sbuf("f_s", [P, 4])
        f_diag = sbuf("f_diag", [P, P])
        g_raw = sbuf("g_raw", [P, D])
        g_mag = sbuf("g_mag", [P, D])
        g_q = sbuf("g_q", [P, D], BF16)

        post = ExitStack()
        f_raw = sbuf("f_raw", [P, INTER], F32, post)
        f_mag = sbuf("f_mag", [P, INTER], F32, post)
        f_q = sbuf("f_q", [P, INTER], BF16, post)
        y = sbuf("y", [P, D], F32, post)
        y_mag = sbuf("y_mag", [P, D], F32, post)
        y_q = sbuf("y_q", [P, D], BF16, post)
        y_qT = sbuf("y_qT", [P, KT * S], BF16, post)
        y_s = sbuf("y_s", [P, 4], F32, post)
        y_step = sbuf("y_step", [P, 1], F32, post)
        gate = sbuf("gate", [P, INTER], F32, post)
        silu = sbuf("silu", [P, INTER], F32, post)
        up = sbuf("up", [P, INTER], F32, post)
        h_mag = sbuf("h_mag", [P, INTER], F32, post)
        h_q = sbuf("h_q", [P, INTER], BF16, post)
        h_qT = sbuf("h_qT", [P, IT * S], BF16, post)
        h_s = sbuf("h_s", [P, 4], F32, post)
        down = sbuf("down", [P, D], F32, post)
        z = sbuf("z", [P, B, D], F32, post)
        z_t = sbuf("z_t", [P, D], F32, post)
        cf = sbuf("cf", [P, KT, S], F32, post)
        sf = sbuf("sf", [P, KT, S], F32, post)
        st6 = sbuf("st6", [P, 6], F32, post)
        mv1 = sbuf("mv1", [P, 2], F32, post)
        ve1 = sbuf("ve1", [P, 2], F32, post)
        rs1 = sbuf("rs1", [P, 2], F32, post)
        stat = [sbuf(f"stat{c}", [P, KT, 2, B], F32, post) for c in range(2)]
        taps = sbuf("taps", [P, 2 * TAPS], F32, post)
        diag = sbuf("diag", [P, 3 * P + TAPS - 1], F32, post)
        band = [sbuf(f"band{c}", [P, 3 * P], F32, post) for c in range(2)]
        cz = sbuf("cz", [P, KT, 2, B], F32, post)
        cz2 = sbuf("cz2", [P, KT, 2, B], F32, post)
        csum = sbuf("csum", [P, 2], F32, post)
        cmu = sbuf("cmu", [P, 2], F32, post)
        gb = sbuf("gb", [P, 2], F32, post)
        dA = sbuf("dA", [P, KT, B], F32, post)
        coef = sbuf("coef", [P, KT, S], F32, post)
        f = sbuf("f", [P, D], F32, post)
        fT = sbuf("fT", [P, KT * S], F32, post)
        ra = sbuf("ra", [P, KT, E + ER], F32, post)
        rb = sbuf("rb", [P, 1, E], F32, post)
        lb = sbuf("lb", [P, D], F32, post)
        rh = sbuf("rh", [P, B, E + ER], F32, post)
        logit = sbuf("logit", [P, B, E], F32, post)
        r_max = sbuf("r_max", [P, B, 1], F32, post)
        r_inv = sbuf("r_inv", [P, B, 1], F32, post)
        prb = sbuf("prb", [P, B, 2 * E], F32, post)
        prw = sbuf("prw", [P, B, 2 * E], F32, post)
        best = sbuf("best", [P, B, 8], F32, post)
        wexp = sbuf("wexp", [P, B, E, 1], F32, post)
        hw = sbuf("hw", [P, B, E, R], F32, post)
        hwT = sbuf("hwT", [P, 2, S], F32, post)
        x4 = sbuf("x4", [P, 2, D], F32, post)
        pA = psum("pA", [P, 3 * 512], F32, post)
        pTb = psum("pTb", [P, 2 * 1024], BF16, post)
        pD = psum("pD", [P, 512], F32, post)
        pZ = psum("pZ", [P, 512], F32, post)
        pYb = psum("pYb", [P, 1024], BF16, post)
        post.close()

        s_a_done = sem("a_done")
        s_a_hi = sem("a_hi")
        s_a_lo = sem("a_lo")
        s_b_mask = sem("b_mask")
        s_band = sem("band")
        s_cT_hi = sem("cT_hi")
        s_cT_lo = sem("cT_lo")
        s_c_in = sem("c_in")
        s_c_trans = sem("c_trans")
        s_c_used = sem("c_used")
        s_coef = sem("coef")
        s_const_in = sem("const_in")
        s_conv = sem("conv")
        s_csum = sem("csum")
        s_ctotal = sem("ctotal")
        s_dA = sem("dA")
        s_d_proj = sem("d_proj")
        s_d_used = sem("d_used")
        s_diag = sem("diag")
        s_exp_done = sem("exp_done")
        s_f = sem("f")
        s_fT = sem("fT")
        s_f_diag = sem("f_diag")
        s_f_in = sem("f_in")
        s_f_mag = sem("f_mag")
        s_f_out = sem("f_out")
        s_f_q = sem("f_q")
        s_f_row = sem("f_row")
        s_f_t = sem("f_t")
        s_f_trans = sem("f_trans")
        s_g_diag = sem("g_diag")
        s_g_in = sem("g_in")
        s_g_mag = sem("g_mag")
        s_g_out = sem("g_out")
        s_g_proj = sem("g_proj")
        s_g_q = sem("g_q")
        s_g_trans = sem("g_trans")
        s_gate = sem("gate")
        s_h_done = sem("h_done")
        s_h_mag = sem("h_mag")
        s_h_q = sem("h_q")
        s_h_qT = sem("h_qT")
        s_h_trans = sem("h_trans")
        s_hw = sem("hw")
        s_hwT = sem("hwT")
        s_hw_t = sem("hw_t")
        s_ident = sem("ident")
        s_k_hi = sem("k_hi")
        s_k_lo = sem("k_lo")
        s_k_proj = sem("k_proj")
        s_l_proj = sem("l_proj")
        s_lnw_in = sem("lnw_in")
        s_mask_add = sem("mask_add")
        s_mask_in = sem("mask_in")
        s_max_done = sem("max_done")
        s_neg_half = sem("neg_half")
        s_norm_done = sem("norm_done")
        s_o_done = sem("o_done")
        s_ones = sem("ones")
        s_p_hi = sem("p_hi")
        s_p_lo = sem("p_lo")
        s_p_trans = sem("p_trans")
        s_q_hi = sem("q_hi")
        s_q_lo = sem("q_lo")
        s_q_proj = sem("q_proj")
        s_r_exp = sem("r_exp")
        s_r_proj = sem("r_proj")
        s_rh = sem("rh")
        s_rstd = sem("rstd")
        s_s_done = sem("s_done")
        s_scored = sem("scored")
        s_sig = sem("sig")
        s_silu = sem("silu")
        s_ssq = sem("ssq")
        s_stats = sem("stats")
        s_top_logit = sem("top_logit")
        s_u_proj = sem("u_proj")
        s_up = sem("up")
        s_up_copy = sem("up_copy")
        s_v_hi = sem("v_hi")
        s_v_lo = sem("v_lo")
        s_v_proj = sem("v_proj")
        s_var_in = sem("var_in")
        s_x1_done = sem("x1_done")
        s_x4_done = sem("x4_done")
        s_xT_hi = sem("xT_hi")
        s_xT_lo = sem("xT_lo")
        s_x_in = sem("x_in")
        s_x_trans = sem("x_trans")
        s_xn = sem("xn")
        s_xw = sem("xw")
        s_y_mag = sem("y_mag")
        s_y_q = sem("y_q")
        s_y_qT = sem("y_qT")
        s_y_trans = sem("y_trans")
        s_z = sem("z")
        s_z_t = sem("z_t")
        s_z_trans = sem("z_trans")
        s_z_used = sem("z_used")
        s_zn = sem("zn")
        s_out = [sem("out_even"), sem("out_odd")]
        s_raw = {c: sem(f"raw_{c}") for c in "qkvob"}
        s_w_hi = {c: sem(f"w{c}_hi") for c in "qkvo"}
        s_w_lo = {c: sem(f"w{c}_lo") for c in "qkvo"}

        block = ctx.enter_context(nc.Block())

        def unless_last(n):
            return not isinstance(n, int) or n < STEPS

        def at(t):
            return slice(t, t + 1) if isinstance(t, int) else bass.ds(t, 1)

        def rows_of(m):
            t = m - H // 2
            return slice(t * FR, (t + 1) * FR) if isinstance(t, int) else bass.ds(t * FR, FR)

        g_trans_bank = pX1[:].bitcast(BF16)[:, NH:2 * NH]

        def later(n):
            return not isinstance(n, int) or n > 0

        @block.sync
        def _(sp):
            def load(c, n, head):
                if later(n):
                    sp.wait_ge(s_w_lo[c], n)
                src = {"q": wq, "k": wk, "v": wv, "o": wo}[c]
                sp.dma_start(w_raw[c][:], src[head]).then_inc(s_raw[c], 16)

            def load_bias(n, head):
                if later(n):
                    sp.wait_ge(s_b_mask, n)
                sp.dma_start(b_raw[:, 0, :], bias[head]).then_inc(s_raw["b"], 16)

            def load_rows(i, src, t):
                if later(i):
                    sp.wait_ge(s_g_mag, i)
                sp.dma_start(g_raw[0:FR, :], src[t]).then_inc(s_g_in, 16)

            sp.dma_start(lnw_col[:, :, 0], ln_w).then_inc(s_lnw_in, 16)
            for b in range(HB):
                sp.dma_start(xr[:, b, :], x[b]).then_inc(s_x_in, 16)
            for c in "qk":
                load(c, 0, 0)
            for kt in range(KT):
                sp.dma_start(cT_raw[:, kt * B * S:(kt + 1) * B * S], cT[kt]).then_inc(s_c_in, 16)
            sp.dma_start(mask_u8[:], mask).then_inc(s_mask_in, 16)
            load_bias(0, 0)
            load("v", 0, 0)
            load("o", 0, 0)
            for b in range(HB, B):
                sp.dma_start(xr[:, b, :], x[b]).then_inc(s_x_in, 16)
            for c in "qk":
                load(c, 1, 1)

            def loads(m, pair, rows=False):
                for odd in range(2):
                    n, head = 2 * m + odd, 2 * pair + odd
                    head1, head2 = head + 1, head + 2
                    if isinstance(head, int):
                        head1, head2 = head1 % H, head2 % H
                    if unless_last(n + 1):
                        load_bias(n + 1, head1)
                    if unless_last(n + 2):
                        load("q", n + 2, head2)
                        load("k", n + 2, head2)
                        if not odd:
                            load("v", m + 1, (pair + 1) % (H // 2) if isinstance(pair, int) else pair + 1)
                    if rows:
                        load_rows(n - H, w_up if odd else w_gate, m - H // 2)
                    if unless_last(n + 1):
                        load("o", n + 1, head1)

            with sp.Fori(0, H // 2 - 1) as m:
                loads(m, m)
            loads(H // 2 - 1, H // 2 - 1)
            sp.wait_ge(s_norm_done, H + 1)
            loads(H // 2, 0, rows=True)
            with sp.Fori(H // 2 + 1, PAIRS - 1) as m:
                loads(m, m - H // 2, rows=True)
            loads(PAIRS - 1, H // 2 - 1, rows=True)

            sp.wait_ge(s_x1_done, 2)
            sp.dma_start(taps[:], conv_w).then_inc(s_const_in, 16)
            sp.dma_start(gb[:, 0:1], gamma).then_inc(s_const_in, 16)
            sp.dma_start(gb[:, 1:2], beta).then_inc(s_const_in, 16)
            sp.dma_start(rb[:, 0, :], router_b).then_inc(s_const_in, 16)
            sp.dma_start(ra[:, :, 0:E], router_w).then_inc(s_const_in, 16)
            sp.dma_start(ra[:, :, E:E + ER], lora_a).then_inc(s_const_in, 16)
            sp.dma_start(lb[:], lora_b).then_inc(s_const_in, 16)
            for t in range(KT):
                if later(t):
                    sp.wait_ge(s_f_mag, t)
                sp.dma_start(f_raw[:], w_down[t * P:(t + 1) * P, :]).then_inc(s_f_in, 16)

            for t in range(B):
                sp.wait_ge(s_x4_done, t + 1)
                sp.dma_start(out[t], x4[:, t % 2, :]).then_inc(s_out[t % 2], 16)
            for done in s_out:
                sp.wait_ge(done, 16 * (B // 2))

        @block.gpsimd
        def _(pool):
            g = nc.gpsimd
            g.memset(ones[:], 1.0).then_inc(s_ones, 1)
            g.memset(neg_half[:], -0.5).then_inc(s_neg_half, 1)
            pool.wait_ge(s_ones, 1)
            g.affine_select(out=ident[:], in_=ones[:], compare_op=ALU.is_equal, fill=0.0, base=0,
                            pattern=[[-1, P]], channel_multiplier=1).then_inc(s_ident, 1)
            pool.wait_ge(s_ident, 1)
            g.tensor_copy(ident_b[:], ident[:]).then_inc(s_ident, 1)
            pool.wait_ge(s_neg_half, 1)

            def rsqrt(dst, src, n):
                pool.wait_ge(s_var_in, n + 1)
                g.tensor_tensor(dst, src, neg_half[:, 0:src.shape[-1]], ALU.pow).then_inc(s_rstd, 1)

            def lo(c, n):
                pool.wait_ge(s_w_hi[c], n + 1)
                g.tensor_tensor(w_lo[c][:], w_raw[c][:], w_hi[c][:].bitcast(F32),
                                ALU.subtract).then_inc(s_w_lo[c], 1)

            def bias_mask(n, half):
                pool.wait_ge(s_raw["b"], 16 * (n + 1))
                if later(n):
                    pool.wait_ge(s_scored, n)
                g.tensor_tensor(b_mask[:], b_raw[:].to_broadcast([P, HB, S]),
                                mask_add[:, half * HB:(half + 1) * HB, :], ALU.add).then_inc(s_b_mask, 1)

            lo("q", 0)
            lo("k", 0)
            rsqrt(rs[:], ve[:], 0)
            rsqrt(rs[:], ve[:], 1)

            def context_low(half):
                for kt in range(KT):
                    pool.wait_ge(s_cT_hi, half * KT + kt + 1)
                    g.tensor_tensor(cT_lo[half][:, kt, :],
                                    cT_raw[:, (2 * kt + half) * NH:(2 * kt + half + 1) * NH],
                                    cT_hi[half][:, kt, :].bitcast(F32), ALU.subtract).then_inc(s_cT_lo, 1)

            context_low(0)
            pool.wait_ge(s_mask_add, 1)
            bias_mask(0, 0)
            lo("v", 0)
            lo("q", 1)
            lo("k", 1)
            rsqrt(rs[:], ve[:], 2)
            rsqrt(rs[:], ve[:], 3)
            context_low(1)

            def pair(m, half):
                for odd in range(2):
                    n = 2 * m + odd
                    if unless_last(n + 1):
                        bias_mask(n + 1, (n + 1) // H if isinstance(n, int) else half)
                    if unless_last(n + 2):
                        lo("q", n + 2)
                        lo("k", n + 2)
                        if odd:
                            lo("v", m + 1)
                    lo("o", n)

            with pool.Fori(0, H // 2 - 1) as m:
                pair(m, 0)
            pair(H // 2 - 1, 0)
            with pool.Fori(H // 2, PAIRS - 1) as m:
                pair(m, 1)
            pair(PAIRS - 1, 1)

            pool.wait_ge(s_x1_done, 2)
            g.memset(diag[:], 1.0).then_inc(s_diag, 1)
            pool.wait_ge(s_diag, 1)
            g.affine_select(out=diag[:], in_=diag[:], compare_op=ALU.is_equal, fill=0.0, base=P + TAPS // 2,
                            pattern=[[-1, 3 * P + TAPS - 1]], channel_multiplier=1).then_inc(s_diag, 1)

            def up_product(t):
                pool.wait_ge(s_up_copy, t + 1)
                g.tensor_tensor(up[:], up[:], gu_row[:, INTER:2 * INTER], ALU.mult).then_inc(s_up, 1)

            one = rs1[:, 0:1], ve1[:, 0:1]
            rsqrt(*one, 4)
            rsqrt(*one, 5)
            up_product(0)
            with pool.Fori(1, B - 1) as t:
                rsqrt(*one, 2 * t + 4)
                rsqrt(*one, 2 * t + 5)
                up_product(t)
            rsqrt(*one, 2 * B + 2)
            up_product(B - 1)
            rsqrt(*one, 2 * B + 3)
            rsqrt(rs1[:], ve1[:], 2 * B + 4)
            with pool.Fori(0, B) as t:
                rsqrt(*one, t + 2 * B + 5)

        @block.scalar
        def _(act):
            a = nc.scalar

            def copy(dst, src):
                return a.activation(dst, src, ACT.Copy)

            def hi(c, n, used):
                act.wait_ge(s_raw[c], 16 * (n + 1))
                if later(n):
                    act.wait_ge(used, n)
                copy(w_hi[c][:], w_raw[c][:]).then_inc(s_w_hi[c], 1)

            def squares(half):
                for b in range(HB):
                    act.wait_ge(s_h_done, half * HB + b + 1)
                    act.drain()
                    a.activation(sq_junk[:], hid[:, b, :], ACT.Square,
                                 accum_out=ssq[:, b:b + 1]).then_inc(s_ssq, 1)

            def x_high(half):
                for b in range(HB):
                    t = half * HB + b
                    act.wait_ge(s_xw, t + 1)
                    copy(xT_hi[half][:, :, b * S:(b + 1) * S],
                         hid[:, b, :].rearrange("p (k s) -> p k s", k=KT)).then_inc(s_xT_hi, 1)

            hi("q", 0, s_q_proj)
            hi("k", 0, s_k_proj)
            squares(0)

            def context_high(half):
                for kt in range(KT):
                    act.wait_ge(s_c_in, 16 * KT)
                    copy(cT_hi[half][:, kt, :],
                         cT_raw[:, (2 * kt + half) * NH:(2 * kt + half + 1) * NH]).then_inc(s_cT_hi, 1)

            context_high(0)
            x_high(0)

            def query_high(n):
                act.wait_ge(s_q_proj, n + 1)
                copy(q_hi[:], pX0[:]).then_inc(s_q_hi, 1)

            def key_high(n):
                act.wait_ge(s_k_proj, n + 1)
                copy(k_hi[:], pX1[:]).then_inc(s_k_hi, 1)

            hi("v", 0, s_v_proj)
            query_high(0)
            hi("q", 1, s_q_proj)
            key_high(0)
            hi("k", 1, s_k_proj)
            squares(1)
            x_high(1)
            context_high(1)

            def pair(m, rows=False):
                for odd in range(2):
                    n = 2 * m + odd
                    act.wait_ge(s_max_done, n + 1)
                    if later(n):
                        act.wait_ge(s_p_trans, n)
                    for b in range(HB):
                        e = a.activation(prob[:, b, :], score[:, b, :], ACT.Exp,
                                         bias=neg_max[:, b:b + 1], accum_out=row_sum[:, b:b + 1])
                    e.then_inc(s_exp_done, 1)
                    if unless_last(n + 1):
                        query_high(n + 1)
                    if unless_last(n + 2):
                        hi("q", n + 2, s_q_proj)
                    if unless_last(n + 1):
                        key_high(n + 1)
                    if unless_last(n + 2):
                        hi("k", n + 2, s_k_proj)
                    if not odd:
                        for i, bank in enumerate((pX0, pX1)):
                            act.wait_ge(s_v_proj, n + i + 1)
                            copy(v_hi[:, 2 * i:2 * i + 2, :], bank[:]).then_inc(s_v_hi, 1)
                    act.wait_ge(s_p_trans, n + 1)
                    copy(pT_hi[:], pS[:]).then_inc(s_p_hi, 1)
                    if odd and unless_last(n + 2):
                        act.wait_ge(s_v_proj, n + 1)
                        hi("v", m + 1, s_v_proj)
                    if rows:
                        i = n - H
                        act.wait_ge(s_g_mag, i + 1)
                        if later(i):
                            act.wait_ge(s_g_trans, i)
                        a.activation(g_q[0:FR, :], g_mag[0:FR, :], ACT.Copy, bias=-MAGIC).then_inc(s_g_q, 1)
                    hi("o", n, s_o_done)
                    act.wait_ge(s_a_done, n + 1)
                    copy(aT_hi[:], pT[:]).then_inc(s_a_hi, 1)
                    if rows:
                        act.wait_ge(s_g_trans, i + 1)
                        copy(gu_row[:, odd * INTER:(odd + 1) * INTER][:, rows_of(m)], pX1[:, 0:FR])
                        copy(wguT[:, :, odd * INTER:(odd + 1) * INTER][:, :, rows_of(m)],
                             g_trans_bank[:, 0:KT * FR].rearrange("p (k r) -> p k r", k=KT)).then_inc(s_g_out, 1)

            pair(0)
            with act.Fori(1, H // 2) as m:
                pair(m)
            pair(H // 2, rows=True)
            with act.Fori(H // 2 + 1, PAIRS - 1) as m:
                pair(m, rows=True)
            pair(PAIRS - 1, rows=True)

            for t in range(KT):
                act.wait_ge(s_f_mag, t + 1)
                if later(t):
                    act.wait_ge(s_f_trans, t)
                a.activation(f_q[:], f_mag[:], ACT.Copy, bias=-MAGIC).then_inc(s_f_q, 1)
                act.wait_ge(s_f_trans, t + 1)
                src = pTb[:].rearrange("p (k s) -> p k s", s=P)
                copy(wdT[:, 0:IT - 1, t * P:(t + 1) * P], src[:, 0:IT - 1, :])
                copy(wdT[0:LAST, IT - 1, t * P:(t + 1) * P], src[0:LAST, IT - 1, :]).then_inc(s_f_out, 1)

            def token_ints(t):
                act.wait_ge(s_y_mag, t + 1)
                if later(t):
                    act.wait_ge(s_y_trans, t)
                a.activation(y_q[:], y_mag[:], ACT.Copy, bias=-MAGIC).then_inc(s_y_q, 1)
                act.wait_ge(s_y_trans, t + 1)
                if later(t):
                    act.wait_ge(s_u_proj, t)
                copy(y_qT[:], pYb[:, 0:KT * S]).then_inc(s_y_qT, 1)

            def keep_z(t):
                act.wait_ge(s_z_t, t + 1)
                copy(z[:, t, :], z_t[:]).then_inc(s_z, 1)

            def ffn_tile(t, more=True):
                act.wait_ge(s_gate, t + 1)
                if later(t):
                    act.wait_ge(s_h_mag, t)
                a.activation(silu[:], gate[:], ACT.Silu).then_inc(s_silu, 1)
                act.wait_ge(s_u_proj, t + 1)
                a.activation(up[:], pA[:, 0:INTER], ACT.Copy, scale=y_step[:, 0:1]).then_inc(s_up_copy, 1)
                if later(t):
                    keep_z(t - 1)
                if more:
                    token_ints(t + 1)
                act.wait_ge(s_h_mag, t + 1)
                if later(t):
                    act.wait_ge(s_h_trans, t)
                a.activation(h_q[:], h_mag[:], ACT.Copy, bias=-MAGIC).then_inc(s_h_q, 1)
                act.wait_ge(s_h_trans, t + 1)
                if later(t):
                    act.wait_ge(s_d_proj, t)
                copy(h_qT[:, 0:(IT - 1) * S], pTb[:, 0:(IT - 1) * S])
                copy(h_qT[0:LAST, (IT - 1) * S:IT * S], pTb[0:LAST, (IT - 1) * S:IT * S]).then_inc(s_h_qT, 1)

            token_ints(0)
            ffn_tile(0)
            with act.Fori(1, B - 1) as t:
                ffn_tile(t)
            ffn_tile(B - 1, more=False)
            keep_z(B - 1)

            act.wait_ge(s_zn, 1)
            a.activation(cz[:], cz2[:], ACT.Tanh, scale=0.5).then_inc(s_sig, 1)
            act.wait_ge(s_dA, 1)

            def weights_of(t):
                if later(t):
                    act.wait_ge(s_c_trans, t)
                for lt in range(KT):
                    last = a.activation(coef[:, lt, :], top[:, lt, t, :], ACT.Identity,
                                        scale=dA[:, lt, at(t)], bias=cz[:, lt, 1, at(t)])
                last.then_inc(s_coef, 1)

            def route_tile(t, more=True):
                if more:
                    weights_of(t + 1)
                act.wait_ge(s_f_t, t + 1)
                copy(fT[:], pD[:]).then_inc(s_fT, 1)
                act.wait_ge(s_r_proj, t + 1)
                copy(rh[:, t, :], pA[:, 0:E + ER]).then_inc(s_rh, 1)

            weights_of(0)
            with act.Fori(0, B - 1) as t:
                route_tile(t)
            route_tile(B - 1, more=False)

            act.wait_ge(s_top_logit, 1)
            a.activation(prb[:, :, 0:E], logit[:], ACT.Exp).then_inc(s_r_exp, 1)
            for t in range(B):
                act.wait_ge(s_hw_t, t + 1)
                if later(t - 1):
                    act.wait_ge(s_l_proj, t - 1)
                copy(hwT[:, t % 2, :], pA[:, (t % 2) * 512:(t % 2) * 512 + S]).then_inc(s_hwT, 1)

        @block.vector
        def _(dve):
            v = nc.vector

            v.memset(stats[:], 0.0)
            dve.wait_ge(s_mask_in, 16)
            dve.drain()
            v.tensor_scalar(mask_add[:], mask_u8[:], -1.0, -MASKED, ALU.add, ALU.mult)
            v.tensor_reduce(row_any[:], mask_u8[:], AX.X, ALU.max).then_inc(s_mask_add, 1)

            def token_prologue(half):
                tiles = range(half * HB, (half + 1) * HB)
                dve.drain()
                for b, t in enumerate(tiles):
                    dve.wait_ge(s_x_in, 16 * (t + 1))
                    v.bn_stats(stats[:, b, :], xr[:, t, :])
                dve.drain()
                for b in range(HB):
                    v.bn_aggr(mv[:, b, :], stats[:, b, :])
                dve.drain()
                v.tensor_scalar(ve[:], mv[:, :, 1], EPS, None, ALU.add).then_inc(s_var_in, 1)
                dve.wait_ge(s_rstd, 2 * half + 1)
                for b, t in enumerate(tiles):
                    v.tensor_scalar(hid[:, b, :], xr[:, t, :], mv[:, b, 0:1], rs[:, b:b + 1],
                                    ALU.subtract, ALU.mult).then_inc(s_h_done, 1)
                dve.drain()
                for b, t in enumerate(tiles):
                    v.tensor_tensor(xr[:, t, :], xr[:, t, :], hid[:, b, :], ALU.add)
                dve.wait_ge(s_ssq, (half + 1) * HB)
                v.tensor_scalar(ve[:], ssq[:], 1.0 / D, EPS, ALU.mult, ALU.add).then_inc(s_var_in, 1)
                dve.wait_ge(s_rstd, 2 * half + 2)
                dve.drain()
                for b in range(HB):
                    v.tensor_scalar(hid[:, b, :], hid[:, b, :], rs[:, b:b + 1], None,
                                    ALU.mult).then_inc(s_xn, 1)
                dve.wait_ge(s_lnw_in, 16)
                for b, t in enumerate(tiles):
                    dve.wait_ge(s_x_trans, t + 1)
                    v.tensor_tensor(hid[:, b, :].rearrange("p (k s) -> p k s", k=KT),
                                    oacc[b][:].rearrange("p (k s) -> p k s", k=KT),
                                    lnw_col[:].to_broadcast([P, KT, S]), ALU.mult).then_inc(s_xw, 1)
                for b, t in enumerate(tiles):
                    dve.wait_ge(s_xT_hi, t + 1)
                    cols = slice(b * S, (b + 1) * S)
                    v.tensor_tensor(xT_lo[half][:, :, cols], hid[:, b, :].rearrange("p (k s) -> p k s", k=KT),
                                    xT_hi[half][:, :, cols].bitcast(F32), ALU.subtract).then_inc(s_xT_lo, 1)

            def query_low(n):
                dve.wait_ge(s_q_hi, n + 1)
                v.tensor_tensor(q_lo[:], pX0[:], q_hi[:].bitcast(F32), ALU.subtract).then_inc(s_q_lo, 1)

            def key_low(n):
                dve.wait_ge(s_k_hi, n + 1)
                v.tensor_tensor(k_lo[:], pX1[:], k_hi[:].bitcast(F32), ALU.subtract).then_inc(s_k_lo, 1)

            token_prologue(0)
            query_low(0)
            key_low(0)
            token_prologue(1)

            def pick_round(last=False):
                dve.drain()
                for r in range(2):
                    v.max(pick8[:, r, :], pick[:, r, :])
                dve.drain()
                if last and REST % 8:
                    v.memset(pick8[:, :, REST % 8:8], LOWEST)
                    dve.drain()
                for r in range(2):
                    v.match_replace(pick[:, r, :], pick8[:, r, :], pick[:, r, :], LOWEST)

            def residual(half):
                dve.wait_ge(s_o_done, (half + 1) * H)
                for b in range(HB):
                    t = half * HB + b
                    last = v.tensor_tensor(xr[:, t, :], oacc[b][:], xr[:, t, :], ALU.add)
                last.then_inc(s_x1_done, 1)

            def pair(m, half, picks=False, rows=False):
                for odd in range(2):
                    n = 2 * m + odd
                    dve.wait_ge(s_b_mask, n + 1)
                    dve.wait_ge(s_s_done, n + 1)
                    v.tensor_tensor(score[:], pS[:].rearrange("p (b s) -> p b s", b=HB), b_mask[:],
                                    ALU.add).then_inc(s_scored, 1)
                    dve.drain()
                    v.tensor_reduce(neg_max[:], score[:], AX.X, ALU.max, negate=True).then_inc(s_max_done, 1)
                    if picks and not odd:
                        dve.drain()
                        for r in range(2):
                            v.tensor_scalar(pick[:, r, ::-1], cT_raw[:, bass.ds((2 * m + r) * S, S)], -1.0, None,
                                            ALU.mult)
                    if picks:
                        pick_round()
                    dve.wait_ge(s_exp_done, n + 1)
                    v.reciprocal(row_inv[:, :, 0], row_sum[:])
                    dve.drain()
                    v.tensor_tensor(row_inv[:, :, 0], row_inv[:, :, 0], row_any[:, half * HB:(half + 1) * HB],
                                    ALU.mult)
                    dve.drain()
                    v.tensor_tensor(prob[:], prob[:], row_inv[:].to_broadcast([P, HB, S]),
                                    ALU.mult).then_inc(s_norm_done, 1)
                    if unless_last(n + 1):
                        query_low(n + 1)
                    if picks:
                        pick_round()
                    if unless_last(n + 1):
                        key_low(n + 1)
                    if not odd:
                        if picks:
                            pick_round()
                        for i, bank in enumerate((pX0, pX1)):
                            dve.wait_ge(s_v_hi, n + i + 1)
                            v.tensor_tensor(v_lo[:, 2 * i:2 * i + 2, :], bank[:].rearrange("p (b d) -> p b d", b=2),
                                            v_hi[:, 2 * i:2 * i + 2, :].bitcast(F32), ALU.subtract).then_inc(s_v_lo, 1)
                            if picks and not i:
                                pick_round()
                    dve.wait_ge(s_p_hi, n + 1)
                    v.tensor_tensor(pT_lo[:], pS[:], pT_hi[:].bitcast(F32), ALU.subtract).then_inc(s_p_lo, 1)
                    if picks and odd:
                        pick_round(last=True)
                        dve.drain()
                        for r in range(2):
                            v.tensor_scalar(top_flat[:, bass.ds((2 * m + r) * S, S)], pick[:, r, ::-1], LOWEST, None,
                                            ALU.not_equal)
                    if rows:
                        i = n - H
                        dve.drain()
                        dve.wait_ge(s_g_in, 16 * (i + 1))
                        v.tensor_reduce(f_s[0:FR, 0:1], g_raw[0:FR, :], AX.X, ALU.max, apply_absolute_value=True)
                        dve.drain()
                        v.tensor_scalar(f_s[0:FR, 1:2], f_s[0:FR, 0:1], 1.0 / QMAX, 1e-8, ALU.mult, ALU.max)
                        dve.drain()
                        v.reciprocal(f_s[0:FR, 2:3], f_s[0:FR, 1:2])
                        if later(i):
                            dve.wait_ge(s_g_trans, i)
                        v.tensor_scalar(f_diag[0:FR, 0:FR], ident[0:FR, 0:FR], f_s[0:FR, 1:2], None,
                                        ALU.mult).then_inc(s_g_diag, 1)
                        dve.drain()
                        if later(i):
                            dve.wait_ge(s_g_q, i)
                        v.tensor_scalar(g_mag[0:FR, :], g_raw[0:FR, :], f_s[0:FR, 2:3], MAGIC,
                                        ALU.mult, ALU.add).then_inc(s_g_mag, 1)
                    dve.wait_ge(s_a_hi, n + 1)
                    v.tensor_tensor(aT_lo[:], pT[:], aT_hi[:].bitcast(F32), ALU.subtract).then_inc(s_a_lo, 1)
                    if isinstance(n, int) and n == H:
                        residual(0)

            with dve.Fori(0, H // 2) as m:
                pair(m, 0, picks=True)
            pair(H // 2, 1, rows=True)
            with dve.Fori(H // 2 + 1, PAIRS - 1) as m:
                pair(m, 1, rows=True)
            pair(PAIRS - 1, 1, rows=True)
            residual(1)

            for t in range(KT):
                dve.wait_ge(s_f_in, 16 * (t + 1))
                dve.drain()
                v.tensor_reduce(f_s[:, 0:1], f_raw[:], AX.X, ALU.max, apply_absolute_value=True)
                dve.drain()
                v.tensor_scalar(f_s[:, 1:2], f_s[:, 0:1], 1.0 / QMAX, 1e-8, ALU.mult, ALU.max)
                dve.drain()
                v.reciprocal(f_s[:, 2:3], f_s[:, 1:2])
                if later(t):
                    dve.wait_ge(s_f_trans, t)
                v.tensor_scalar(f_diag[:], ident[:], f_s[:, 1:2], None, ALU.mult).then_inc(s_f_diag, 1)
                dve.drain()
                if later(t):
                    dve.wait_ge(s_f_q, t)
                v.tensor_scalar(f_mag[:], f_raw[:], f_s[:, 2:3], MAGIC, ALU.mult, ALU.add).then_inc(s_f_mag, 1)
                dve.wait_ge(s_f_trans, t + 1)
                v.tensor_copy(sd_row[:, t * P:(t + 1) * P], pD[:, 0:P]).then_inc(s_f_row, 1)

            dve.wait_ge(s_diag, 2)
            dve.wait_ge(s_const_in, 16 * 7)
            for c in range(2):
                v.tensor_scalar(band[c][:], diag[:, 0:3 * P], taps[:, c * TAPS:c * TAPS + 1], None, ALU.mult)
                for j in range(1, TAPS):
                    dve.drain()
                    v.scalar_tensor_tensor(out=band[c][:], in0=diag[:, j:j + 3 * P],
                                           scalar=taps[:, c * TAPS + j:c * TAPS + j + 1], in1=band[c][:],
                                           op0=ALU.mult, op1=ALU.add)
            dve.drain()
            v.memset(prb[:, :, E:2 * E], -1.0).then_inc(s_band, 1)

            def layernorm(dst, src, n, tile=None):
                dve.drain()
                v.bn_stats(st6[:], src)
                dve.drain()
                v.bn_aggr(mv1[:], st6[:])
                dve.drain()
                v.tensor_scalar(ve1[:, 0:1], mv1[:, 1:2], EPS, None, ALU.add).then_inc(s_var_in, 1)
                dve.wait_ge(s_rstd, n + 1)
                if tile is not None and later(tile):
                    dve.wait_ge(s_z, tile)
                    dve.wait_ge(s_z_trans, tile)
                return v.tensor_scalar(dst, src, mv1[:, 0:1], rs1[:, 0:1], ALU.subtract, ALU.mult)

            def scale_of(tile, s):
                dve.drain()
                v.tensor_reduce(s[:, 0:1], tile, AX.X, ALU.max, apply_absolute_value=True)
                dve.drain()
                v.tensor_scalar(s[:, 1:2], s[:, 0:1], 1.0 / QMAX, 1e-8, ALU.mult, ALU.max)
                dve.drain()
                v.reciprocal(s[:, 2:3], s[:, 1:2])
                dve.drain()

            def token_scale(t, n):
                layernorm(y[:], xr[:, t, :], n)
                scale_of(y[:], y_s)
                if later(t):
                    dve.wait_ge(s_y_q, t)
                v.tensor_scalar(y_mag[:], y[:], y_s[:, 2:3], MAGIC, ALU.mult, ALU.add).then_inc(s_y_mag, 1)

            def residual_norm(t, n):
                dve.wait_ge(s_d_proj, t + 1)
                v.scalar_tensor_tensor(out=down[:], in0=pD[:], scalar=h_s[:, 1:2], in1=sd_row[:],
                                       op0=ALU.mult, op1=ALU.mult).then_inc(s_d_used, 1)
                dve.drain()
                v.tensor_tensor(xr[:, t, :], xr[:, t, :], down[:], ALU.add)
                layernorm(z_t[:], xr[:, t, :], n, tile=t).then_inc(s_z_t, 1)

            def channel_stats(t):
                dve.wait_ge(s_z_trans, t + 1)
                zT = pZ[:].rearrange("p (k s) -> p k s", k=KT)
                v.tensor_tensor(cf[:], zT, top[:, :, t, :], ALU.mult)
                dve.drain()
                v.tensor_tensor(sf[:], zT, cf[:], ALU.subtract).then_inc(s_z_used, 1)
                dve.drain()
                for br, part in enumerate((cf, sf)):
                    v.tensor_reduce(stat[0][:, :, br, at(t)], part[:], AX.X, ALU.max)
                    v.tensor_reduce(stat[1][:, :, br, at(t)], part[:], AX.X, ALU.add)

            def ffn_tile(t, before=None, after=None):
                dve.drain()
                if later(t):
                    dve.wait_ge(s_up_copy, t)
                v.tensor_copy(y_step[:], y_s[:, 1:2])
                dve.drain()
                dve.wait_ge(s_g_proj, t + 1)
                if later(t):
                    dve.wait_ge(s_silu, t)
                v.scalar_tensor_tensor(out=gate[:], in0=pA[:, 0:INTER], scalar=y_step[:, 0:1], in1=gu_row[:, 0:INTER],
                                       op0=ALU.mult, op1=ALU.mult).then_inc(s_gate, 1)
                if before is not None:
                    residual_norm(t - 1, before)
                if after is not None:
                    token_scale(t + 1, after)
                if before is not None:
                    channel_stats(t - 1)
                dve.wait_ge(s_silu, t + 1)
                dve.wait_ge(s_up, t + 1)
                v.tensor_tensor(silu[:], silu[:], up[:], ALU.mult)
                scale_of(silu[:], h_s)
                if later(t):
                    dve.wait_ge(s_h_q, t)
                v.tensor_scalar(h_mag[:], silu[:], h_s[:, 2:3], MAGIC, ALU.mult, ALU.add).then_inc(s_h_mag, 1)

            token_scale(0, 4)
            ffn_tile(0, after=5)
            with dve.Fori(1, B - 1) as t:
                ffn_tile(t, before=2 * t + 4, after=2 * t + 5)
            ffn_tile(B - 1, before=2 * B + 2)
            residual_norm(B - 1, 2 * B + 3)
            channel_stats(B - 1)

            dve.drain()
            for br, n in enumerate((CRUCIAL, REST)):
                v.tensor_scalar(stat[1][:, :, br, :], stat[1][:, :, br, :], 1.0 / S, S / n,
                                ALU.mult, ALU.mult).then_inc(s_stats, 1)
            dve.wait_ge(s_conv, 1)
            conv = pA[:, 0:KT * 2 * B].rearrange("p (k r b) -> p k r b", k=KT, r=2)
            v.tensor_copy(cz[:], conv)
            dve.drain()
            v.tensor_reduce(csum[:], cz[:].rearrange("p k r b -> p r k b"), AX.XY, ALU.add).then_inc(s_csum, 1)
            dve.wait_ge(s_ctotal, 1)
            v.tensor_scalar(cmu[:], pA[:, 512:514], 1.0 / (B * D), None, ALU.mult)
            dve.drain()
            for br in range(2):
                v.tensor_scalar(cz[:, :, br, :], cz[:, :, br, :], cmu[:, br:br + 1], None, ALU.subtract)
            dve.drain()
            v.tensor_tensor(cz2[:], cz[:], cz[:], ALU.mult)
            dve.drain()
            v.tensor_reduce(csum[:], cz2[:].rearrange("p k r b -> p r k b"), AX.XY, ALU.add).then_inc(s_csum, 1)
            dve.wait_ge(s_ctotal, 2)
            v.tensor_scalar(ve1[:], pA[:, 1024:1026], 1.0 / (B * D), EPS, ALU.mult, ALU.add).then_inc(s_var_in, 1)
            dve.wait_ge(s_rstd, 2 * B + 5)
            for br in range(2):
                v.tensor_scalar(cz2[:, :, br, :], cz[:, :, br, :], rs1[:, br:br + 1], gb[:, 0:1],
                                ALU.mult, ALU.mult)
            dve.drain()
            v.tensor_scalar(cz2[:], cz2[:], gb[:, 1:2], 0.0, ALU.add, ALU.max).then_inc(s_zn, 1)
            dve.wait_ge(s_sig, 1)
            v.tensor_scalar(cz[:], cz[:], 0.5, 0.5, ALU.mult, ALU.add)
            dve.drain()
            v.tensor_tensor(dA[:], cz[:, :, 0, :], cz[:, :, 1, :], ALU.subtract).then_inc(s_dA, 1)

            def route_tile(t):
                dve.wait_ge(s_c_trans, t + 1)
                v.tensor_tensor(down[:], pZ[:], z[:, t, :], ALU.mult).then_inc(s_c_used, 1)
                dve.drain()
                v.tensor_tensor(xr[:, t, :], down[:], xr[:, t, :], ALU.add)
                dve.drain()
                v.bn_stats(st6[:], xr[:, t, :])
                dve.drain()
                v.bn_aggr(mv1[:], st6[:])
                dve.drain()
                v.tensor_scalar(ve1[:, 0:1], mv1[:, 1:2], EPS, None, ALU.add).then_inc(s_var_in, 1)
                dve.wait_ge(s_rstd, t + 2 * B + 6)
                if later(t):
                    dve.wait_ge(s_f_t, t)
                v.tensor_scalar(f[:], xr[:, t, :], mv1[:, 0:1], rs1[:, 0:1],
                                ALU.subtract, ALU.mult).then_inc(s_f, 1)

            route_tile(0)
            with dve.Fori(1, B) as t:
                route_tile(t)

            dve.wait_ge(s_rh, B)
            v.tensor_tensor(logit[:], rh[:, :, 0:E], rb[:].to_broadcast([P, B, E]), ALU.add)
            dve.drain()
            v.tensor_reduce(r_max[:, :, 0], logit[:], AX.X, ALU.max)
            dve.drain()
            v.tensor_tensor(logit[:], logit[:], r_max[:].to_broadcast([P, B, E]),
                            ALU.subtract).then_inc(s_top_logit, 1)
            dve.wait_ge(s_r_exp, 1)
            v.tensor_reduce(r_max[:, :, 0], prb[:, :, 0:E], AX.X, ALU.add)
            dve.drain()
            v.reciprocal(r_inv[:, :, 0], r_max[:, :, 0])
            dve.drain()
            v.tensor_tensor(prb[:, :, 0:E], prb[:, :, 0:E], r_inv[:].to_broadcast([P, B, E]), ALU.mult)
            dve.drain()
            for t in range(B):
                v.max(best[:, t, :], prb[:, t, :])
            dve.drain()
            v.tensor_tensor(r_max[:, :, 0], best[:, :, 0], best[:, :, 1], ALU.add)
            v.memset(best[:, :, 2:8], -1.0)
            dve.drain()
            for t in range(B):
                v.match_replace(prw[:, t, :], best[:, t, :], prb[:, t, :], -2.0)
            v.reciprocal(r_inv[:, :, 0], r_max[:, :, 0])
            dve.drain()
            v.scalar_tensor_tensor(out=wexp[:, :, :, 0], in0=prw[:, :, 0:E], scalar=-2.0, in1=prb[:, :, 0:E],
                                   op0=ALU.is_equal, op1=ALU.mult)
            dve.drain()
            v.tensor_tensor(wexp[:, :, :, 0], wexp[:, :, :, 0], r_inv[:].to_broadcast([P, B, E]), ALU.mult)
            dve.drain()
            for t in range(B):
                v.tensor_tensor(hw[:, t, :, :], rh[:, t, E:E + ER].rearrange("p (e r) -> p e r", e=E),
                                wexp[:, t, :, :].to_broadcast([P, E, R]), ALU.mult).then_inc(s_hw, 1)
            for t in range(B):
                dve.wait_ge(s_l_proj, t + 1)
                if t >= 2:
                    dve.wait_ge(s_out[t % 2], 16 * (t // 2))
                v.scalar_tensor_tensor(out=x4[:, t % 2, :], in0=(pD, pZ)[t % 2][:], scalar=8.0 / R,
                                       in1=xr[:, t, :], op0=ALU.mult, op1=ALU.add).then_inc(s_x4_done, 1)

        @block.tensor
        def _(pe):
            mm = nc.tensor.matmul

            def three(dst, left, right, start=True, stop=True, lint=False):
                (lh, ll), (rh, rl) = left, right
                mm(dst, lh, rl, start=start, stop=False, skip_group_check=lint)
                mm(dst, ll, rh, start=False, stop=False, skip_group_check=lint)
                return mm(dst, lh, rh, start=False, stop=stop, skip_group_check=lint)

            def tr(dst, src, ident):
                return mm(dst, src, ident, is_transpose=True, start=True, stop=True)

            pe.wait_ge(s_ident, 2)
            def x_transposes(half):
                for b in range(HB):
                    t = half * HB + b
                    pe.wait_ge(s_xn, t + 1)
                    bank = oacc[b]
                    for kt in range(KT):
                        last = tr(bank[:, kt * S:(kt + 1) * S], hid[:, b, kt * P:(kt + 1) * P], ident[:])
                    last.then_inc(s_x_trans, 1)

            x_transposes(0)

            def project(dst, c, src, half):
                for kt in range(KT):
                    w = tuple(w[c][:, kt * P:(kt + 1) * P] for w in (w_hi, w_lo))
                    last = three(dst, w, tuple(s[half][:, kt, :] for s in src), start=kt == 0, stop=kt == KT - 1)
                return last

            def queries(n, half):
                pe.wait_ge(s_w_lo["q"], n + 1)
                project(pX0[:], "q", (xT_hi, xT_lo), half).then_inc(s_q_proj, 1)

            def keys(n, half):
                pe.wait_ge(s_w_lo["k"], n + 1)
                project(pX1[:], "k", (cT_hi, cT_lo), half).then_inc(s_k_proj, 1)

            def values(bank, batches, half):
                for i, b in enumerate(batches):
                    for kt in range(KT):
                        c = tuple(t[half][:, kt, b * S:(b + 1) * S] for t in (cT_hi, cT_lo))
                        w = tuple(w["v"][:, kt * 2 * DH:(kt + 1) * 2 * DH] for w in (w_hi, w_lo))
                        last = three(bank[:, i * 2 * DH:(i + 1) * 2 * DH], c, w, start=kt == 0, stop=kt == KT - 1)
                last.then_inc(s_v_proj, 1)

            def outputs(n, start=False):
                pe.wait_ge(s_a_lo, n + 1)
                pe.wait_ge(s_w_lo["o"], n + 1)
                for b in range(HB):
                    cols = slice(b * S, (b + 1) * S)
                    last = three(oacc[b][:], (aT_hi[:, cols], aT_lo[:, cols]), (w_hi["o"][:], w_lo["o"][:]),
                                 start=start, stop=False, lint=True)
                last.then_inc(s_o_done, 1)

            def pair(m, half, rows=False):
                for odd in range(2):
                    n = 2 * m + odd
                    pe.wait_ge(s_q_lo, n + 1)
                    pe.wait_ge(s_k_lo, n + 1)
                    if later(n):
                        pe.wait_ge(s_p_lo, n)
                    for b in range(HB):
                        cols = slice(b * S, (b + 1) * S)
                        last = three(pS[:, cols], (q_hi[:, cols], q_lo[:, cols]), (k_hi[:, cols], k_lo[:, cols]))
                    last.then_inc(s_s_done, 1)
                    if unless_last(n + 1):
                        next_half = (n + 1) // H if isinstance(n, int) else half
                        if isinstance(n, int) and n + 1 == H:
                            pe.wait_ge(s_xT_lo, B)
                            pe.wait_ge(s_cT_lo, 2 * KT)
                        if odd:
                            pe.wait_ge(s_v_lo, n)
                        queries(n + 1, next_half)
                        if odd:
                            pe.wait_ge(s_v_lo, n + 1)
                        if rows and not (isinstance(n, int) and n == H):
                            pe.wait_ge(s_g_out, n - H)
                        keys(n + 1, next_half)
                    if not odd:
                        pe.wait_ge(s_w_lo["v"], m + 1)
                        pe.wait_ge(s_q_lo, n + 2)
                        values(pX0, (0, 1), half)
                        pe.wait_ge(s_k_lo, n + 2)
                        values(pX1, (2, 3), half)
                    pe.wait_ge(s_norm_done, n + 1)
                    for b in range(HB):
                        last = tr(pS[:, b * S:(b + 1) * S], prob[:, b, :], ident[:])
                    last.then_inc(s_p_trans, 1)
                    if later(n):
                        if isinstance(n, int) and n == H + 1:
                            pe.wait_ge(s_x1_done, 1)
                        outputs(n - 1, start=isinstance(n, int) and n % H == 1)
                    pe.wait_ge(s_p_lo, n + 1)
                    pe.wait_ge(s_v_lo, 2 * m + 2)
                    for b in range(HB):
                        cols = slice(b * S, (b + 1) * S)
                        heads = slice(odd * DH, (odd + 1) * DH)
                        last = three(pT[:, cols], (v_hi[:, b, heads], v_lo[:, b, heads]),
                                     (pT_hi[:, cols], pT_lo[:, cols]))
                    last.then_inc(s_a_done, 1)
                    if rows:
                        pe.wait_ge(s_g_diag, n - H + 1)
                        if isinstance(n, int) and n + 1 == STEPS:
                            pe.wait_ge(s_g_out, n - H)
                        else:
                            pe.wait_ge(s_k_lo, n + 2)
                        mm(pX1[:, 0:FR], ones[0:FR, :], f_diag[0:FR, 0:FR], start=True, stop=True)
                        pe.wait_ge(s_g_q, n - H + 1)
                        for kt in range(KT):
                            last = tr(g_trans_bank[:, kt * FR:(kt + 1) * FR], g_q[0:FR, kt * P:(kt + 1) * P],
                                      ident_b[0:FR, 0:FR])
                        last.then_inc(s_g_trans, 1)

            pe.wait_ge(s_xT_lo, HB)
            queries(0, 0)
            pe.wait_ge(s_cT_lo, KT)
            keys(0, 0)
            x_transposes(1)
            pair(0, 0)
            with pe.Fori(1, H // 2 - 1) as m:
                pair(m, 0)
            pair(H // 2 - 1, 0)
            pair(H // 2, 1, rows=True)
            with pe.Fori(H // 2 + 1, PAIRS - 1) as m:
                pair(m, 1, rows=True)
            pair(PAIRS - 1, 1, rows=True)
            outputs(STEPS - 1)

            pe.wait_ge(s_x1_done, 2)
            pe.wait_ge(s_g_out, H)
            for t in range(KT):
                pe.wait_ge(s_f_diag, t + 1)
                if later(t):
                    pe.wait_ge(s_f_row, t)
                mm(pD[:, 0:P], ones[:], f_diag[:], start=True, stop=True)
                pe.wait_ge(s_f_q, t + 1)
                if later(t):
                    pe.wait_ge(s_f_out, t)
                for k in range(IT):
                    cols = min(P, INTER - k * P)
                    last = tr(pTb[0:cols, k * P:(k + 1) * P], f_q[:, k * P:k * P + cols], ident_b[:])
                last.then_inc(s_f_trans, 1)
            pe.wait_ge(s_f_out, KT)
            pe.wait_ge(s_f_row, KT)

            def token_transposes(t):
                pe.wait_ge(s_y_q, t + 1)
                if later(t):
                    pe.wait_ge(s_y_qT, t)
                for kt in range(KT):
                    last = tr(pYb[:, kt * S:(kt + 1) * S], y_q[:, kt * P:(kt + 1) * P], ident_b[:])
                last.then_inc(s_y_trans, 1)

            def z_transposes(t):
                pe.wait_ge(s_z_t, t + 1)
                if later(t):
                    pe.wait_ge(s_z_used, t)
                for kt in range(KT):
                    last = tr(pZ[:, kt * S:(kt + 1) * S], z_t[:, kt * P:(kt + 1) * P], ident[:])
                last.then_inc(s_z_trans, 1)

            def inner(start):
                for c0 in range(0, INTER, 512):
                    c1 = min(c0 + 512, INTER)
                    for kt in range(KT):
                        last = mm(pA[:, c0:c1], y_qT[:, kt * S:(kt + 1) * S], wguT[:, kt, start + c0:start + c1],
                                  start=kt == 0, stop=kt == KT - 1)
                return last

            def gate_product(t):
                pe.wait_ge(s_y_qT, t + 1)
                if later(t):
                    pe.wait_ge(s_up_copy, t)
                inner(0).then_inc(s_g_proj, 1)

            def ffn_tile(t, more=True):
                pe.wait_ge(s_gate, t + 1)
                inner(INTER).then_inc(s_u_proj, 1)
                if later(t):
                    z_transposes(t - 1)
                if more:
                    token_transposes(t + 1)
                    gate_product(t + 1)
                pe.wait_ge(s_h_q, t + 1)
                if later(t):
                    pe.wait_ge(s_h_qT, t)
                for k in range(IT):
                    cols = min(P, INTER - k * P)
                    last = tr(pTb[0:cols, k * S:(k + 1) * S], h_q[:, k * P:k * P + cols], ident_b[:])
                last.then_inc(s_h_trans, 1)
                pe.wait_ge(s_h_qT, t + 1)
                if later(t):
                    pe.wait_ge(s_d_used, t)
                for k in range(IT):
                    rows = min(P, INTER - k * P)
                    last = mm(pD[:], h_qT[0:rows, k * S:(k + 1) * S], wdT[0:rows, k, :],
                              start=k == 0, stop=k == IT - 1)
                last.then_inc(s_d_proj, 1)

            token_transposes(0)
            gate_product(0)
            ffn_tile(0)
            ffn_tile(1)
            with pe.Fori(2, B - 1) as t:
                ffn_tile(t)
            ffn_tile(B - 1, more=False)
            z_transposes(B - 1)

            pe.wait_ge(s_stats, 2)
            pe.wait_ge(s_band, 1)
            for lt in range(KT):
                terms = [(c, d) for c in range(2) for d in (-1, 0, 1) if 0 <= lt + d < KT]
                for i, (c, d) in enumerate(terms):
                    last = mm(pA[:, lt * 2 * B:(lt + 1) * 2 * B], band[c][:, (1 - d) * P:(2 - d) * P],
                              stat[c][:, lt + d, :, :], start=i == 0, stop=i == len(terms) - 1)
            last.then_inc(s_conv, 1)
            for i in range(2):
                pe.wait_ge(s_csum, i + 1)
                mm(pA[:, 512 * (i + 1):512 * (i + 1) + 2], ones[:], csum[:], start=True, stop=True)\
                    .then_inc(s_ctotal, 1)

            def coef_transposes(t):
                pe.wait_ge(s_coef, t + 1)
                if later(t):
                    pe.wait_ge(s_c_used, t)
                for kt in range(KT):
                    last = tr(pZ[:, kt * P:(kt + 1) * P], coef[:, kt, :], ident[:])
                last.then_inc(s_c_trans, 1)

            def route_tile(t, more=True):
                if more:
                    coef_transposes(t + 1)
                pe.wait_ge(s_f, t + 1)
                for kt in range(KT):
                    last = tr(pD[:, kt * S:(kt + 1) * S], f[:, kt * P:(kt + 1) * P], ident[:])
                last.then_inc(s_f_t, 1)
                pe.wait_ge(s_fT, t + 1)
                if later(t):
                    pe.wait_ge(s_rh, t)
                for kt in range(KT):
                    last = mm(pA[:, 0:E + ER], fT[:, kt * S:(kt + 1) * S], ra[:, kt, :],
                              start=kt == 0, stop=kt == KT - 1)
                last.then_inc(s_r_proj, 1)

            coef_transposes(0)
            route_tile(0)
            with pe.Fori(1, B - 1) as t:
                route_tile(t)
            route_tile(B - 1, more=False)

            def hidden_transpose(t):
                pe.wait_ge(s_hw, t + 1)
                if t >= 2:
                    pe.wait_ge(s_hwT, t - 1)
                tr(pA[:, (t % 2) * 512:(t % 2) * 512 + S], hw[:, t, :, :], ident[:]).then_inc(s_hw_t, 1)

            pe.wait_ge(s_rh, B)
            hidden_transpose(0)
            for t in range(B):
                if t + 1 < B:
                    hidden_transpose(t + 1)
                pe.wait_ge(s_hwT, t + 1)
                if t >= 2:
                    pe.wait_ge(s_x4_done, t - 1)
                mm((pD, pZ)[t % 2][:], hwT[:, t % 2, :], lb[:], start=True, stop=True).then_inc(s_l_proj, 1)


def kernel(**inputs):
    import concourse.bacc as bacc
    from concourse.bass_utils import run_bass_kernel_spmd

    def host(name):
        return np.asarray(inputs[name])

    def tile_rows(w):
        return w.T.reshape(KT, P, -1).transpose(1, 0, 2)

    def per_head(w):
        return w.reshape(H, DH, KT, P).transpose(0, 3, 2, 1).reshape(H, P, KT * DH)

    def rows(v):
        return np.broadcast_to(v.reshape(1, -1), (P, v.size))

    arrays = {
        "x": host("x"),
        "cT": host("ctx_4096").reshape(B * S, D).T.reshape(KT, P, B * S),
        "mask": host("mask_BxSxS2_bk0").transpose(1, 0, 2),
        "bias": host("L0_xattn_position_bias"),
        "ln_w": host("L0_xattn_ln_weight").reshape(KT, P).T,
        "wq": per_head(host("L0_xattn_w_q")),
        "wk": per_head(host("L0_xattn_w_k")),
        "wv": per_head(host("L0_xattn_w_v")).reshape(H // 2, 2, P, KT, DH).transpose(0, 2, 3, 1, 4)
        .reshape(H // 2, P, KT * 2 * DH),
        "wo": host("L0_xattn_w_out").reshape(D, H, DH).transpose(1, 2, 0),
        "w_gate": host("L0_ffn_w_gate").reshape(H // 2, FR, D),
        "w_up": host("L0_ffn_w_up").reshape(H // 2, FR, D),
        "w_down": host("L0_ffn_w_down"),
        "conv_w": rows(host("L1_xattn_conv_w")),
        "gamma": rows(host("L1_xattn_bn_gamma")),
        "beta": rows(host("L1_xattn_bn_beta")),
        "router_w": tile_rows(host("L1_ffn_router_w")),
        "router_b": rows(host("L1_ffn_router_b")),
        "lora_a": tile_rows(host("L1_ffn_A").reshape(ER, D)),
        "lora_b": host("L1_ffn_Bm").transpose(0, 2, 1).reshape(ER, D),
    }
    arrays = {f"in_{name}": np.ascontiguousarray(a) for name, a in arrays.items()}
    nc = bacc.Bacc("TRN2", target_bir_lowering=False, num_devices=1)
    args = [nc.dram_tensor(name, a.shape, mybir.dt.from_np(a.dtype), kind="ExternalInput").ap()
            for name, a in arrays.items()]
    out = nc.dram_tensor("out", (B, S, D), F32, kind="ExternalOutput").ap()
    layers_kernel(nc, *args, out)
    result = run_bass_kernel_spmd(nc, [arrays], core_ids=[0])
    return result.results[0]["out"]
```

```python
from contextlib import ExitStack

import numpy as np

import concourse.bass as bass
from concourse import mybir

F32 = mybir.dt.float32
F32R = mybir.dt.float32r
BF16 = mybir.dt.bfloat16
U8 = mybir.dt.uint8
ALU = mybir.AluOpType
ACT = mybir.ActivationFunctionType
AX = mybir.AxisListType

P = 128
B = 8
S = 128
D = 512
KT = D // P
H = 32
DH = 128
HB = B // 2
NH = HB * S
STEPS = 2 * H
PAIRS = STEPS // 2
INTER = 1376
IT = -(-INTER // P)
LAST = INTER - (IT - 1) * P
FR = INTER * 2 // H
E = 8
R = 16
ER = E * R
EPS = 1e-5
MAGIC = 12582912.0
QMAX = 127.0
LOWEST = -3.4028234663852886e38
MASKED = -1e30
TAPS = 7
CRUCIAL = int(0.6 * S) + int(0.6 * S) % 2
REST = S - CRUCIAL


def layers_kernel(nc, x, cT, mask, bias, ln_w, wq, wk, wv, wo, w_gate, w_up, w_down,
                  conv_w, gamma, beta, router_w, router_b, lora_a, lora_b, out):
    ctx = ExitStack()

    def sbuf(name, shape, dt=F32, stack=ctx):
        return stack.enter_context(nc.sbuf_tensor(name, shape, dt))

    def psum(name, shape, dt=F32, stack=ctx):
        return stack.enter_context(nc.psum_tensor(name, shape, dt))

    def sem(name):
        return ctx.enter_context(nc.semaphore(name))

    with ctx:
        xr = sbuf("xr", [P, B, D])
        top_flat = sbuf("top", [P, KT * B * S], BF16)
        top = top_flat[:].rearrange("p (k b s) -> p k b s", k=KT, b=B)
        ident = sbuf("ident", [P, P])
        ident_b = sbuf("ident_b", [P, P], BF16)
        ones = sbuf("ones", [P, P])
        neg_half = sbuf("neg_half", [P, B])
        f_raw = [sbuf(f"f_raw{i}", [P, INTER]) for i in range(2)]
        g_raw = sbuf("g_raw", [P, D])
        g_mag = sbuf("g_mag", [P, D])
        g_q = sbuf("g_q", [P, D], BF16)
        f_s = sbuf("f_s", [P, 4])
        f_diag = sbuf("f_diag", [P, P])
        taps = sbuf("taps", [P, 2 * TAPS])
        diag = sbuf("diag", [P, 3 * P + TAPS - 1])

        early = ExitStack()
        xT_hi = [sbuf("xT0_hi", [P, KT, NH], F32R, early)]
        xT_lo = [sbuf("xT0_lo", [P, KT, NH], F32R, early)]
        cT_hi = [sbuf("cT0_hi", [P, KT, NH], F32R, early)]
        cT_lo = [sbuf("cT0_lo", [P, KT, NH], F32R, early)]
        cT_raw = sbuf("cT_raw", [P, KT * B * S], F32, early)
        hid = sbuf("hid", [P, B, D], F32, early)
        mask_u8 = sbuf("mask_u8", [P, B, S], U8, early)

        att = ExitStack()
        xT_hi.append(sbuf("xT1_hi", [P, KT, NH], F32R, att))
        xT_lo.append(sbuf("xT1_lo", [P, KT, NH], F32R, att))
        cT_hi.append(sbuf("cT1_hi", [P, KT, NH], F32R, att))
        cT_lo.append(sbuf("cT1_lo", [P, KT, NH], F32R, att))
        width = {"q": D, "k": D, "v": 2 * D, "o": D}
        w_raw = {c: sbuf(f"raw_{c}", [P, width[c]], F32, att) for c in "qkvo"}
        w_hi = {c: sbuf(f"w{c}_hi", [P, width[c]], F32R, att) for c in "qkvo"}
        w_lo = {c: sbuf(f"w{c}_lo", [P, width[c]], F32R, att) for c in "qkvo"}
        b_raw = sbuf("b_raw", [P, 1, S], F32, att)
        b_mask = sbuf("b_mask", [P, HB, S], F32, att)
        score = sbuf("score", [P, HB, S], F32, att)
        q_hi = sbuf("q_hi", [P, NH], F32R, att)
        q_lo = sbuf("q_lo", [P, NH], F32R, att)
        k_hi = sbuf("k_hi", [P, NH], F32R, att)
        k_lo = sbuf("k_lo", [P, NH], F32R, att)
        v_hi = sbuf("v_hi", [P, HB, 2 * DH], F32R, att)
        v_lo = sbuf("v_lo", [P, HB, 2 * DH], F32R, att)
        prob = sbuf("prob", [P, HB, S], F32, att)
        pT_hi = sbuf("pT_hi", [P, NH], F32R, att)
        pT_lo = sbuf("pT_lo", [P, NH], F32R, att)
        aT_hi = sbuf("aT_hi", [P, NH], F32R, att)
        aT_lo = sbuf("aT_lo", [P, NH], F32R, att)
        mask_add = sbuf("mask_add", [P, B, S], BF16, att)
        row_any = sbuf("row_any", [P, B], F32, att)
        neg_max = sbuf("neg_max", [P, HB], F32, att)
        row_sum = sbuf("row_sum", [P, HB], F32, att)
        row_inv = sbuf("row_inv", [P, HB, 1], F32, att)
        stats = sbuf("stats", [P, HB, 6], F32, att)
        mv = sbuf("mv", [P, HB, 2], F32, att)
        ve = sbuf("ve", [P, HB], F32, att)
        rs = sbuf("rs", [P, HB], F32, att)
        rs2 = sbuf("rs2", [P, HB], F32, att)
        keep = sbuf("keep", [P, B], F32, att)
        shift = sbuf("shift", [P, B], F32, att)
        lnw_col = sbuf("lnw_col", [P, KT, 1], F32, att)
        pick = sbuf("pick", [P, 2, S], F32, att)
        pick8 = sbuf("pick8", [P, 2, 8], F32, att)
        oacc = [psum(f"oacc{b}", [P, D], F32, att) for b in range(HB)]
        pX0 = psum("pX0", [P, NH], F32, att)
        pX1 = psum("pX1", [P, NH], F32, att)
        pS = psum("pS", [P, NH], F32, att)
        pT = psum("pT", [P, NH], F32, att)
        att.close()
        early.close()

        wguT = sbuf("wguT", [P, KT, 2 * INTER], BF16)
        gu_row = sbuf("gu_row", [P, 2 * INTER])
        wdT = sbuf("wdT", [P, IT, D], BF16)
        sd_row = sbuf("sd_row", [P, D])
        f_q = sbuf("f_q", [P, KT, INTER], BF16)
        f_steps = sbuf("f_steps", [P, KT])
        y = sbuf("y", [P, D])
        y_mag = sbuf("y_mag", [P, D])
        y_q = sbuf("y_q", [P, D], BF16)
        y_qT = sbuf("y_qT", [P, KT * S], BF16)
        y_s = sbuf("y_s", [P, 4])
        y_steps = sbuf("y_steps", [P, B])
        st6 = sbuf("st6", [P, 2, 6])
        mv1 = sbuf("mv1", [P, 2, 2])
        ve1 = sbuf("ve1", [P, 2])
        rs1 = sbuf("rs1", [P, 2])


        post = ExitStack()
        f_diags = sbuf("f_diags", [P, KT, P], F32, post)
        gate = sbuf("gate", [P, INTER], F32, post)
        silu = sbuf("silu", [P, INTER], F32, post)
        up = sbuf("up", [P, INTER], F32, post)
        h_mag = sbuf("h_mag", [P, INTER], F32, post)
        h_q = sbuf("h_q", [P, INTER], BF16, post)
        h_qT = sbuf("h_qT", [P, IT * S], BF16, post)
        h_s = sbuf("h_s", [P, 4], F32, post)
        down = sbuf("down", [P, D], F32, post)
        z = sbuf("z", [P, B, D], F32, post)
        z_t = sbuf("z_t", [P, D], F32, post)
        up_step = sbuf("up_step", [P, 1], F32, post)
        h_steps = sbuf("h_steps", [P, B], F32, post)
        zT = sbuf("zT", [P, KT, S], F32, post)
        split = sbuf("split", [P, 2, KT, S], F32, post)
        stat = [sbuf(f"stat{c}", [P, KT, 2, B], F32, post) for c in range(2)]
        tapped = sbuf("tapped", [P, TAPS, KT, 2, B], F32, post)
        cz = sbuf("cz", [P, KT, 2, B], F32, post)
        cz2 = sbuf("cz2", [P, KT, 2, B], F32, post)
        csum = sbuf("csum", [P, 2], F32, post)
        cmu = sbuf("cmu", [P, 2], F32, post)
        gb = sbuf("gb", [P, 2], F32, post)
        dA = sbuf("dA", [P, KT, B], F32, post)
        coef = sbuf("coef", [P, B, KT, S], F32, post)
        zc = sbuf("zc", [P, 2, D], F32, post)
        f = sbuf("f", [P, 2, D], F32, post)
        fT = sbuf("fT", [P, 2, KT * S], F32, post)
        ra = sbuf("ra", [P, KT, E + ER], F32, post)
        rb = sbuf("rb", [P, 1, E], F32, post)
        lb = sbuf("lb", [P, D], F32, post)
        rh = sbuf("rh", [P, B, E + ER], F32, post)
        logit = sbuf("logit", [P, B, E], F32, post)
        r_max = sbuf("r_max", [P, B, 1], F32, post)
        r_inv = sbuf("r_inv", [P, B, 1], F32, post)
        prb = sbuf("prb", [P, B, 2 * E], F32, post)
        prw = sbuf("prw", [P, B, 2 * E], F32, post)
        best = sbuf("best", [P, B, 8], F32, post)
        wexp = sbuf("wexp", [P, B, E, 1], F32, post)
        hwT = sbuf("hwT", [P, 2, S], F32, post)
        pA = psum("pA", [P, 3 * 512], F32, post)
        pTb = psum("pTb", [P, 2 * 1024], BF16, post)
        pD = psum("pD", [P, 512], F32, post)
        pZ = psum("pZ", [P, 512], F32, post)
        pYb = psum("pYb", [P, 1024], BF16, post)
        post.close()
        sum_junk = zc[:].rearrange("p i (k s) -> p i k s", k=KT)
        hw = f[:].rearrange("p i (b e r) -> p (i b) e r", e=E, r=R)
        f_bank = pTb[:].bitcast(F32)
        c_bank = (pZ, pD)

        s_a_done = sem("a_done")
        s_a_hi = sem("a_hi")
        s_a_lo = sem("a_lo")
        s_b_mask = sem("b_mask")
        s_cT_hi = sem("cT_hi")
        s_cT_lo = sem("cT_lo")
        s_c_in = [sem("c_in_first"), sem("c_in_second")]
        s_c_trans = sem("c_trans")
        s_c_used = sem("c_used")
        s_coef = sem("coef")
        s_coef_first = sem("coef_first")
        s_const_in = sem("const_in")
        s_conv = sem("conv")
        s_csum = sem("csum")
        s_ctotal = sem("ctotal")
        s_dA = sem("dA")
        s_d_proj = sem("d_proj")
        s_d_used = sem("d_used")
        s_diag = sem("diag")
        s_exp_done = sem("exp_done")
        s_f = sem("f")
        s_fT = sem("fT")
        s_f_diag = sem("f_diag")
        s_f_in = [sem("f_in_even"), sem("f_in_odd")]
        s_taps_in = sem("taps_in")
        s_f_mag = sem("f_mag")
        s_f_out = sem("f_out")
        s_f_q = sem("f_q")
        s_f_row = sem("f_row")
        s_f_t = sem("f_t")
        s_f_trans = sem("f_trans")
        s_f_step = sem("f_step")
        s_g_diag = sem("g_diag")
        s_g_in = sem("g_in")
        s_g_mag = sem("g_mag")
        s_g_out = sem("g_out")
        s_g_proj = sem("g_proj")
        s_g_q = sem("g_q")
        s_g_trans = sem("g_trans")
        s_gate = sem("gate")
        s_h_done = sem("h_done")
        s_h_mag = sem("h_mag")
        s_h_q = sem("h_q")
        s_h_qT = sem("h_qT")
        s_h_trans = sem("h_trans")
        s_hw = sem("hw")
        s_hwT = sem("hwT")
        s_hw_t = sem("hw_t")
        s_ident = sem("ident")
        s_k_hi = sem("k_hi")
        s_k_lo = sem("k_lo")
        s_k_proj = sem("k_proj")
        s_l_proj = sem("l_proj")
        s_lnw_in = sem("lnw_in")
        s_mask_add = sem("mask_add")
        s_mask_in = sem("mask_in")
        s_max_done = sem("max_done")
        s_neg_half = sem("neg_half")
        s_norm_done = sem("norm_done")
        s_o_done = sem("o_done")
        s_ones = sem("ones")
        s_p_hi = sem("p_hi")
        s_p_lo = sem("p_lo")
        s_p_trans = sem("p_trans")
        s_q_hi = sem("q_hi")
        s_q_lo = sem("q_lo")
        s_q_proj = sem("q_proj")
        s_r_exp = sem("r_exp")
        s_r_proj = sem("r_proj")
        s_rh = sem("rh")
        s_rstd = sem("rstd")
        s_s_done = sem("s_done")
        s_scored = sem("scored")
        s_sig = sem("sig")
        s_silu = sem("silu")
        s_ssq = sem("ssq")
        s_tapped = sem("tapped")
        s_top_logit = sem("top_logit")
        s_u_proj = sem("u_proj")
        s_up = sem("up")
        s_up_copy = sem("up_copy")
        s_v_hi = sem("v_hi")
        s_v_lo = sem("v_lo")
        s_v_proj = sem("v_proj")
        s_var_in = sem("var_in")
        s_x1_done = sem("x1_done")
        s_x4_done = sem("x4_done")
        s_xT_hi = sem("xT_hi")
        s_xT_lo = sem("xT_lo")
        s_x_in = [sem("x_in_first"), sem("x_in_second")]
        s_x_trans = sem("x_trans")
        s_xn = sem("xn")
        s_xw = sem("xw")
        s_y_mag = sem("y_mag")
        s_y_q = sem("y_q")
        s_y_qT = sem("y_qT")
        s_y_trans = sem("y_trans")
        s_z = sem("z")
        s_z_t = sem("z_t")
        s_z_trans = sem("z_trans")
        s_zT = sem("zT")
        s_cf = sem("cf")
        s_sf = sem("sf")
        s_maxed = sem("maxed")
        s_summed = sem("summed")
        s_zn = sem("zn")
        s_out = [sem("out_even"), sem("out_odd")]
        s_raw = {c: sem(f"raw_{c}") for c in "qkvob"}
        s_w_hi = {c: sem(f"w{c}_hi") for c in "qkvo"}
        s_w_lo = {c: sem(f"w{c}_lo") for c in "qkvo"}

        block = ctx.enter_context(nc.Block())

        def unless_last(n):
            return not isinstance(n, int) or n < STEPS

        def at(t):
            return slice(t, t + 1) if isinstance(t, int) else bass.ds(t, 1)

        DOWN_STEPS = (H, H + 1, STEPS - 2, STEPS - 1)

        def rows_of(m):
            t = m - H // 2
            return slice(t * FR, (t + 1) * FR) if isinstance(t, int) else bass.ds(t * FR, FR)

        wd_banks = pX0[:].bitcast(BF16), pX1[:].bitcast(BF16)
        wd_blocks = range(8), range(8, IT)
        g_trans_bank = pX1[:].bitcast(BF16)[:, NH:2 * NH]

        def later(n):
            return not isinstance(n, int) or n > 0

        CHUNKS = -(-INTER // 512)
        chunks = [(512 * j, min(512 * (j + 1), INTER)) for j in range(CHUNKS)]

        def live(t):
            return not isinstance(t, int) or 0 <= t < B


        @block.sync
        def _(sp):
            def load(c, n, head):
                if later(n):
                    sp.wait_ge(s_w_lo[c], n)
                src = {"q": wq, "k": wk, "v": wv, "o": wo}[c]
                sp.dma_start(w_raw[c][:], src[head]).then_inc(s_raw[c], 16)

            def load_bias(n, head):
                if later(n):
                    sp.wait_ge(s_b_mask, n)
                sp.dma_start(b_raw[:, 0, :], bias[head]).then_inc(s_raw["b"], 16)

            def load_rows(i, src, t):
                if later(i):
                    sp.wait_ge(s_g_mag, i)
                sp.dma_start(g_raw[0:FR, :], src[t]).then_inc(s_g_in, 16)

            sp.dma_start(taps[:], conv_w).then_inc(s_taps_in, 16)
            sp.dma_start(xr[:, 0:HB, :], x[0:HB].transpose([1, 0, 2])).then_inc(s_x_in[0], 16)
            sp.dma_start(lnw_col[:, :, 0], ln_w).then_inc(s_lnw_in, 16)
            for c in "qk":
                load(c, 0, 0)
            for half in range(2):
                for kt in range(KT):
                    sp.dma_start(cT_raw[:, (2 * kt + half) * NH:(2 * kt + half + 1) * NH],
                                 cT[kt, :, half * NH:(half + 1) * NH]).then_inc(s_c_in[half], 16)
                if half == 0:
                    sp.dma_start(xr[:, HB:B, :], x[HB:B].transpose([1, 0, 2])).then_inc(s_x_in[1], 16)
            sp.dma_start(mask_u8[:], mask).then_inc(s_mask_in, 16)
            load_bias(0, 0)
            load("v", 0, 0)
            load("o", 0, 0)
            for c in "qk":
                load(c, 1, 1)

            def loads(m, pair, rows=False):
                for odd in range(2):
                    n, head = 2 * m + odd, 2 * pair + odd
                    head1, head2 = head + 1, head + 2
                    if isinstance(head, int):
                        head1, head2 = head1 % H, head2 % H
                    if unless_last(n + 1):
                        load_bias(n + 1, head1)
                    if unless_last(n + 2):
                        load("q", n + 2, head2)
                        load("k", n + 2, head2)
                        if not odd:
                            load("v", m + 1, (pair + 1) % (H // 2) if isinstance(pair, int) else pair + 1)
                    if rows and unless_last(n + 1):
                        load_rows(n - H + 1, w_gate if odd else w_up, m - H // 2 + odd)
                    if unless_last(n + 1):
                        load("o", n + 1, head1)

            sp.dma_start(f_raw[0][:], w_down[0:P, :]).then_inc(s_f_in[0], 16)
            with sp.Fori(0, H // 2 - 1) as m:
                loads(m, m)
            sp.dma_start(f_raw[1][:], w_down[P:2 * P, :]).then_inc(s_f_in[1], 16)
            loads(H // 2 - 1, H // 2 - 1)
            load_rows(0, w_gate, 0)
            loads(H // 2, 0, rows=True)
            sp.wait_ge(s_f_q, 1)
            sp.dma_start(f_raw[0][:], w_down[2 * P:3 * P, :]).then_inc(s_f_in[0], 16)
            with sp.Fori(H // 2 + 1, PAIRS - 1) as m:
                loads(m, m - H // 2, rows=True)
            sp.wait_ge(s_f_q, 2)
            sp.dma_start(f_raw[1][:], w_down[3 * P:4 * P, :]).then_inc(s_f_in[1], 16)
            loads(PAIRS - 1, H // 2 - 1, rows=True)

            sp.wait_ge(s_x1_done, 2)
            sp.dma_start(gb[:, 0:1], gamma).then_inc(s_const_in, 16)
            sp.dma_start(gb[:, 1:2], beta).then_inc(s_const_in, 16)
            sp.dma_start(rb[:, 0, :], router_b).then_inc(s_const_in, 16)
            sp.dma_start(ra[:, :, 0:E], router_w).then_inc(s_const_in, 16)
            sp.dma_start(ra[:, :, E:E + ER], lora_a).then_inc(s_const_in, 16)
            sp.dma_start(lb[:], lora_b).then_inc(s_const_in, 16)

            for t in range(B):
                sp.wait_ge(s_x4_done, t + 1)
                sp.dma_start(out[t], xr[:, t, :]).then_inc(s_out[t % 2], 16)
            for done in s_out:
                sp.wait_ge(done, 16 * (B // 2))

        @block.gpsimd
        def _(pool):
            g = nc.gpsimd
            g.memset(ones[:], 1.0).then_inc(s_ones, 1)
            g.memset(neg_half[:], -0.5).then_inc(s_neg_half, 1)
            pool.wait_ge(s_ones, 1)
            g.affine_select(out=ident[:], in_=ones[:], compare_op=ALU.is_equal, fill=0.0, base=0,
                            pattern=[[-1, P]], channel_multiplier=1).then_inc(s_ident, 1)
            pool.wait_ge(s_ident, 1)
            g.tensor_copy(ident_b[:], ident[:]).then_inc(s_ident, 1)
            pool.wait_ge(s_neg_half, 1)

            def rsqrt(dst, src, n):
                pool.wait_ge(s_var_in, n + 1)
                g.tensor_tensor(dst, src, neg_half[:, 0:src.shape[-1]], ALU.pow).then_inc(s_rstd, 1)

            def lo(c, n):
                pool.wait_ge(s_w_hi[c], n + 1)
                g.tensor_tensor(w_lo[c][:], w_raw[c][:], w_hi[c][:].bitcast(F32),
                                ALU.subtract).then_inc(s_w_lo[c], 1)

            def bias_mask(n, half):
                pool.wait_ge(s_raw["b"], 16 * (n + 1))
                if later(n):
                    pool.wait_ge(s_scored, n)
                g.tensor_tensor(b_mask[:], b_raw[:].to_broadcast([P, HB, S]),
                                mask_add[:, half * HB:(half + 1) * HB, :], ALU.add).then_inc(s_b_mask, 1)

            g.memset(diag[:], 1.0).then_inc(s_diag, 1)
            pool.wait_ge(s_diag, 1)
            g.affine_select(out=diag[:], in_=diag[:], compare_op=ALU.is_equal, fill=0.0, base=P + TAPS // 2,
                            pattern=[[-1, 3 * P + TAPS - 1]], channel_multiplier=1).then_inc(s_diag, 1)
            lo("q", 0)
            lo("k", 0)
            rsqrt(rs[:], ve[:], 0)
            rsqrt(rs2[:], ve[:], 1)

            def context_low(half, tiles=range(KT)):
                for kt in tiles:
                    pool.wait_ge(s_cT_hi, half * KT + kt + 1)
                    g.tensor_tensor(cT_lo[half][:, kt, :],
                                    cT_raw[:, (2 * kt + half) * NH:(2 * kt + half + 1) * NH],
                                    cT_hi[half][:, kt, :].bitcast(F32), ALU.subtract).then_inc(s_cT_lo, 1)

            context_low(0)
            rsqrt(rs[:], ve[:], 2)
            rsqrt(rs2[:], ve[:], 3)
            pool.wait_ge(s_mask_add, 1)
            bias_mask(0, 0)
            lo("v", 0)
            lo("q", 1)
            lo("k", 1)

            def pair(m, half):
                for odd in range(2):
                    n = 2 * m + odd
                    if unless_last(n + 1):
                        bias_mask(n + 1, (n + 1) // H if isinstance(n, int) else half)
                    if unless_last(n + 2):
                        lo("q", n + 2)
                        lo("k", n + 2)
                        if odd:
                            lo("v", m + 1)
                    lo("o", n)

            pair(0, 0)
            for t in range(HB, B):
                pool.wait_ge(s_xT_hi, t + 1)
                cols = slice((t - HB) * S, (t - HB + 1) * S)
                g.tensor_tensor(xT_lo[1][:, :, cols], hid[:, t, :].rearrange("p (k s) -> p k s", k=KT),
                                xT_hi[1][:, :, cols].bitcast(F32), ALU.subtract).then_inc(s_xT_lo, 1)
            with pool.Fori(1, H // 2 - 2) as m:
                pair(m, 0)
            context_low(1, range(0, KT // 2))
            pair(H // 2 - 2, 0)
            context_low(1, range(KT // 2, KT))
            pair(H // 2 - 1, 0)
            pair(H // 2, 1)
            with pool.Fori(H // 2 + 1, PAIRS - 1) as m:
                pair(m, 1)
            pair(PAIRS - 1, 1)

            def ffn_step(t):
                if live(t - 2):
                    pool.wait_ge(s_zT, t - 1)
                    if later(t - 2):
                        pool.wait_ge(s_maxed, t - 2)
                        pool.wait_ge(s_summed, t - 2)
                    g.tensor_tensor(split[:, 0], zT[:], top[:, :, t - 2, :], ALU.mult).then_inc(s_cf, 1)
                    pool.wait_ge(s_cf, t - 1)
                    g.tensor_tensor(split[:, 1], zT[:], split[:, 0], ALU.subtract).then_inc(s_sf, 1)
                if live(t - 1) or live(t + 2):
                    rsqrt(rs1[:], ve1[:], t + 6)
                if live(t + 1):
                    for j, (c0, c1) in enumerate(chunks):
                        pool.wait_ge(s_up_copy, CHUNKS * (t + 1) + j + 1)
                        g.tensor_tensor(up[:, c0:c1], up[:, c0:c1], gu_row[:, INTER + c0:INTER + c1],
                                        ALU.mult).then_inc(s_up, 1)

            for t in range(-2, 2):
                ffn_step(t)
            with pool.Fori(2, B - 2) as t:
                ffn_step(t)
            for t in range(B - 2, B + 2):
                ffn_step(t)
            rsqrt(rs1[:], ve1[:], B + 7)
            with pool.Fori(0, B // 2) as p:
                rsqrt(rs1[:], ve1[:], p + B + 8)

        @block.scalar
        def _(act):
            a = nc.scalar

            def copy(dst, src):
                return a.activation(dst, src, ACT.Copy)

            def hi(c, n, used):
                act.wait_ge(s_raw[c], 16 * (n + 1))
                if later(n):
                    act.wait_ge(used, n)
                copy(w_hi[c][:], w_raw[c][:]).then_inc(s_w_hi[c], 1)

            def x_high(half):
                for b in range(HB):
                    t = half * HB + b
                    act.wait_ge(s_xw, t + 1)
                    copy(xT_hi[half][:, :, b * S:(b + 1) * S],
                         hid[:, t, :].rearrange("p (k s) -> p k s", k=KT)).then_inc(s_xT_hi, 1)

            hi("q", 0, s_q_proj)
            hi("k", 0, s_k_proj)

            def context_high(half):
                for kt in range(KT):
                    act.wait_ge(s_c_in[half], 16 * KT)
                    copy(cT_hi[half][:, kt, :],
                         cT_raw[:, (2 * kt + half) * NH:(2 * kt + half + 1) * NH]).then_inc(s_cT_hi, 1)

            x_high(0)
            context_high(0)

            def query_high(n):
                act.wait_ge(s_q_proj, n + 1)
                copy(q_hi[:], pX0[:]).then_inc(s_q_hi, 1)

            def key_high(n):
                act.wait_ge(s_k_proj, n + 1)
                copy(k_hi[:], pX1[:]).then_inc(s_k_hi, 1)

            hi("v", 0, s_v_proj)
            query_high(0)
            hi("q", 1, s_q_proj)
            key_high(0)
            hi("k", 1, s_k_proj)
            x_high(1)

            def pair(m, rows=False):
                for odd in range(2):
                    n = 2 * m + odd
                    act.wait_ge(s_max_done, n + 1)
                    if later(n):
                        act.wait_ge(s_p_trans, n)
                    for b in range(HB):
                        e = a.activation(prob[:, b, :], score[:, b, :], ACT.Exp,
                                         bias=neg_max[:, b:b + 1], accum_out=row_sum[:, b:b + 1])
                    e.then_inc(s_exp_done, 1)
                    if unless_last(n + 1):
                        query_high(n + 1)
                    if unless_last(n + 2):
                        hi("q", n + 2, s_q_proj)
                    if rows:
                        chunk = n - H
                        act.wait_ge(s_g_mag, chunk + 1)
                        if later(chunk):
                            act.wait_ge(s_g_trans, chunk)
                        a.activation(g_q[0:FR, :], g_mag[0:FR, :], ACT.Copy, bias=-MAGIC).then_inc(s_g_q, 1)
                    if unless_last(n + 1):
                        key_high(n + 1)
                    if unless_last(n + 2):
                        hi("k", n + 2, s_k_proj)
                    if not odd:
                        for i, bank in enumerate((pX0, pX1)):
                            act.wait_ge(s_v_proj, n + i + 1)
                            copy(v_hi[:, 2 * i:2 * i + 2, :], bank[:]).then_inc(s_v_hi, 1)
                    act.wait_ge(s_p_trans, n + 1)
                    copy(pT_hi[:], pS[:]).then_inc(s_p_hi, 1)
                    if odd and unless_last(n + 2):
                        act.wait_ge(s_v_proj, n + 1)
                        hi("v", m + 1, s_v_proj)
                    hi("o", n, s_o_done)
                    if rows:
                        act.wait_ge(s_g_trans, chunk + 1)
                        copy(gu_row[:, odd * INTER:(odd + 1) * INTER][:, rows_of(m)], pX1[:, 0:FR])
                        copy(wguT[:, :, odd * INTER:(odd + 1) * INTER][:, :, rows_of(m)],
                             g_trans_bank[:, 0:KT * FR].rearrange("p (k r) -> p k r", k=KT)).then_inc(s_g_out, 1)
                    act.wait_ge(s_a_done, n + 1)
                    copy(aT_hi[:], pT[:]).then_inc(s_a_hi, 1)
                    if isinstance(n, int) and n == 0:
                        context_high(1)
                    if isinstance(n, int) and n in DOWN_STEPS:
                        i = DOWN_STEPS.index(n)
                        act.wait_ge(s_f_mag, i + 1)
                        a.activation(f_q[:, i, :], f_raw[i % 2][:], ACT.Copy, bias=-MAGIC).then_inc(s_f_q, 1)

            pair(0)
            with act.Fori(1, H // 2) as m:
                pair(m)
            pair(H // 2, rows=True)
            with act.Fori(H // 2 + 1, PAIRS - 1) as m:
                pair(m, rows=True)
            pair(PAIRS - 1, rows=True)

            def down_tile(t):
                cols = slice(t * P, (t + 1) * P)
                first, second = (bank.rearrange("p (k s) -> p k s", s=P) for bank in wd_banks)
                act.wait_ge(s_f_trans, 2 * t + 1)
                copy(wdT[:, 0:8, cols], first).then_inc(s_f_out, 1)
                act.wait_ge(s_f_trans, 2 * t + 2)
                copy(wdT[:, 8:IT - 1, cols], second[:, 0:IT - 9, :])
                copy(wdT[0:LAST, IT - 1, cols], second[0:LAST, IT - 9, :]).then_inc(s_f_out, 1)

            down_tile(0)

            def ffn_step(t):
                if live(t + 1):
                    act.wait_ge(s_y_mag, t + 2)
                    if later(t + 1):
                        act.wait_ge(s_y_trans, t + 1)
                    a.activation(y_q[:], y_mag[:], ACT.Copy, bias=-MAGIC).then_inc(s_y_q, 1)
                    if isinstance(t, int) and t == -1:
                        down_tile(1)
                    act.wait_ge(s_y_trans, t + 2)
                    if later(t + 1):
                        act.wait_ge(s_u_proj, CHUNKS * (t + 1))
                    copy(y_qT[:], pYb[:, 0:KT * S]).then_inc(s_y_qT, 1)
                    if isinstance(t, int) and t == -1:
                        down_tile(2)
                        down_tile(3)
                if live(t - 2):
                    act.drain()
                    act.wait_ge(s_sf, t - 1)
                    for br in range(2):
                        for lt in range(KT):
                            last = a.activation(sum_junk[:, br, lt, :], split[:, br, lt, :], ACT.Copy,
                                                accum_out=stat[1][:, lt, br, at(t - 2)])
                    last.then_inc(s_summed, 1)
                if live(t):
                    act.wait_ge(s_h_mag, t + 1)
                    if later(t):
                        act.wait_ge(s_h_trans, t)
                    a.activation(h_q[:], h_mag[:], ACT.Copy, bias=-MAGIC).then_inc(s_h_q, 1)
                if live(t + 1):
                    copy(up_step[:], y_steps[:, at(t + 1)])
                    act.drain()
                    for j, (c0, c1) in enumerate(chunks):
                        act.wait_ge(s_u_proj, CHUNKS * (t + 1) + j + 1)
                        a.activation(up[:, c0:c1], pA[:, c0:c1], ACT.Copy,
                                     scale=up_step[:, 0:1]).then_inc(s_up_copy, 1)
                if live(t + 1):
                    act.wait_ge(s_gate, CHUNKS * (t + 2))
                    a.activation(silu[:], gate[:], ACT.Silu).then_inc(s_silu, 1)
                if live(t):
                    act.wait_ge(s_h_trans, t + 1)
                    if later(t):
                        act.wait_ge(s_d_proj, t)
                    copy(h_qT[:, 0:(IT - 1) * S], pTb[:, 0:(IT - 1) * S])
                    copy(h_qT[0:LAST, (IT - 1) * S:IT * S],
                         pTb[0:LAST, (IT - 1) * S:IT * S]).then_inc(s_h_qT, 1)
                if live(t - 1):
                    act.wait_ge(s_z_t, t)
                    copy(z[:, t - 1, :], z_t[:]).then_inc(s_z, 1)
                    act.wait_ge(s_z_trans, t)
                    if later(t - 1):
                        act.wait_ge(s_sf, t - 1)
                    copy(zT[:], pZ[:].rearrange("p (k s) -> p k s", k=KT)).then_inc(s_zT, 1)

            ffn_step(-1)

            for t in range(2):
                ffn_step(t)
            with act.Fori(2, B - 2) as t:
                ffn_step(t)
            for t in range(B - 2, B + 2):
                ffn_step(t)

            act.wait_ge(s_zn, 1)
            a.activation(cz[:], cz2[:], ACT.Tanh, scale=0.5).then_inc(s_sig, 1)
            act.wait_ge(s_dA, 1)

            def weights_of(p):
                for i in range(2):
                    t = 2 * p + i
                    for lt in range(KT):
                        last = a.activation(coef[:, t, lt, :], top[:, lt, t, :], ACT.Identity,
                                            scale=dA[:, lt, at(t)], bias=cz[:, lt, 1, at(t)])
                    last.then_inc(s_coef, 1)

            def route_pair(p, more=True):
                for i in range(2):
                    act.wait_ge(s_f_t, 2 * p + i + 1)
                    copy(fT[:, i, :], f_bank[:, i * 512:(i + 1) * 512]).then_inc(s_fT, 1)
                if more:
                    weights_of(p + 2)
                for i in range(2):
                    act.wait_ge(s_r_proj, 2 * p + i + 1)
                    copy(rh[:, 2 * p + i, :], pA[:, i * 512:i * 512 + E + ER]).then_inc(s_rh, 1)

            weights_of(1)
            for p in range(B // 2):
                route_pair(p, more=p + 2 < B // 2)

            act.wait_ge(s_top_logit, 1)
            a.activation(prb[:, :, 0:E], logit[:], ACT.Exp).then_inc(s_r_exp, 1)
            for t in range(B):
                act.wait_ge(s_hw_t, t + 1)
                if later(t - 1):
                    act.wait_ge(s_l_proj, t - 1)
                copy(hwT[:, t % 2, :], pA[:, (t % 2) * 512:(t % 2) * 512 + S]).then_inc(s_hwT, 1)

        @block.vector
        def _(dve):
            v = nc.vector

            v.memset(stats[:], 0.0)

            def normed(half):
                tiles = range(half * HB, (half + 1) * HB)
                cols = slice(half * HB, (half + 1) * HB)
                dve.drain()
                dve.wait_ge(s_x_in[half], 16)
                for b, t in enumerate(tiles):
                    v.bn_stats(stats[:, b, :], xr[:, t, :])
                dve.drain()
                for b in range(HB):
                    v.bn_aggr(mv[:, b, :], stats[:, b, :])
                dve.drain()
                v.tensor_scalar(ve[:], mv[:, :, 1], EPS, None, ALU.add).then_inc(s_var_in, 1)
                dve.wait_ge(s_rstd, 2 * half + 1)
                v.tensor_tensor(ve[:], mv[:, :, 1], rs[:], ALU.mult)
                v.tensor_scalar(keep[:, cols], rs[:], 1.0, None, ALU.add)
                v.tensor_tensor(shift[:, cols], mv[:, :, 0], rs[:], ALU.mult)
                dve.drain()
                v.tensor_tensor(ve[:], ve[:], rs[:], ALU.mult)
                dve.drain()
                v.tensor_scalar(ve[:], ve[:], EPS, None, ALU.add).then_inc(s_var_in, 1)
                dve.wait_ge(s_rstd, 2 * half + 2)
                v.tensor_tensor(rs[:], rs[:], rs2[:], ALU.mult)
                dve.drain()
                for b, t in enumerate(tiles):
                    v.tensor_scalar(hid[:, t, :], xr[:, t, :], mv[:, b, 0:1], rs[:, b:b + 1],
                                    ALU.subtract, ALU.mult).then_inc(s_xn, 1)

            def weighted(half):
                tiles = range(half * HB, (half + 1) * HB)
                dve.wait_ge(s_lnw_in, 16)
                for b, t in enumerate(tiles):
                    dve.wait_ge(s_x_trans, t + 1)
                    v.tensor_tensor(hid[:, t, :].rearrange("p (k s) -> p k s", k=KT),
                                    oacc[b][:].rearrange("p (k s) -> p k s", k=KT),
                                    lnw_col[:].to_broadcast([P, KT, S]), ALU.mult).then_inc(s_xw, 1)
                if half:
                    return
                for b, t in enumerate(tiles):
                    dve.wait_ge(s_xT_hi, t + 1)
                    cols = slice(b * S, (b + 1) * S)
                    v.tensor_tensor(xT_lo[half][:, :, cols], hid[:, t, :].rearrange("p (k s) -> p k s", k=KT),
                                    xT_hi[half][:, :, cols].bitcast(F32), ALU.subtract).then_inc(s_xT_lo, 1)

            def add_norm(half):
                dve.drain()
                for t in range(half * HB, (half + 1) * HB):
                    v.tensor_scalar(xr[:, t, :], xr[:, t, :], keep[:, t:t + 1], shift[:, t:t + 1],
                                    ALU.mult, ALU.subtract)

            def query_low(n):
                dve.wait_ge(s_q_hi, n + 1)
                v.tensor_tensor(q_lo[:], pX0[:], q_hi[:].bitcast(F32), ALU.subtract).then_inc(s_q_lo, 1)

            def key_low(n):
                dve.wait_ge(s_k_hi, n + 1)
                v.tensor_tensor(k_lo[:], pX1[:], k_hi[:].bitcast(F32), ALU.subtract).then_inc(s_k_lo, 1)

            normed(0)
            weighted(0)
            dve.wait_ge(s_mask_in, 16)
            v.tensor_scalar(mask_add[:], mask_u8[:], -1.0, -MASKED, ALU.add, ALU.mult)
            v.tensor_reduce(row_any[:], mask_u8[:], AX.X, ALU.max).then_inc(s_mask_add, 1)
            normed(1)
            query_low(0)
            key_low(0)
            weighted(1)

            def pick_round(last=False):
                dve.drain()
                for r in range(2):
                    v.max(pick8[:, r, :], pick[:, r, :])
                dve.drain()
                if last and REST % 8:
                    v.memset(pick8[:, :, REST % 8:8], LOWEST)
                    dve.drain()
                for r in range(2):
                    v.match_replace(pick[:, r, :], pick8[:, r, :], pick[:, r, :], LOWEST)

            def residual(half):
                dve.wait_ge(s_o_done, (half + 1) * H)
                for b in range(HB):
                    t = half * HB + b
                    last = v.tensor_tensor(xr[:, t, :], oacc[b][:], xr[:, t, :], ALU.add)
                last.then_inc(s_x1_done, 1)

            def pair(m, half, picks=False, rows=False):
                for odd in range(2):
                    n = 2 * m + odd
                    dve.wait_ge(s_b_mask, n + 1)
                    dve.wait_ge(s_s_done, n + 1)
                    v.tensor_tensor(score[:], pS[:].rearrange("p (b s) -> p b s", b=HB), b_mask[:],
                                    ALU.add).then_inc(s_scored, 1)
                    dve.drain()
                    v.tensor_reduce(neg_max[:], score[:], AX.X, ALU.max, negate=True).then_inc(s_max_done, 1)
                    if rows:
                        chunk = n - H
                        dve.drain()
                        dve.wait_ge(s_g_in, 16 * (chunk + 1))
                        v.tensor_reduce(f_s[0:FR, 0:1], g_raw[0:FR, :], AX.X, ALU.max, apply_absolute_value=True)
                        dve.drain()
                        v.tensor_scalar(f_s[0:FR, 1:2], f_s[0:FR, 0:1], 1.0 / QMAX, 1e-8, ALU.mult, ALU.max)
                        dve.drain()
                        v.reciprocal(f_s[0:FR, 2:3], f_s[0:FR, 1:2])
                        if later(chunk):
                            dve.wait_ge(s_g_trans, chunk)
                        v.tensor_scalar(f_diag[0:FR, 0:FR], ident[0:FR, 0:FR], f_s[0:FR, 1:2], None,
                                        ALU.mult).then_inc(s_g_diag, 1)
                        dve.drain()
                        if later(chunk):
                            dve.wait_ge(s_g_q, chunk)
                        v.tensor_scalar(g_mag[0:FR, :], g_raw[0:FR, :], f_s[0:FR, 2:3], MAGIC,
                                        ALU.mult, ALU.add).then_inc(s_g_mag, 1)
                    if picks and not odd:
                        dve.drain()
                        for r in range(2):
                            v.tensor_scalar(pick[:, r, ::-1], cT_raw[:, bass.ds((2 * m + r) * S, S)], -1.0, None,
                                            ALU.mult)
                    if picks:
                        pick_round()
                    if not odd:
                        query_low(n + 1)
                    dve.wait_ge(s_exp_done, n + 1)
                    v.reciprocal(row_inv[:, :, 0], row_sum[:])
                    dve.drain()
                    v.tensor_tensor(row_inv[:, :, 0], row_inv[:, :, 0], row_any[:, half * HB:(half + 1) * HB],
                                    ALU.mult)
                    dve.drain()
                    v.tensor_tensor(prob[:], prob[:], row_inv[:].to_broadcast([P, HB, S]),
                                    ALU.mult).then_inc(s_norm_done, 1)
                    if odd and unless_last(n + 1):
                        query_low(n + 1)
                    if picks:
                        pick_round()
                    if unless_last(n + 1):
                        key_low(n + 1)
                    if not odd:
                        if picks:
                            pick_round()
                        for i, bank in enumerate((pX0, pX1)):
                            dve.wait_ge(s_v_hi, n + i + 1)
                            v.tensor_tensor(v_lo[:, 2 * i:2 * i + 2, :], bank[:].rearrange("p (b d) -> p b d", b=2),
                                            v_hi[:, 2 * i:2 * i + 2, :].bitcast(F32), ALU.subtract).then_inc(s_v_lo, 1)
                            if picks and not i:
                                pick_round()
                    dve.wait_ge(s_p_hi, n + 1)
                    v.tensor_tensor(pT_lo[:], pS[:], pT_hi[:].bitcast(F32), ALU.subtract).then_inc(s_p_lo, 1)
                    if picks and odd:
                        pick_round(last=True)
                        dve.drain()
                        for r in range(2):
                            v.tensor_scalar(top_flat[:, bass.ds((2 * m + r) * S, S)], pick[:, r, ::-1], LOWEST, None,
                                            ALU.not_equal)
                    if isinstance(n, int) and n in DOWN_STEPS:
                        i = DOWN_STEPS.index(n)
                        dve.drain()
                        dve.wait_ge(s_f_in[i % 2], 16 * (i // 2 + 1))
                        v.tensor_reduce(f_s[:, 0:1], f_raw[i % 2][:], AX.X, ALU.max, apply_absolute_value=True)
                        dve.drain()
                        v.tensor_scalar(f_steps[:, i:i + 1], f_s[:, 0:1], 1.0 / QMAX, 1e-8, ALU.mult, ALU.max)
                        dve.drain()
                        v.reciprocal(f_s[:, 2:3], f_steps[:, i:i + 1])
                        dve.drain()
                        v.tensor_scalar(f_raw[i % 2][:], f_raw[i % 2][:], f_s[:, 2:3], MAGIC,
                                        ALU.mult, ALU.add).then_inc(s_f_mag, 1)
                    dve.wait_ge(s_a_hi, n + 1)
                    v.tensor_tensor(aT_lo[:], pT[:], aT_hi[:].bitcast(F32), ALU.subtract).then_inc(s_a_lo, 1)
                    if isinstance(n, int) and n in (1, H - 1):
                        add_norm(n // (H - 1))
                    if isinstance(n, int) and n == H:
                        residual(0)

            dve.wait_ge(s_c_in[1], 16 * KT)
            pair(0, 0, picks=True)
            with dve.Fori(1, H // 2 - 1) as m:
                pair(m, 0, picks=True)
            pair(H // 2 - 1, 0, picks=True)
            pair(H // 2, 1, rows=True)
            with dve.Fori(H // 2 + 1, PAIRS - 1) as m:
                pair(m, 1, rows=True)
            pair(PAIRS - 1, 1, rows=True)

            def maxima(t):
                if live(t):
                    dve.wait_ge(s_sf, t + 1)
                    for br in range(2):
                        last = v.tensor_reduce(stat[0][:, :, br, at(t)], split[:, br], AX.X, ALU.max)
                    last.then_inc(s_maxed, 1)

            def hidden_ints(t):
                dve.drain()
                v.tensor_scalar(h_steps[:, at(t)], h_s[:, 0:1], 1.0 / QMAX, 1e-8, ALU.mult, ALU.max)
                dve.drain()
                v.reciprocal(h_s[:, 2:3], h_steps[:, at(t)])
                dve.drain()
                dve.wait_ge(s_h_q, t)
                v.tensor_scalar(h_mag[:], silu[:], h_s[:, 2:3], MAGIC, ALU.mult, ALU.add).then_inc(s_h_mag, 1)

            def ffn_step(t):
                dve.drain()
                if live(t + 2):
                    v.bn_stats(st6[:, 1, :], xr[:, t + 2, :])
                if live(t):
                    dve.wait_ge(s_silu, t + 1)
                    dve.wait_ge(s_up, CHUNKS * (t + 1))
                    v.tensor_tensor(silu[:], silu[:], up[:], ALU.mult)
                    dve.drain()
                    v.tensor_reduce(h_s[:, 0:1], silu[:], AX.X, ALU.max, apply_absolute_value=True)
                if isinstance(t, int) and t == B - 1:
                    hidden_ints(t)
                if live(t - 1):
                    dve.wait_ge(s_d_proj, t)
                    v.scalar_tensor_tensor(out=down[:], in0=pD[:], scalar=h_steps[:, at(t - 1)], in1=sd_row[:],
                                           op0=ALU.mult, op1=ALU.mult).then_inc(s_d_used, 1)
                dve.drain()
                side_by_side = live(t) and not (isinstance(t, int) and t == B - 1)
                if side_by_side:
                    v.tensor_scalar(h_steps[:, at(t)], h_s[:, 0:1], 1.0 / QMAX, 1e-8, ALU.mult, ALU.max)
                if live(t - 1):
                    v.tensor_tensor(xr[:, t - 1, :], xr[:, t - 1, :], down[:], ALU.add)
                dve.drain()
                if side_by_side:
                    v.reciprocal(h_s[:, 2:3], h_steps[:, at(t)])
                if live(t - 1):
                    v.bn_stats(st6[:, 0, :], xr[:, t - 1, :])
                dve.drain()
                if live(t - 1):
                    v.bn_aggr(mv1[:, 0, :], st6[:, 0, :])
                if live(t + 2):
                    v.bn_aggr(mv1[:, 1, :], st6[:, 1, :])
                if side_by_side:
                    if later(t):
                        dve.wait_ge(s_h_q, t)
                    v.tensor_scalar(h_mag[:], silu[:], h_s[:, 2:3], MAGIC, ALU.mult, ALU.add).then_inc(s_h_mag, 1)
                dve.drain()
                if live(t - 1) or live(t + 2):
                    v.tensor_scalar(ve1[:], mv1[:, :, 1], EPS, None, ALU.add).then_inc(s_var_in, 1)
                if live(t + 1):
                    for j, (c0, c1) in enumerate(chunks):
                        dve.wait_ge(s_g_proj, CHUNKS * (t + 1) + j + 1)
                        if j == 0 and later(t + 1):
                            dve.wait_ge(s_silu, t + 1)
                        v.scalar_tensor_tensor(out=gate[:, c0:c1], in0=pA[:, c0:c1], scalar=y_steps[:, at(t + 1)],
                                               in1=gu_row[:, c0:c1], op0=ALU.mult, op1=ALU.mult).then_inc(s_gate, 1)
                if live(t - 1) or live(t + 2):
                    dve.wait_ge(s_rstd, t + 7)
                if live(t + 2):
                    v.tensor_scalar(y[:], xr[:, t + 2, :], mv1[:, 1, 0:1], rs1[:, 1:2], ALU.subtract, ALU.mult)
                if live(t - 1):
                    if later(t - 1):
                        dve.wait_ge(s_z, t - 1)
                        dve.wait_ge(s_z_trans, t - 1)
                    v.tensor_scalar(z_t[:], xr[:, t - 1, :], mv1[:, 0, 0:1], rs1[:, 0:1],
                                    ALU.subtract, ALU.mult).then_inc(s_z_t, 1)
                if live(t + 2):
                    dve.drain()
                    v.tensor_reduce(y_s[:, 0:1], y[:], AX.X, ALU.max, apply_absolute_value=True)
                    dve.drain()
                    v.tensor_scalar(y_steps[:, at(t + 2)], y_s[:, 0:1], 1.0 / QMAX, 1e-8, ALU.mult, ALU.max)
                    dve.drain()
                    v.reciprocal(y_s[:, 2:3], y_steps[:, at(t + 2)])
                    dve.drain()
                    if later(t + 2):
                        dve.wait_ge(s_y_q, t + 2)
                    v.tensor_scalar(y_mag[:], y[:], y_s[:, 2:3], MAGIC, ALU.mult, ALU.add).then_inc(s_y_mag, 1)
                maxima(t - 2)

            v.memset(mv1[:], 0.0)
            dve.drain()
            ffn_step(-2)
            residual(1)
            ffn_step(-1)

            for t in range(KT):
                v.tensor_scalar(f_diags[:, t, :], ident[:], f_steps[:, t:t + 1], None, ALU.mult).then_inc(s_f_diag, 1)

            dve.drain()
            v.memset(prb[:, :, E:2 * E], -1.0)
            ffn_step(0)
            dve.wait_ge(s_f_step, 1)
            v.tensor_copy(sd_row[:], pD[:]).then_inc(s_f_row, 1)
            ffn_step(1)
            with dve.Fori(2, B - 2) as t:
                ffn_step(t)
            for t in range(B - 2, B + 2):
                ffn_step(t)

            dve.drain()
            dve.wait_ge(s_taps_in, 16)
            for j in range(TAPS):
                v.tensor_scalar(tapped[:, j], stat[0][:], taps[:, j:j + 1], None, ALU.mult)
            dve.wait_ge(s_summed, B)
            for br, n in enumerate((CRUCIAL, REST)):
                v.tensor_scalar(stat[1][:, :, br, :], stat[1][:, :, br, :], 1.0 / S, S / n,
                                ALU.mult, ALU.mult)
            dve.drain()
            for j in range(TAPS):
                v.scalar_tensor_tensor(out=tapped[:, j], in0=stat[1][:], scalar=taps[:, TAPS + j:TAPS + j + 1],
                                       in1=tapped[:, j], op0=ALU.mult, op1=ALU.add).then_inc(s_tapped, 1)
            dve.wait_ge(s_const_in, 16 * 6)
            dve.wait_ge(s_conv, 1)
            conv = pA[:, 0:KT * 2 * B].rearrange("p (k r b) -> p k r b", k=KT, r=2)
            v.tensor_copy(cz[:], conv)
            dve.drain()
            v.tensor_reduce(csum[:], cz[:].rearrange("p k r b -> p r k b"), AX.XY, ALU.add).then_inc(s_csum, 1)
            dve.wait_ge(s_ctotal, 1)
            v.tensor_scalar(cmu[:], pA[:, 512:514], 1.0 / (B * D), None, ALU.mult)
            dve.drain()
            for br in range(2):
                v.tensor_scalar(cz[:, :, br, :], cz[:, :, br, :], cmu[:, br:br + 1], None, ALU.subtract)
            dve.drain()
            v.tensor_tensor(cz2[:], cz[:], cz[:], ALU.mult)
            dve.drain()
            v.tensor_reduce(csum[:], cz2[:].rearrange("p k r b -> p r k b"), AX.XY, ALU.add).then_inc(s_csum, 1)
            dve.wait_ge(s_ctotal, 2)
            v.tensor_scalar(ve1[:], pA[:, 1024:1026], 1.0 / (B * D), EPS, ALU.mult, ALU.add).then_inc(s_var_in, 1)
            dve.wait_ge(s_rstd, B + 8)
            for br in range(2):
                v.tensor_scalar(cz2[:, :, br, :], cz[:, :, br, :], rs1[:, br:br + 1], gb[:, 0:1],
                                ALU.mult, ALU.mult)
            dve.drain()
            v.tensor_scalar(cz2[:], cz2[:], gb[:, 1:2], 0.0, ALU.add, ALU.max).then_inc(s_zn, 1)
            dve.wait_ge(s_sig, 1)
            v.tensor_scalar(cz[:], cz[:], 0.5, 0.5, ALU.mult, ALU.add)
            dve.drain()
            v.tensor_tensor(dA[:], cz[:, :, 0, :], cz[:, :, 1, :], ALU.subtract).then_inc(s_dA, 1)

            def route_pair(p):
                for i in range(2):
                    dve.wait_ge(s_c_trans, 2 * p + i + 1)
                    v.tensor_tensor(zc[:, i, :], c_bank[i][:], z[:, 2 * p + i, :], ALU.mult).then_inc(s_c_used, 1)
                dve.drain()
                for i in range(2):
                    v.tensor_tensor(xr[:, 2 * p + i, :], zc[:, i, :], xr[:, 2 * p + i, :], ALU.add)
                dve.drain()
                for i in range(2):
                    v.bn_stats(st6[:, i, :], xr[:, 2 * p + i, :])
                dve.drain()
                for i in range(2):
                    v.bn_aggr(mv1[:, i, :], st6[:, i, :])
                dve.drain()
                v.tensor_scalar(ve1[:], mv1[:, :, 1], EPS, None, ALU.add).then_inc(s_var_in, 1)
                dve.wait_ge(s_rstd, p + B + 9)
                for i in range(2):
                    if later(p):
                        dve.wait_ge(s_f_t, 2 * p + i - 1)
                    v.tensor_scalar(f[:, i, :], xr[:, 2 * p + i, :], mv1[:, i, 0:1], rs1[:, i:i + 1],
                                    ALU.subtract, ALU.mult).then_inc(s_f, 1)

            dve.drain()
            for t in range(2):
                for lt in range(KT):
                    last = v.tensor_scalar(coef[:, t, lt, :], top[:, lt, t, :], dA[:, lt, t:t + 1],
                                           cz[:, lt, 1, t:t + 1], ALU.mult, ALU.add)
                last.then_inc(s_coef_first, 1)
            route_pair(0)
            with dve.Fori(1, B // 2) as p:
                route_pair(p)

            dve.wait_ge(s_rh, B)
            v.tensor_tensor(logit[:], rh[:, :, 0:E], rb[:].to_broadcast([P, B, E]), ALU.add)
            dve.drain()
            v.tensor_reduce(r_max[:, :, 0], logit[:], AX.X, ALU.max)
            dve.drain()
            v.tensor_tensor(logit[:], logit[:], r_max[:].to_broadcast([P, B, E]),
                            ALU.subtract).then_inc(s_top_logit, 1)
            dve.wait_ge(s_r_exp, 1)
            v.tensor_reduce(r_max[:, :, 0], prb[:, :, 0:E], AX.X, ALU.add)
            dve.drain()
            v.reciprocal(r_inv[:, :, 0], r_max[:, :, 0])
            dve.drain()
            v.tensor_tensor(prb[:, :, 0:E], prb[:, :, 0:E], r_inv[:].to_broadcast([P, B, E]), ALU.mult)
            dve.drain()
            for t in range(B):
                v.max(best[:, t, :], prb[:, t, :])
            dve.drain()
            v.tensor_tensor(r_max[:, :, 0], best[:, :, 0], best[:, :, 1], ALU.add)
            v.memset(best[:, :, 2:8], -1.0)
            dve.drain()
            for t in range(B):
                v.match_replace(prw[:, t, :], best[:, t, :], prb[:, t, :], -2.0)
            v.reciprocal(r_inv[:, :, 0], r_max[:, :, 0])
            dve.drain()
            v.scalar_tensor_tensor(out=wexp[:, :, :, 0], in0=prw[:, :, 0:E], scalar=-2.0, in1=prb[:, :, 0:E],
                                   op0=ALU.is_equal, op1=ALU.mult)
            dve.drain()
            v.tensor_tensor(wexp[:, :, :, 0], wexp[:, :, :, 0], r_inv[:].to_broadcast([P, B, E]), ALU.mult)
            dve.drain()
            for t in range(B):
                v.tensor_tensor(hw[:, t, :, :], rh[:, t, E:E + ER].rearrange("p (e r) -> p e r", e=E),
                                wexp[:, t, :, :].to_broadcast([P, E, R]), ALU.mult).then_inc(s_hw, 1)
            for t in range(B):
                dve.wait_ge(s_l_proj, t + 1)
                v.scalar_tensor_tensor(out=xr[:, t, :], in0=(pD, pZ)[t % 2][:], scalar=8.0 / R,
                                       in1=xr[:, t, :], op0=ALU.mult, op1=ALU.add).then_inc(s_x4_done, 1)

        @block.tensor
        def _(pe):
            mm = nc.tensor.matmul

            def three(dst, left, right, start=True, stop=True, lint=False):
                (lh, ll), (rh, rl) = left, right
                mm(dst, lh, rl, start=start, stop=False, skip_group_check=lint)
                mm(dst, ll, rh, start=False, stop=False, skip_group_check=lint)
                return mm(dst, lh, rh, start=False, stop=stop, skip_group_check=lint)

            def tr(dst, src, ident):
                return mm(dst, src, ident, is_transpose=True, start=True, stop=True)

            pe.wait_ge(s_ident, 2)
            def x_transposes(half):
                for b in range(HB):
                    t = half * HB + b
                    pe.wait_ge(s_xn, t + 1)
                    bank = oacc[b]
                    for kt in range(KT):
                        last = tr(bank[:, kt * S:(kt + 1) * S], hid[:, t, kt * P:(kt + 1) * P], ident[:])
                    last.then_inc(s_x_trans, 1)

            x_transposes(0)

            def project(dst, c, src, half):
                for kt in range(KT):
                    w = tuple(w[c][:, kt * P:(kt + 1) * P] for w in (w_hi, w_lo))
                    last = three(dst, w, tuple(s[half][:, kt, :] for s in src), start=kt == 0, stop=kt == KT - 1)
                return last

            def queries(n, half):
                pe.wait_ge(s_w_lo["q"], n + 1)
                project(pX0[:], "q", (xT_hi, xT_lo), half).then_inc(s_q_proj, 1)

            def keys(n, half):
                pe.wait_ge(s_w_lo["k"], n + 1)
                project(pX1[:], "k", (cT_hi, cT_lo), half).then_inc(s_k_proj, 1)

            def values(bank, batches, half):
                for i, b in enumerate(batches):
                    for kt in range(KT):
                        c = tuple(t[half][:, kt, b * S:(b + 1) * S] for t in (cT_hi, cT_lo))
                        w = tuple(w["v"][:, kt * 2 * DH:(kt + 1) * 2 * DH] for w in (w_hi, w_lo))
                        last = three(bank[:, i * 2 * DH:(i + 1) * 2 * DH], c, w, start=kt == 0, stop=kt == KT - 1)
                last.then_inc(s_v_proj, 1)

            def outputs(n, start=False):
                pe.wait_ge(s_a_lo, n + 1)
                pe.wait_ge(s_w_lo["o"], n + 1)
                for b in range(HB):
                    cols = slice(b * S, (b + 1) * S)
                    last = three(oacc[b][:], (aT_hi[:, cols], aT_lo[:, cols]), (w_hi["o"][:], w_lo["o"][:]),
                                 start=start, stop=False, lint=True)
                last.then_inc(s_o_done, 1)

            def pair(m, half, rows=False):
                for odd in range(2):
                    n = 2 * m + odd
                    pe.wait_ge(s_q_lo, n + 1)
                    pe.wait_ge(s_k_lo, n + 1)
                    if later(n):
                        pe.wait_ge(s_p_lo, n)
                    for b in range(HB):
                        cols = slice(b * S, (b + 1) * S)
                        last = three(pS[:, cols], (q_hi[:, cols], q_lo[:, cols]), (k_hi[:, cols], k_lo[:, cols]))
                    last.then_inc(s_s_done, 1)
                    if unless_last(n + 1):
                        next_half = (n + 1) // H if isinstance(n, int) else half
                        if isinstance(n, int) and n + 1 == H:
                            pe.wait_ge(s_xT_lo, B)
                            pe.wait_ge(s_cT_lo, 2 * KT)
                        if odd:
                            pe.wait_ge(s_v_lo, n)
                        queries(n + 1, next_half)
                        if odd:
                            pe.wait_ge(s_v_lo, n + 1)
                        if rows and not (isinstance(n, int) and n == H):
                            pe.wait_ge(s_g_out, n - H)
                        keys(n + 1, next_half)
                    if not odd:
                        pe.wait_ge(s_w_lo["v"], m + 1)
                        pe.wait_ge(s_q_lo, n + 2)
                        values(pX0, (0, 1), half)
                        pe.wait_ge(s_k_lo, n + 2)
                        values(pX1, (2, 3), half)
                    last_step = isinstance(n, int) and n + 1 == STEPS
                    if last_step:
                        outputs(n - 1)
                    pe.wait_ge(s_norm_done, n + 1)
                    for b in range(HB):
                        last = tr(pS[:, b * S:(b + 1) * S], prob[:, b, :], ident[:])
                    last.then_inc(s_p_trans, 1)
                    if later(n) and not last_step:
                        if isinstance(n, int) and n == H + 1:
                            pe.wait_ge(s_x1_done, 1)
                        if isinstance(n, int) and n == 1:
                            pe.wait_ge(s_xw, B)
                        outputs(n - 1, start=isinstance(n, int) and n % H == 1)
                    if rows:
                        pe.wait_ge(s_g_diag, n - H + 1)
                        if isinstance(n, int) and n + 1 == STEPS:
                            pe.wait_ge(s_g_out, n - H)
                        elif odd:
                            pe.wait_ge(s_k_lo, n + 2)
                        else:
                            pe.wait_ge(s_v_lo, n + 2)
                        mm(pX1[:, 0:FR], ones[0:FR, :], f_diag[0:FR, 0:FR], start=True, stop=True)
                        pe.wait_ge(s_g_q, n - H + 1)
                        for kt in range(KT):
                            last = tr(g_trans_bank[:, kt * FR:(kt + 1) * FR], g_q[0:FR, kt * P:(kt + 1) * P],
                                      ident_b[0:FR, 0:FR])
                        last.then_inc(s_g_trans, 1)
                    pe.wait_ge(s_p_lo, n + 1)
                    pe.wait_ge(s_v_lo, 2 * m + 2)
                    for b in range(HB):
                        cols = slice(b * S, (b + 1) * S)
                        heads = slice(odd * DH, (odd + 1) * DH)
                        last = three(pT[:, cols], (v_hi[:, b, heads], v_lo[:, b, heads]),
                                     (pT_hi[:, cols], pT_lo[:, cols]))
                    last.then_inc(s_a_done, 1)

            pe.wait_ge(s_xT_lo, HB)
            queries(0, 0)
            pe.wait_ge(s_cT_lo, KT)
            keys(0, 0)
            x_transposes(1)
            pair(0, 0)
            with pe.Fori(1, H // 2 - 1) as m:
                pair(m, 0)
            pair(H // 2 - 1, 0)
            pair(H // 2, 1, rows=True)
            with pe.Fori(H // 2 + 1, PAIRS - 1) as m:
                pair(m, 1, rows=True)
            pair(PAIRS - 1, 1, rows=True)
            def down_tile(t):
                pe.wait_ge(s_f_q, t + 1)
                for bank, blocks in enumerate(wd_blocks):
                    if later(t):
                        pe.wait_ge(s_f_out, 2 * t - 1 + bank)
                    for k in blocks:
                        cols = min(P, INTER - k * P)
                        last = tr(wd_banks[bank][0:cols, (k - blocks[0]) * P:(k - blocks[0] + 1) * P],
                                  f_q[:, t, k * P:k * P + cols], ident_b[:])
                    last.then_inc(s_f_trans, 1)

            pe.wait_ge(s_g_out, H)
            down_tile(0)
            outputs(STEPS - 1)
            down_tile(1)

            def token_transposes(t):
                pe.wait_ge(s_y_q, t + 1)
                if later(t):
                    pe.wait_ge(s_y_qT, t)
                for kt in range(KT):
                    last = tr(pYb[:, kt * S:(kt + 1) * S], y_q[:, kt * P:(kt + 1) * P], ident_b[:])
                last.then_inc(s_y_trans, 1)

            def down_steps():
                pe.wait_ge(s_f_out, 2 * KT)
                pe.wait_ge(s_f_diag, KT)
                for t in range(KT):
                    last = mm(pD[:, t * P:(t + 1) * P], ones[:], f_diags[:, t, :], start=True, stop=True)
                last.then_inc(s_f_step, 1)
                pe.wait_ge(s_f_row, 1)

            def ffn_step(t):
                if live(t + 1):
                    if later(t + 1):
                        token_transposes(t + 1)
                    pe.wait_ge(s_y_qT, t + 2)
                    for j in range(CHUNKS):
                        if later(t + 1):
                            pe.wait_ge(s_up_copy, CHUNKS * t + j + 1)
                        inner(j, 0).then_inc(s_g_proj, 1)
                    if isinstance(t, int) and t == -1:
                        down_tile(3)
                if live(t + 1):
                    for j in range(CHUNKS):
                        pe.wait_ge(s_gate, CHUNKS * (t + 1) + j + 1)
                        inner(j, INTER).then_inc(s_u_proj, 1)
                if live(t):
                    pe.wait_ge(s_h_q, t + 1)
                    if later(t):
                        pe.wait_ge(s_h_qT, t)
                    for k in range(IT):
                        cols = min(P, INTER - k * P)
                        last = tr(pTb[0:cols, k * S:(k + 1) * S], h_q[:, k * P:k * P + cols], ident_b[:])
                    last.then_inc(s_h_trans, 1)
                if live(t - 1):
                    pe.wait_ge(s_z_t, t)
                    if later(t - 1):
                        pe.wait_ge(s_zT, t - 1)
                    for kt in range(KT):
                        last = tr(pZ[:, kt * S:(kt + 1) * S], z_t[:, kt * P:(kt + 1) * P], ident[:])
                    last.then_inc(s_z_trans, 1)
                if isinstance(t, int) and t == 0:
                    down_steps()
                if live(t):
                    pe.wait_ge(s_h_qT, t + 1)
                    if later(t):
                        pe.wait_ge(s_d_used, t)
                    for k in range(IT):
                        rows = min(P, INTER - k * P)
                        last = mm(pD[:], h_qT[0:rows, k * S:(k + 1) * S], wdT[0:rows, k, :],
                                  start=k == 0, stop=k == IT - 1)
                    last.then_inc(s_d_proj, 1)

            def inner(j, start):
                c0, c1 = chunks[j]
                for kt in range(KT):
                    last = mm(pA[:, c0:c1], y_qT[:, kt * S:(kt + 1) * S], wguT[:, kt, start + c0:start + c1],
                              start=kt == 0, stop=kt == KT - 1)
                return last

            token_transposes(0)
            down_tile(2)
            pe.wait_ge(s_x1_done, 2)
            ffn_step(-1)

            for t in range(2):
                ffn_step(t)
            with pe.Fori(2, B - 2) as t:
                ffn_step(t)
            for t in range(B - 2, B + 2):
                ffn_step(t)

            width = 2 * B
            pe.wait_ge(s_diag, 2)
            pe.wait_ge(s_tapped, TAPS)
            order = sorted(range(TAPS), key=lambda j: abs(j - TAPS // 2))
            for j in order:
                last = mm(pA[:, 0:KT * width], diag[:, j + P:j + 2 * P], tapped[:, j],
                          start=j == order[0], stop=j == order[-1], skip_group_check=True)
                if j < TAPS // 2:
                    last = mm(pA[:, width:KT * width], diag[:, j + 2 * P:j + 3 * P], tapped[:, j, 0:KT - 1],
                              start=False, stop=j == order[-1], skip_group_check=True)
                if j > TAPS // 2:
                    last = mm(pA[:, 0:(KT - 1) * width], diag[:, j:j + P], tapped[:, j, 1:KT],
                              start=False, stop=j == order[-1], skip_group_check=True)
            last.then_inc(s_conv, 1)
            for i in range(2):
                pe.wait_ge(s_csum, i + 1)
                mm(pA[:, 512 * (i + 1):512 * (i + 1) + 2], ones[:], csum[:], start=True, stop=True)\
                    .then_inc(s_ctotal, 1)

            def coef_transposes(p):
                for i in range(2):
                    if p == 0:
                        pe.wait_ge(s_coef_first, i + 1)
                    else:
                        pe.wait_ge(s_coef, 2 * p + i - 1)
                    if later(p):
                        pe.wait_ge(s_c_used, 2 * p + i - 1)
                    for kt in range(KT):
                        last = tr(c_bank[i][:, kt * P:(kt + 1) * P], coef[:, 2 * p + i, kt, :], ident[:])
                    last.then_inc(s_c_trans, 1)

            def route_pair(p, more=True):
                if more:
                    coef_transposes(p + 1)
                for i in range(2):
                    pe.wait_ge(s_f, 2 * p + i + 1)
                    if later(p):
                        pe.wait_ge(s_fT, 2 * p + i - 1)
                    for kt in range(KT):
                        last = tr(f_bank[:, i * 512 + kt * S:i * 512 + (kt + 1) * S],
                                  f[:, i, kt * P:(kt + 1) * P], ident[:])
                    last.then_inc(s_f_t, 1)
                for i in range(2):
                    pe.wait_ge(s_fT, 2 * p + i + 1)
                    if later(p):
                        pe.wait_ge(s_rh, 2 * p + i - 1)
                    for kt in range(KT):
                        last = mm(pA[:, i * 512:i * 512 + E + ER], fT[:, i, kt * S:(kt + 1) * S], ra[:, kt, :],
                                  start=kt == 0, stop=kt == KT - 1)
                    last.then_inc(s_r_proj, 1)

            pe.wait_ge(s_const_in, 16 * 6)
            coef_transposes(0)
            for p in range(B // 2):
                route_pair(p, more=p + 1 < B // 2)

            def hidden_transpose(t):
                pe.wait_ge(s_hw, t + 1)
                if t >= 2:
                    pe.wait_ge(s_hwT, t - 1)
                tr(pA[:, (t % 2) * 512:(t % 2) * 512 + S], hw[:, t, :, :], ident[:]).then_inc(s_hw_t, 1)

            pe.wait_ge(s_rh, B)
            hidden_transpose(0)
            for t in range(B):
                if t + 1 < B:
                    hidden_transpose(t + 1)
                pe.wait_ge(s_hwT, t + 1)
                if t >= 2:
                    pe.wait_ge(s_x4_done, t - 1)
                mm((pD, pZ)[t % 2][:], hwT[:, t % 2, :], lb[:], start=True, stop=True).then_inc(s_l_proj, 1)


def kernel(**inputs):
    import concourse.bacc as bacc
    from concourse.bass_utils import run_bass_kernel_spmd

    def host(name):
        return np.asarray(inputs[name])

    def tile_rows(w):
        return w.T.reshape(KT, P, -1).transpose(1, 0, 2)

    def per_head(w):
        return w.reshape(H, DH, KT, P).transpose(0, 3, 2, 1).reshape(H, P, KT * DH)

    def rows(v):
        return np.broadcast_to(v.reshape(1, -1), (P, v.size))

    arrays = {
        "x": host("x"),
        "cT": host("ctx_4096").reshape(B * S, D).T.reshape(KT, P, B * S),
        "mask": host("mask_BxSxS2_bk0").transpose(1, 0, 2),
        "bias": host("L0_xattn_position_bias"),
        "ln_w": host("L0_xattn_ln_weight").reshape(KT, P).T,
        "wq": per_head(host("L0_xattn_w_q")),
        "wk": per_head(host("L0_xattn_w_k")),
        "wv": per_head(host("L0_xattn_w_v")).reshape(H // 2, 2, P, KT, DH).transpose(0, 2, 3, 1, 4)
        .reshape(H // 2, P, KT * 2 * DH),
        "wo": host("L0_xattn_w_out").reshape(D, H, DH).transpose(1, 2, 0),
        "w_gate": host("L0_ffn_w_gate").reshape(H // 2, FR, D),
        "w_up": host("L0_ffn_w_up").reshape(H // 2, FR, D),
        "w_down": host("L0_ffn_w_down"),
        "conv_w": rows(host("L1_xattn_conv_w")),
        "gamma": rows(host("L1_xattn_bn_gamma")),
        "beta": rows(host("L1_xattn_bn_beta")),
        "router_w": tile_rows(host("L1_ffn_router_w")),
        "router_b": rows(host("L1_ffn_router_b")),
        "lora_a": tile_rows(host("L1_ffn_A").reshape(ER, D)),
        "lora_b": host("L1_ffn_Bm").transpose(0, 2, 1).reshape(ER, D),
    }
    arrays = {f"in_{name}": np.ascontiguousarray(a) for name, a in arrays.items()}
    nc = bacc.Bacc("TRN2", target_bir_lowering=False, num_devices=1)
    args = [nc.dram_tensor(name, a.shape, mybir.dt.from_np(a.dtype), kind="ExternalInput").ap()
            for name, a in arrays.items()]
    out = nc.dram_tensor("out", (B, S, D), F32, kind="ExternalOutput").ap()
    layers_kernel(nc, *args, out)
    result = run_bass_kernel_spmd(nc, [arrays], core_ids=[0])
    return result.results[0]["out"]
```
